# Optimizing a Trainium2 kernel written in Bass

```python
import numpy as np
import jax
import jax.numpy as jnp

def _softmax(x, axis=-1):
    return jax.nn.softmax(x, axis=axis)

def _gelu(x):
    return jax.nn.gelu(x, approximate=True)

def _silu(x):
    return jax.nn.silu(x)

def _sigmoid(x):
    return jax.nn.sigmoid(x)

def _layernorm(x, axis=-1, eps=1e-05):
    m = jnp.mean(x, axis=axis, keepdims=True)
    v = jnp.var(x, axis=axis, keepdims=True)
    return (x - m) / jnp.sqrt(v + eps)

def _scatter_add(tgt, idx, src, axis=0):
    return tgt.at[idx].add(src)

def _segment_sum(src, seg, n):
    return jax.ops.segment_sum(src, seg, n)
kernel_name = 'mk_adaln_d2_jaxref_r8_8c9f8e'

def setup_inputs(seed: int=0):
    np.random.seed(seed)
    _w = jnp.asarray

    def _L0_attn_setup():
        import jax, jax.numpy as jnp
        import numpy as np
        N_EMBD = 128
        N_HEAD = 16
        HEAD_DIM = N_EMBD // N_HEAD
        LATENT_DIM = N_EMBD // 2
        B, T = (4, 256)
        key = jax.random.key(seed)
        ks = jax.random.split(key, 5)

        def init(k, fan_in, fan_out):
            bound = 1.0 / np.sqrt(fan_in)
            return jax.random.uniform(k, (fan_in, fan_out), jnp.float32, -bound, bound)
        return {'x': jax.random.normal(ks[0], (B, T, N_EMBD), jnp.float32), 'Wc_down': init(ks[1], N_EMBD, LATENT_DIM), 'Wq_up': init(ks[2], LATENT_DIM, N_EMBD), 'Wkv_up': init(ks[3], LATENT_DIM, 2 * HEAD_DIM), 'Wc_proj': init(ks[4], N_EMBD, N_EMBD)}
    _L0_attn_in = _L0_attn_setup()

    def _L0_ffn_setup():
        import jax, jax.numpy as jnp
        import numpy as np
        from math import ceil
        CAPACITY_FACTOR = 2.0
        MIN_CAPACITY = 4
        key = jax.random.key(seed)
        ks = jax.random.split(key, 4)
        B, S, D, Di, E = (4, 256, 128, 512, 8)
        x = jax.random.normal(ks[0], (B, S, D), dtype=jnp.float32)
        Wr = jax.random.normal(ks[1], (D, E), dtype=jnp.float32) * D ** (-0.5)
        W1 = jax.random.normal(ks[2], (E, D, Di), dtype=jnp.float32) * D ** (-0.5)
        b1 = jnp.zeros((E, Di), dtype=jnp.float32)
        W2 = jax.random.normal(ks[3], (E, Di, D), dtype=jnp.float32) * Di ** (-0.5)
        b2 = jnp.zeros((E, D), dtype=jnp.float32)
        return {'x': x, 'Wr': Wr, 'W1': W1, 'b1': b1, 'W2': W2, 'b2': b2}
    _L0_ffn_in = _L0_ffn_setup()
    _L0_c = _w((lambda *s: np.random.randn(*s).astype(np.float32) * 0.05)(8, 128))
    _L0_wmod = _w((lambda *s: np.random.randn(*s).astype(np.float32) * 0.05)(128, 6 * 128) * 128 ** (-0.5))

    def _L1_attn_setup():
        import jax, jax.numpy as jnp
        import numpy as np
        NUM_HEADS = 16
        D_MODEL = 128
        HEAD_DIM = D_MODEL // NUM_HEADS
        WINDOW = 64
        SCALE = 8.0 / HEAD_DIM
        LN_EPS = 1e-05

        def _layernorm(t, gamma, beta):
            mu = jnp.mean(t, axis=-1, keepdims=True)
            var = jnp.var(t, axis=-1, keepdims=True)
            return (t - mu) * jax.lax.rsqrt(var + LN_EPS) * gamma + beta
        key = jax.random.key(seed)
        ks = jax.random.split(key, 4)
        x = jax.random.normal(ks[0], (4, 1024, D_MODEL), dtype=jnp.float32)
        W_qkv = jax.random.normal(ks[1], (D_MODEL, 3 * D_MODEL), dtype=jnp.float32) * D_MODEL ** (-0.5)
        ln_gamma = jnp.ones((HEAD_DIM,), dtype=jnp.float32)
        ln_beta = jnp.zeros((HEAD_DIM,), dtype=jnp.float32)
        W_proj = jax.random.normal(ks[2], (D_MODEL, D_MODEL), dtype=jnp.float32) * D_MODEL ** (-0.5)
        b_proj = jax.random.normal(ks[3], (D_MODEL,), dtype=jnp.float32) * 0.02
        return {'x': x, 'W_qkv': W_qkv, 'ln_gamma': ln_gamma, 'ln_beta': ln_beta, 'W_proj': W_proj, 'b_proj': b_proj}
    _L1_attn_in = _L1_attn_setup()

    def _L1_ffn_setup():
        import jax, jax.numpy as jnp
        import numpy as np
        DIM = 128

        def _reference_tuple_inner(x, W_r, W_k, W_v, mu_r, mu_k):
            B, T, C = x.shape
            x_prev = jnp.concatenate([jnp.zeros((B, 1, C), x.dtype), x[:, :-1, :]], axis=1)
            xr = mu_r * x + (1.0 - mu_r) * x_prev
            xk = mu_k * x + (1.0 - mu_k) * x_prev
            r = jax.nn.sigmoid(jnp.einsum('btc,dc->btd', xr, W_r))
            k = jnp.einsum('btc,dc->btd', xk, W_k)
            k_act = jnp.square(jax.nn.relu(k))
            out = r * jnp.einsum('btc,dc->btd', k_act, W_v)
            new_state = x[:, -1, :]
            return (out, new_state)
        key = jax.random.key(seed)
        ks = jax.random.split(key, 6)
        B, T, C = (8, 256, DIM)
        x = jax.random.normal(ks[0], (B, T, C), dtype=jnp.float32)
        s = 1.0 / np.sqrt(C)
        W_r = jax.random.uniform(ks[1], (C, C), jnp.float32, -s, s)
        W_k = jax.random.uniform(ks[2], (C, C), jnp.float32, -s, s)
        W_v = jax.random.uniform(ks[3], (C, C), jnp.float32, -s, s)
        mu_r = jax.random.uniform(ks[4], (C,), jnp.float32)
        mu_k = jax.random.uniform(ks[5], (C,), jnp.float32)
        return {'x': x, 'W_r': W_r, 'W_k': W_k, 'W_v': W_v, 'mu_r': mu_r, 'mu_k': mu_k}
    _L1_ffn_in = _L1_ffn_setup()
    _L1_c = _w((lambda *s: np.random.randn(*s).astype(np.float32) * 0.05)(8, 128))
    _L1_wmod = _w((lambda *s: np.random.randn(*s).astype(np.float32) * 0.05)(128, 6 * 128) * 128 ** (-0.5))
    _d = {'L0_attn_x': _L0_attn_in['x'], 'L0_attn_Wc_down': _L0_attn_in['Wc_down'], 'L0_attn_Wq_up': _L0_attn_in['Wq_up'], 'L0_attn_Wkv_up': _L0_attn_in['Wkv_up'], 'L0_attn_Wc_proj': _L0_attn_in['Wc_proj'], 'L0_ffn_Wr': _L0_ffn_in['Wr'], 'L0_ffn_W1': _L0_ffn_in['W1'], 'L0_ffn_b1': _L0_ffn_in['b1'], 'L0_ffn_W2': _L0_ffn_in['W2'], 'L0_ffn_b2': _L0_ffn_in['b2'], 'L0_c': _L0_c, 'L0_wmod': _L0_wmod, 'L1_attn_W_qkv': _L1_attn_in['W_qkv'], 'L1_attn_ln_gamma': _L1_attn_in['ln_gamma'], 'L1_attn_ln_beta': _L1_attn_in['ln_beta'], 'L1_attn_W_proj': _L1_attn_in['W_proj'], 'L1_attn_b_proj': _L1_attn_in['b_proj'], 'L1_ffn_W_r': _L1_ffn_in['W_r'], 'L1_ffn_W_k': _L1_ffn_in['W_k'], 'L1_ffn_W_v': _L1_ffn_in['W_v'], 'L1_ffn_mu_r': _L1_ffn_in['mu_r'], 'L1_ffn_mu_k': _L1_ffn_in['mu_k'], 'L1_c': _L1_c, 'L1_wmod': _L1_wmod}
    _x0 = _d['L0_attn_x']
    _d['L0_attn_x'] = jax.random.normal(jax.random.fold_in(jax.random.key(seed), 1), (8, 512, 128), dtype=_x0.dtype)
    del _x0
    return _d

def reference(L0_attn_x, L0_attn_Wc_down, L0_attn_Wq_up, L0_attn_Wkv_up, L0_attn_Wc_proj, L0_ffn_Wr, L0_ffn_W1, L0_ffn_b1, L0_ffn_W2, L0_ffn_b2, L0_c, L0_wmod, L1_attn_W_qkv, L1_attn_ln_gamma, L1_attn_ln_beta, L1_attn_W_proj, L1_attn_b_proj, L1_ffn_W_r, L1_ffn_W_k, L1_ffn_W_v, L1_ffn_mu_r, L1_ffn_mu_k, L1_c, L1_wmod):

    def _L0_attn_ref(x, Wc_down, Wq_up, Wkv_up, Wc_proj):
        import jax, jax.numpy as jnp
        import numpy as np
        N_EMBD = 128
        N_HEAD = 16
        HEAD_DIM = N_EMBD // N_HEAD
        LATENT_DIM = N_EMBD // 2
        B, T = (4, 256)
        Bsz, Tlen, C = x.shape
        latent = x @ Wc_down
        q = (latent @ Wq_up).reshape(Bsz, Tlen, N_HEAD, HEAD_DIM)
        kv = latent @ Wkv_up
        k, v = (kv[..., :HEAD_DIM], kv[..., HEAD_DIM:])
        scale = 1.0 / np.sqrt(HEAD_DIM)
        att = jnp.einsum('bthd,bsd->bhts', q, k) * scale
        causal = jnp.tril(jnp.ones((Tlen, Tlen), dtype=bool))
        att = jnp.where(causal[None, None], att, -jnp.inf)
        att = jax.nn.softmax(att, axis=-1)
        y = jnp.einsum('bhts,bsd->bthd', att, v).reshape(Bsz, Tlen, C)
        return y @ Wc_proj

    def _L0_ffn_ref(x, Wr, W1, b1, W2, b2):
        import jax, jax.numpy as jnp
        import numpy as np
        from math import ceil
        CAPACITY_FACTOR = 2.0
        MIN_CAPACITY = 4
        B, S, D = x.shape
        E = Wr.shape[1]
        N = B * S
        k = max(MIN_CAPACITY, ceil(N * CAPACITY_FACTOR / E))
        xt = x.reshape(N, D)
        scores = jax.nn.softmax(xt @ Wr, axis=-1)
        G, idx = jax.lax.top_k(scores.T, k)
        X_in = xt[idx]
        h = jax.nn.gelu(jnp.einsum('ekd,edh->ekh', X_in, W1) + b1[:, None, :], approximate=False)
        X_e = jnp.einsum('ekh,ehd->ekd', h, W2) + b2[:, None, :]
        contrib = (G[..., None] * X_e).reshape(E * k, D)
        out = jnp.zeros((N, D), dtype=x.dtype).at[idx.reshape(-1)].add(contrib)
        return out.reshape(B, S, D)

    def _L1_attn_ref(x, W_qkv, ln_gamma, ln_beta, W_proj, b_proj):
        import jax, jax.numpy as jnp
        import numpy as np
        NUM_HEADS = 16
        D_MODEL = 128
        HEAD_DIM = D_MODEL // NUM_HEADS
        WINDOW = 64
        SCALE = 8.0 / HEAD_DIM
        LN_EPS = 1e-05

        def _layernorm(t, gamma, beta):
            mu = jnp.mean(t, axis=-1, keepdims=True)
            var = jnp.var(t, axis=-1, keepdims=True)
            return (t - mu) * jax.lax.rsqrt(var + LN_EPS) * gamma + beta
        B, N, C = x.shape
        nw = N // WINDOW
        xw = x.reshape(B * nw, WINDOW, C)
        qkv = (xw @ W_qkv).reshape(B * nw, WINDOW, 3, NUM_HEADS, HEAD_DIM)
        q, k, v = (qkv[:, :, 0], qkv[:, :, 1], qkv[:, :, 2])
        q = _layernorm(q, ln_gamma, ln_beta)
        k = _layernorm(k, ln_gamma, ln_beta)
        attn = jnp.einsum('bqhd,bkhd->bhqk', q * SCALE, k)
        attn = jax.nn.softmax(attn, axis=-1)
        out = jnp.einsum('bhqk,bkhd->bqhd', attn, v).reshape(B * nw, WINDOW, C)
        out = out @ W_proj + b_proj
        return out.reshape(B, N, C)

    def _L1_ffn_ref(x, W_r, W_k, W_v, mu_r, mu_k):
        import jax, jax.numpy as jnp
        import numpy as np
        DIM = 128

        def _reference_tuple_inner(x, W_r, W_k, W_v, mu_r, mu_k):
            B, T, C = x.shape
            x_prev = jnp.concatenate([jnp.zeros((B, 1, C), x.dtype), x[:, :-1, :]], axis=1)
            xr = mu_r * x + (1.0 - mu_r) * x_prev
            xk = mu_k * x + (1.0 - mu_k) * x_prev
            r = jax.nn.sigmoid(jnp.einsum('btc,dc->btd', xr, W_r))
            k = jnp.einsum('btc,dc->btd', xk, W_k)
            k_act = jnp.square(jax.nn.relu(k))
            out = r * jnp.einsum('btc,dc->btd', k_act, W_v)
            new_state = x[:, -1, :]
            return (out, new_state)
        return _reference_tuple_inner(x, W_r, W_k, W_v, mu_r, mu_k)[0]
    x = L0_attn_x
    mod = (_silu(L0_c) @ L0_wmod).reshape(L0_c.shape[0], 6, 1, -1)
    sa, ca, ga, sb, cb, gb = (mod[:, 0], mod[:, 1], mod[:, 2], mod[:, 3], mod[:, 4], mod[:, 5])
    ga = (2 * (ga >= 0) - 1) * jnp.maximum(jnp.abs(ga), 0.25)
    gb = (2 * (gb >= 0) - 1) * jnp.maximum(jnp.abs(gb), 0.25)
    h = _layernorm(x, axis=-1) * (1 + ca) + sa
    x = x + ga * _L0_attn_ref(h, L0_attn_Wc_down, L0_attn_Wq_up, L0_attn_Wkv_up, L0_attn_Wc_proj)
    h = _layernorm(x, axis=-1) * (1 + cb) + sb
    x = x + gb * _L0_ffn_ref(h, L0_ffn_Wr, L0_ffn_W1, L0_ffn_b1, L0_ffn_W2, L0_ffn_b2)
    mod = (_silu(L1_c) @ L1_wmod).reshape(L1_c.shape[0], 6, 1, -1)
    sa, ca, ga, sb, cb, gb = (mod[:, 0], mod[:, 1], mod[:, 2], mod[:, 3], mod[:, 4], mod[:, 5])
    ga = (2 * (ga >= 0) - 1) * jnp.maximum(jnp.abs(ga), 0.25)
    gb = (2 * (gb >= 0) - 1) * jnp.maximum(jnp.abs(gb), 0.25)
    h = _layernorm(x, axis=-1) * (1 + ca) + sa
    x = x + ga * _L1_attn_ref(h, L1_attn_W_qkv, L1_attn_ln_gamma, L1_attn_ln_beta, L1_attn_W_proj, L1_attn_b_proj)
    h = _layernorm(x, axis=-1) * (1 + cb) + sb
    x = x + gb * _L1_ffn_ref(h, L1_ffn_W_r, L1_ffn_W_k, L1_ffn_W_v, L1_ffn_mu_r, L1_ffn_mu_k)
    return x

_drawn_inputs = setup_inputs


def setup_inputs(seed=0):
    import zlib

    import numpy as np

    out = dict(_drawn_inputs(seed))
    spreads = {'L0_ffn_b1': (0.0, 2.0),
     'L0_ffn_b2': (0.0, 2.0),
     'L1_attn_ln_gamma': (1.0, 0.6),
     'L1_attn_ln_beta': (0.0, 2.0)}
    factors = {'L0_attn_Wc_down': 8.0,
     'L0_attn_Wq_up': 8.0,
     'L0_attn_Wkv_up': 8.0,
     'L0_attn_Wc_proj': 8.0,
     'L1_attn_b_proj': 200.0,
     'L1_ffn_W_r': 8.0,
     'L1_ffn_W_k': 2.997,
     'L1_ffn_W_v': 2.763,
     'L1_ffn_mu_r': 8.0,
     'L1_ffn_mu_k': 4.669,
     'L0_ffn_Wr': 8.0,
     'L0_ffn_W1': 8.0,
     'L0_ffn_W2': 8.0,
     'L1_attn_W_qkv': 8.0,
     'L1_attn_W_proj': 8.0}
    for name, (base, spread) in spreads.items():
        noise = np.random.default_rng([zlib.crc32(name.encode()), seed]).standard_normal(out[name].shape)
        drawn = base * np.exp(spread * noise) if base else spread * noise
        out[name] = jnp.asarray(drawn.astype(out[name].dtype))
    for name, factor in factors.items():
        out[name] = (out[name] * factor).astype(out[name].dtype)
    return out
```

```python
from contextlib import ExitStack

import concourse.bass as bass
from concourse import mybir

F32 = mybir.dt.float32
BF16 = mybir.dt.bfloat16
I32 = mybir.dt.int32
ALU = mybir.AluOpType
ACT = mybir.ActivationFunctionType
AX_X = mybir.AxisListType.X

P = 128
NB, T, D = 8, 512, 128
NT = T // P
NTILE = NB * NT
NH, DH = 16, 8
LAT = 64
NE, DI = 8, 512
CAP = 1024
NC_DI = DI // P
NS = CAP // P
ROW = D + NE
EPS = 1e-5
BIG = 1.0e30
PARTS = 3
NPR = PARTS * PARTS * DH
KR = 96
KM = KR + PARTS
QB = 3
NSTEP = 10
STEPS = [(g, i) for g in range(NT) for i in range(g + 1)]
W1WIN = 64
BITS = 30
NCH = 6


def max_groups():
    out = []
    for g in range(NT):
        per = 512 // (P * (g + 1))
        out += [(g, list(range(h, h + per))) for h in range(0, NH, per)]
    return out


GROUPS = max_groups()
NGRP = len(GROUPS)
MAX_STEPS = 8
SLOTS = 4


def spread_groups():
    cost = [P * (g + 1) * len(hs) + 150 for g, hs in GROUPS]
    out = {(s, x): [] for s in range(NSTEP) for x in range(SLOTS)}
    acc = 0
    for k, c in enumerate(cost):
        x = min(int(acc / sum(cost) * MAX_STEPS * SLOTS), MAX_STEPS * SLOTS - 1)
        out[divmod(x, SLOTS)].append(k)
        acc += c
    return out


PLACES = spread_groups()
CHUNKS = [[k for x in range(SLOTS) for k in PLACES[s, x]] for s in range(NSTEP)]


class Shared:
    pass


class Misc:

    def __init__(self, order, banks):
        self.banks = banks
        self.index = {u: k for k, u in enumerate(order)}

    def __contains__(self, u):
        return u in self.index

    def bank(self, u):
        return self.index[u] % self.banks

    def full(self, u):
        return self.index[u] // self.banks + 1


MISC0 = {1: [("bc", -1)], 2: [("hT", 2)], 3: [("lat", 2)], 4: [("q", 2)], 5: [("k", 2), ("h2", -2)],
         6: [("v", 2), ("lg", -2)], 7: [("pj", -1)], 8: [("m", 1)]}
LEAD, TAIL = 2, 2


def misc_order(sched):
    return [(kind, n + o) for n in range(-LEAD, NB + TAIL) for s in range(NSTEP)
            for kind, o in sched.get(s, []) if 0 <= n + o < NB]


def build(nc, ins, out):
    ctx = ExitStack()
    with ctx:
        program(nc, ctx, ins, out)


def program(nc, ctx, ins, out, stop_after=None):
    def sb(name, shape, dt=F32):
        return ctx.enter_context(nc.sbuf_tensor(name, shape, dt))

    def sem(name):
        return ctx.enter_context(nc.semaphore(name))

    mid = ExitStack()
    a0 = ExitStack()

    def sbm(name, shape, dt=F32):
        return mid.enter_context(nc.sbuf_tensor(name, shape, dt))

    def sb0(name, shape, dt=F32):
        return a0.enter_context(nc.sbuf_tensor(name, shape, dt))

    def dram(name, shape, dt):
        return nc.dram_tensor(name, shape, dt, kind="Internal").ap()

    d_q = [dram(f"d_q{i}", [PARTS, DH, NH, T], BF16) for i in range(2)]
    d_k = [dram(f"d_k{i}", [PARTS, DH, T], BF16) for i in range(2)]
    d_m = [dram(f"d_m{i}", [PARTS, 64, P], BF16) for i in range(2)]
    d_y = [dram(f"d_y{i}", [4, DH + 1, 4, T], F32) for i in range(2)]
    d_r = [dram(f"d_r{i}", [NH, T], F32) for i in range(2)]
    d_tab = dram("d_tab", [NB * T, ROW], F32)

    d_acc = dram("d_acc", [NB * T, D], F32)

    bank = [a0.enter_context(nc.psum_tensor(f"bank{i}", [P, 512], F32)) for i in range(4)]
    ps_s = [a0.enter_context(nc.psum_tensor(f"ps_s{i}", [P, 1024], F32)) for i in range(2)]
    ps_mx, ps_y, ps_misc = bank[0:2], bank[2], bank[3]

    X = sb("X", [P, NTILE, D])
    ident = sb("ident", [P, P])
    identb = sb("identb", [P, P], BF16)
    maskT = sb("maskT", [P, P], BF16)
    neghalf = sb("neghalf", [P, NT])
    onehot = sb("onehot", [NB, NB, P])
    modT = sb("modT", [P, 2, NCH, NB])
    modR = sb("modR", [NB, 2, NCH * D])
    w_qkv = sb("w_qkv", [P, 3 * D])
    w_proj = sb("w_proj", [P, D])
    b_proj = sb("b_proj", [P, D])
    w_cm = sb("w_cm", [P, 3, D])
    mu = sb("mu", [P, 2])
    gamma = sb("gamma", [P, 1])
    beta = sb("beta", [P, 1])
    SC = sbm("SC", [P, NE, NTILE])
    w1 = sbm("w1", [P, NE, DI])
    w2 = sbm("w2", [P, NE, NC_DI, D])
    b1T = sbm("b1T", [P, NE, NC_DI])
    b2r = sbm("b2r", [1, NE, D])
    zrow = sbm("zrow", [P, D])
    cT = sb0("cT", [P, 2, NB])
    sT_e = sb0("sT_e", [P, 2, NB])
    siluT = sb0("siluT", [P, 2, NB])
    wmod = sb0("wmod", [P, 2, NCH * D])
    gtmp = sb0("gtmp", [NB, 2, 2, D])
    w_down = sb0("w_down", [P, LAT])
    w_q = sb0("w_q", [LAT, D])
    w_kv = sb0("w_kv", [LAT, 2 * DH])
    w_cp = sb0("w_cp", [P, D])
    w_r = sb0("w_r", [P, NE])
    Q = [sb0(f"Q{i}", [P, NH, T], BF16) for i in range(QB)]
    K = [sb0(f"K{i}", [P, T], BF16) for i in range(QB)]
    VE = [sb0(f"VE{i}", [P, NT, 32]) for i in range(QB)]
    PR = [sb0(f"PR{i}", [P, 4, 512]) for i in range(2)]
    MX = [sb0(f"MX{i}", [P, 64]) for i in range(2)]

    stat = sb0("stat", [P, NT, 6])
    mv = [sb0(f"mv{i}", [P, NT, 2]) for i in range(2)]
    ve = sb0("ve", [P, NT])
    rs = [sb0(f"rs{i}", [P, NT]) for i in range(2)]
    xn = sb0("xn", [P, NT, D])
    hT = sb0("hT", [P, T])
    latT = sb0("latT", [LAT, T])
    qs = sb0("qs", [P, PARTS, T], BF16)
    qr = sb0("qr", [P, T])
    ks = sb0("ks", [DH, PARTS, T], BF16)
    kr = sb0("kr", [DH, T])
    ms = sb0("ms", [64, PARTS, P], BF16)
    mr = sb0("mr", [64, P])
    ysb = [sb0(f"ysb{i}", [P, 512]) for i in range(2)]
    yt = sb0("yt", [P, T])
    lc = sb0("lc", [P, NH * T // P])
    rc = sb0("rc", [P, NH * T // P])
    rl = sb0("rl", [P, T])
    yn = sb0("yn", [P, T])
    wg = sb0("wg", [P, D])
    cbsb = [sb0(f"cbsb{i}", [P, 2, D]) for i in range(2)]
    stat2 = sb0("stat2", [P, NT, 6])
    mv2 = sb0("mv2", [P, NT, 2])
    ve2 = sb0("ve2", [P, NT])
    rs2 = sb0("rs2", [P, NT])
    xn2 = sb0("xn2", [P, NT, D])
    tab = sb0("tab", [P, NT, ROW])
    h2T = sb0("h2T", [P, T])
    lgm = sb0("lgm", [P, NT])
    lge = sb0("lge", [P, NT, NE])
    lgx = sb0("lgx", [P, NT, NE])
    lgs = sb0("lgs", [P, NT])
    lgr = sb0("lgr", [P, NT])

    s_x = [sem(f"x_loaded{b}") for b in range(NB)]
    s_w = sem("weights_loaded")
    s_lw = sem("late_weights_loaded")
    s_phase = sem("phase_done")
    s_cst, s_cst2 = sem("consts_cleared"), sem("consts_ready")
    s_mod_e, s_silu, s_modps, s_modT = sem("mod_exp"), sem("silu_ready"), sem("mod_ps_full"), sem("mod_done")
    names = ["sT_full", "exp_done", "pv_done", "mx_full", "red_done", "misc_full", "misc_free",
             "mv_rdy", "rs_rdy", "xn_rdy", "q1_rdy", "q2_rdy", "q3_rdy", "k1_rdy", "k2_rdy", "k3_rdy", 
             "m_rdy", "y_ev", "rc_rdy", "yn_rdy", "cb_rdy", "mv2_rdy", "rs2_rdy", "xn2_rdy", "h2_rdy", "lgx_rdy", "tab_rdy"]
    S = {n: sem("a0_" + n) for n in names}
    dnames = ["q_st0", "q_st1", "k_st0", "k_st1", "q_in0", "q_in1", "m_st", "m_in0", "m_in1", "y_st0", "y_st1",
              "yt_in", "lc_in", "r_st", "rl_in", "tab_st"]
    DS = {n: sem("a0_" + n) for n in dnames}
    s_act, s_dve, s_pool = sem("act_chain"), sem("dve_chain"), sem("pool_chain")

    weights = [
        (cT[:, 0, :], ins["L0_c"].rearrange("b d -> d b")), (cT[:, 1, :], ins["L1_c"].rearrange("b d -> d b")),
        (wmod[:, 0, :], ins["L0_wmod"]), (wmod[:, 1, :], ins["L1_wmod"]),
        (w_down[:, :], ins["L0_attn_Wc_down"]), (w_q[:, :], ins["L0_attn_Wq_up"]), (w_kv[:, :], ins["L0_attn_Wkv_up"]),
        (w_cp[:, :], ins["L0_attn_Wc_proj"]), (w_r[:, :], ins["L0_ffn_Wr"]),
    ]
    N_W = len(weights)
    def per_head(name):
        return bass.AP(ins[name].tensor, 0, [[0, NH], [1, DH], [1, 1]])

    late_weights = [
        (w_qkv[:, :], ins["L1_attn_W_qkv"]), (w_proj[:, :], ins["L1_attn_W_proj"]),
        (b_proj[:, :], bass.AP(ins["L1_attn_b_proj"].tensor, 0, [[0, P], [1, D]])),
        (w_cm[:, 0, :], ins["L1_ffn_W_r"]), (w_cm[:, 1, :], ins["L1_ffn_W_k"]), (w_cm[:, 2, :], ins["L1_ffn_W_v"]),
        (mu[:, 0:1], ins["L1_ffn_mu_r"].rearrange("(p o) -> p o", o=1)),
        (mu[:, 1:2], ins["L1_ffn_mu_k"].rearrange("(p o) -> p o", o=1)),
        (gamma[:, :], per_head("L1_attn_ln_gamma")), (beta[:, :], per_head("L1_attn_ln_beta")),
        (w1[:, :, :], ins["L0_ffn_W1"].rearrange("e d f -> d e f")),
        (b1T[:, :, :], ins["L0_ffn_b1"].rearrange("e (c p) -> p e c", p=P)),
        (b2r[:, :, :], ins["L0_ffn_b2"].rearrange("(o e) d -> o e d", o=1)),
    ] + [(w2[:, e, :, :], ins["L0_ffn_W2"][e].rearrange("(c p) d -> p c d", p=P)) for e in range(NE)]

    block = a0.enter_context(nc.Block())
    M0 = Misc(misc_order(MISC0), 1)
    chains = {}

    def link(eng, s, ins):
        chains[id(s)] = chains.get(id(s), 0) + 1
        ins.then_inc(s, 1)
        eng.wait_ge(s, chains[id(s)])

    def barrier(eng, k):
        eng.drain().then_inc(s_phase, 1)
        eng.wait_ge(s_phase, 5 * k)

    def bc(ap, shape):
        return ap.to_broadcast(shape)

    @block.tensor
    def _(pe):
        pe.wait_ge(s_w, 16 * N_W)
        pe.wait_ge(s_silu, 1)
        for l in range(2):
            for c in range(NCH):
                last = nc.tensor.matmul(ps_misc[:, (l * NCH + c) * NB:(l * NCH + c + 1) * NB],
                                        wmod[:, l, c * D:(c + 1) * D], siluT[:, l, :], start=True, stop=True)
        last.then_inc(s_modps, 1)
        for l in range(2):
            for h in range(2):
                last = nc.tensor.matmul(ps_s[l][0:NB, h * 512:h * 512 + 384], siluT[:, l, :],
                                        wmod[:, l, h * 384:(h + 1) * 384], start=True, stop=True)
        last.then_inc(s_modps, 1)
        barrier(pe, 1)

        def acquire(u):
            if M0.index[u] >= 1:
                pe.wait_ge(S["misc_free"], M0.index[u])

        def scores_T(b, s, half):
            g, i = STEPS[s]
            if s == 0 and half == 0:
                pe.wait_ge(DS[f"m_in{b % 2}"], 48 * (b // 2 + 1))
            t2 = 2 * (NSTEP * b + s) + half
            if t2 >= 2:
                pe.wait_ge(S["exp_done"], t2 - 1)
            for hh in range(2):
                hg = 2 * half + hh
                last = nc.tensor.matmul(ps_s[half][:, 512 * hh:512 * hh + 512], K[b % QB][0:KM, P * i:P * i + P],
                                        Q[b % QB][0:KM, 4 * hg:4 * hg + 4, P * g:P * g + P],
                                        start=True, stop=(i < g))
            if i == g:
                for hh in range(2):
                    last = nc.tensor.matmul(ps_s[half][:, 512 * hh:512 * hh + 512], maskT[:, :],
                                            bc(identb[:, :].unsqueeze(1), [P, 4, P]), start=False, stop=True)
            last.then_inc(S["sT_full"], 1)

        def values(t, part):
            b, s = divmod(t, NSTEP)
            g, i = STEPS[s]
            if part == 1:
                return
            pe.wait_ge(S["exp_done"], 2 * t + 2)
            if s == 0:
                pe.wait_ge(S["misc_free"], M0.full(("v", b)))
            if i == 0 and NT * b + g >= 1:
                pe.wait_ge(S["y_ev"], NT * b + g)
            for j in range(4):
                last = nc.tensor.matmul(ps_y[32 * j:32 * j + 32, :], VE[b % QB][:, i, :], PR[t % 2][:, j, :],
                                        start=(i == 0), stop=(i == g), tile_position=(0, 32 * j))
            last.then_inc(S["pv_done"], 1)

        def maxima(b, groups):
            for k in groups:
                g, hs = GROUPS[k]
                G = NGRP * b + k
                w = P * (g + 1)
                if k == 0:
                    pe.wait_ge(DS[f"q_in{b % 2}"], 64 * (b // 2 + 1))
                if G >= 2:
                    pe.wait_ge(S["red_done"], G - 1)
                for x, h in enumerate(hs):
                    nc.tensor.matmul(ps_mx[G % 2][:, x * w:(x + 1) * w], Q[b % QB][0:KR, h, P * g:P * g + P],
                                     K[b % QB][0:KR, 0:w], start=(x == 0), stop=False, skip_group_check=True)
                diag = ps_mx[G % 2][:, 0:len(hs) * w].rearrange("p (x w) -> p x w", w=w)[:, :, w - P:w]
                nc.tensor.matmul(diag, identb[:, :], bc(maskT[:, :].unsqueeze(1), [P, len(hs), P]),
                                 start=False, stop=True, skip_group_check=True).then_inc(S["mx_full"], 1)

        def misc(kind, b):
            acquire((kind, b))
            m = ps_misc
            if kind == "hT":
                pe.wait_ge(S["xn_rdy"], b + 1)
                for i in range(NT):
                    last = nc.tensor.transpose(m[:, P * i:P * i + P], xn[:, i, :], ident[:, :])
            elif kind == "lat":
                last = nc.tensor.matmul(m[0:LAT, :], w_down[:, :], hT[:, :], start=True, stop=True)
            elif kind == "q":
                last = nc.tensor.matmul(m[:, :], w_q[:, :], latT[:, :], start=True, stop=True)
            elif kind == "k":
                last = nc.tensor.matmul(m[0:DH, :], w_kv[:, 0:DH], latT[:, :], start=True, stop=True)
            elif kind == "v":
                for i in range(NT):
                    last = nc.tensor.matmul(m[:, DH * i:DH * i + DH], latT[:, P * i:P * i + P], w_kv[:, DH:2 * DH],
                                            start=True, stop=True)
            elif kind == "m":
                pe.wait_ge(S["red_done"], NGRP * (b + 1))
                last = nc.tensor.transpose(m[0:64, 0:P], MX[b % 2][:, :], ident[:, :])
            elif kind == "bc":
                last = nc.tensor.matmul(m[:, 0:384], onehot[:, b, :], modR[:, 0, 2 * D:5 * D], start=True, stop=True)
            elif kind == "pj":
                pe.wait_ge(S["yn_rdy"], b + 1)
                for i in range(NT):
                    last = nc.tensor.matmul(m[:, P * i:P * i + P], yn[:, P * i:P * i + P], wg[:, :],
                                            start=True, stop=True)
            elif kind == "h2":
                pe.wait_ge(S["h2_rdy"], b + 1)
                for i in range(NT):
                    last = nc.tensor.transpose(m[:, P * i:P * i + P], tab[:, i, 0:D], ident[:, :])
            elif kind == "lg":
                for i in range(NT):
                    last = nc.tensor.matmul(m[:, NE * i:NE * i + NE], h2T[:, P * i:P * i + P], w_r[:, :],
                                            start=True, stop=True)
            last.then_inc(S["misc_full"], 1)

        for n in range(-LEAD, NB + TAIL):
            for s in range(NSTEP):
                t = NSTEP * n + s - 1
                for x in range(SLOTS):
                    if x < 2 and 0 <= n < NB:
                        scores_T(n, s, x)
                    if x >= 2 and 0 <= t < NSTEP * NB:
                        values(t, x - 2)
                    if 0 <= n + 1 < NB:
                        maxima(n + 1, PLACES[s, x])
                for kind, o in MISC0.get(s, []):
                    if (kind, n + o) in M0:
                        misc(kind, n + o)
        barrier(pe, 2)

    @block.scalar
    def _(act):
        act.wait_ge(s_w, 16 * N_W)
        nc.scalar.activation(sT_e[:, :, :], cT[:, :, :], ACT.Exp, scale=-1.0).then_inc(s_mod_e, 1)
        barrier(act, 1)

        def full(u):
            act.wait_ge(S["misc_full"], M0.full(u))

        def misc(kind, b):
            m = ps_misc
            if kind == "hT":
                full((kind, b))
                nc.scalar.activation(hT[:, :], m[:, :], ACT.Identity, bias=modT[:, 0, 0, b:b + 1],
                                     scale=modT[:, 0, 1, b:b + 1]).then_inc(S["misc_free"], 1)
            elif kind == "lat":
                full((kind, b))
                nc.scalar.activation(latT[:, :], m[0:LAT, :], ACT.Copy).then_inc(S["misc_free"], 1)
            elif kind == "q":
                full((kind, b))
                if b >= 1:
                    act.wait_ge(DS[f"q_st{(b - 1) % 2}"], 16 * PARTS * ((b - 1) // 2 + 1))
                nc.scalar.activation(qs[:, 0, :], m[:, :], ACT.Copy).then_inc(S["q1_rdy"], 1)
            elif kind == "k":
                full((kind, b))
                if b >= 1:
                    act.wait_ge(DS[f"k_st{(b - 1) % 2}"], 16 * ((b - 1) // 2 + 1))
                nc.scalar.activation(ks[:, 0, :], m[0:DH, :], ACT.Copy).then_inc(S["k1_rdy"], 1)
            elif kind == "bc":
                full((kind, b))
                if b >= 2:
                    act.wait_ge(S["h2_rdy"], b - 1)
                nc.scalar.activation(cbsb[b % 2][:, :, :], m[:, D:3 * D].rearrange("p (a d) -> p a d", a=2),
                                     ACT.Copy).then_inc(S["cb_rdy"], 1)
            elif kind == "h2":
                full((kind, b))
                nc.scalar.activation(h2T[:, :], m[:, :], ACT.Copy).then_inc(S["misc_free"], 1)

        def y_out(Y):
            b, g = divmod(Y, NT)
            act.wait_ge(S["pv_done"], NSTEP * b + STEPS.index((g, g)) + 1)
            if Y >= 2:
                act.wait_ge(DS[f"y_st{Y % 2}"], 64 * (Y // 2))
            nc.scalar.activation(ysb[Y % 2][:, :], ps_y[:, :], ACT.Copy).then_inc(S["y_ev"], 1)

        for n in range(-LEAD, NB + TAIL):
            for s in range(NSTEP):
                t = NSTEP * n + s
                if 0 <= n < NB:
                    for half in range(2):
                        act.wait_ge(S["sT_full"], 2 * t + half + 1)
                        if t >= 2:
                            act.wait_ge(S["pv_done"], t - 1)
                        nc.scalar.activation(PR[t % 2][:, 2 * half:2 * half + 2, :],
                                             ps_s[half][:, :].rearrange("p (a f) -> p a f", a=2), ACT.Exp,
                                             scale=DH ** -0.5).then_inc(S["exp_done"], 1)
                if 0 <= t - 1 < NSTEP * NB:
                    b, ps = divmod(t - 1, NSTEP)
                    g, i = STEPS[ps]
                    if g == i:
                        y_out(NT * b + g)
                for kind, o in MISC0.get(s, []):
                    if (kind, n + o) in M0:
                        misc(kind, n + o)
                if s == 8 and 0 <= n - 2 < NB:
                    b = n - 2
                    act.wait_ge(S["misc_free"], M0.full(("lg", b)))
                    nc.scalar.activation(lgx[:, :, :], lge[:, :, :], ACT.Exp).then_inc(S["lgx_rdy"], 1)
        barrier(act, 2)

    @block.vector
    def _(dve):
        def lk(ins):
            link(dve, s_dve, ins)

        nc.vector.memset(neghalf[:, :], -0.5)
        nc.vector.memset(zrow[:, :], 0.0)
        for v in VE:
            nc.vector.memset(v[:, :, :], 0.0)
        lk(nc.vector.memset(K[0][:, :].bitcast(F32), 0.0))
        for k in K[1:]:
            lk(nc.vector.memset(k[:, :].bitcast(F32), 0.0))
        for v in VE:
            nc.vector.memset(v[:, :, DH:DH + 1], 1.0)
        for k in K:
            lk(nc.vector.memset(k[KR:KM, :], -1.0))
        dve.wait_ge(s_mod_e, 1)
        lk(nc.vector.tensor_scalar_add(sT_e[:, :, :], sT_e[:, :, :], 1.0))
        lk(nc.vector.reciprocal(siluT[:, :, :], sT_e[:, :, :]))
        nc.vector.tensor_tensor(siluT[:, :, :], siluT[:, :, :], cT[:, :, :], ALU.mult).then_inc(s_silu, 1)
        dve.wait_ge(s_modps, 1)
        lk(nc.vector.tensor_copy(modT[:, :, :, :].rearrange("p l c b -> p (l c b)"), ps_misc[:, 0:2 * NCH * NB]))
        for c in (1, 4):
            lk(nc.vector.tensor_scalar_add(modT[:, :, c, :], modT[:, :, c, :], 1.0))
        dve.wait_ge(s_modps, 2)
        for l in range(2):
            lk(nc.vector.tensor_copy(modR[:, l, :].rearrange("b (h f) -> b h f", h=2),
                                     ps_s[l][0:NB, :].rearrange("b (h f) -> b h f", h=2)[:, :, 0:384]))
        gates = modR[:, :, :].rearrange("b l (h r) -> b l h r", h=2)[:, :, :, 2 * D:3 * D]
        for l in range(2):
            lk(nc.vector.tensor_scalar(gtmp[:, l, :, :], gates[:, l, :, :], 0.0, 2.0, ALU.is_ge, ALU.mult))
            lk(nc.vector.scalar_tensor_tensor(gates[:, l, :, :], gtmp[:, l, :, :], -1.0, gates[:, l, :, :],
                                              ALU.add, ALU.mult))
            lk(nc.vector.tensor_scalar(gates[:, l, :, :], gates[:, l, :, :], 0.25, None, ALU.max))
            lk(nc.vector.scalar_tensor_tensor(gates[:, l, :, :], gtmp[:, l, :, :], -1.0, gates[:, l, :, :],
                                              ALU.add, ALU.mult))
            lk(nc.vector.tensor_scalar_add(modR[:, l, 4 * D:5 * D], modR[:, l, 4 * D:5 * D], 1.0))
        barrier(dve, 1)

        def full(u):
            dve.wait_ge(S["misc_full"], M0.full(u))

        def free(u):
            dve.wait_ge(S["misc_free"], M0.full(u))

        def norm_stats(src, st, m_, rdy):
            for i in range(NT):
                last = nc.vector.bn_stats(st[:, i, :], src[:, i, :])
            lk(last)
            for i in range(NT):
                last = nc.vector.bn_aggr(m_[:, i, :], st[:, i, :])
            last.then_inc(rdy, 1)

        def norm_apply(dst, src, m_, r_, rdy):
            for i in range(NT):
                last = nc.vector.tensor_scalar(dst[:, i, :], src[:, i, :], m_[:, i, 0:1], r_[:, i:i + 1],
                                               ALU.subtract, ALU.mult)
            last.then_inc(rdy, 1)

        def misc(kind, b):
            m = ps_misc
            if kind == "q":
                dve.wait_ge(S["q1_rdy"], b + 1)
                if b >= 1:
                    dve.wait_ge(S["q3_rdy"], b)
                nc.vector.tensor_tensor(qr[:, :], m[:, :], qs[:, 0, :], ALU.subtract).then_inc(S["misc_free"], 1)
                free((kind, b))
                nc.vector.tensor_copy(qs[:, 1, :], qr[:, :]).then_inc(S["q2_rdy"], 1)
            elif kind == "k":
                dve.wait_ge(S["k1_rdy"], b + 1)
                if b >= 1:
                    dve.wait_ge(S["k3_rdy"], b)
                nc.vector.tensor_tensor(kr[:, :], m[0:DH, :], ks[:, 0, :], ALU.subtract).then_inc(S["misc_free"], 1)
                free((kind, b))
                nc.vector.tensor_copy(ks[:, 1, :], kr[:, :]).then_inc(S["k2_rdy"], 1)
            elif kind == "v":
                full((kind, b))
                nc.vector.tensor_copy(VE[b % QB][:, :, 0:DH],
                                      m[:, 0:NT * DH].rearrange("p (i d) -> p i d", d=DH)).then_inc(S["misc_free"], 1)
            elif kind == "m":
                full((kind, b))
                if b >= 1:
                    dve.wait_ge(DS["m_st"], 16 * b)
                lk(nc.vector.tensor_copy(ms[:, 0, :], m[0:64, 0:P]))
                nc.vector.tensor_tensor(mr[:, :], m[0:64, 0:P], ms[:, 0, :], ALU.subtract).then_inc(S["misc_free"], 1)
                free((kind, b))
                lk(nc.vector.tensor_copy(ms[:, 1, :], mr[:, :]))
                nc.vector.tensor_tensor(ms[:, 2, :], mr[:, :], ms[:, 1, :], ALU.subtract).then_inc(S["m_rdy"], 1)
            elif kind == "bc":
                dve.wait_ge(S["cb_rdy"], b + 1)
                nc.vector.tensor_tensor(wg[:, :], m[:, 0:D], w_cp[:, :], ALU.mult).then_inc(S["misc_free"], 1)
            elif kind == "pj":
                full((kind, b))
                nc.vector.tensor_tensor(X[:, NT * b:NT * b + NT, :], X[:, NT * b:NT * b + NT, :],
                                        m[:, :].rearrange("p (i d) -> p i d", i=NT), ALU.add).then_inc(S["misc_free"], 1)
            elif kind == "lg":
                full((kind, b))
                lg = m[:, 0:NT * NE].rearrange("p (i e) -> p i e", i=NT)
                lk(nc.vector.tensor_reduce(lgm[:, :], lg, AX_X, ALU.max))
                if b >= 1:
                    dve.wait_ge(S["lgx_rdy"], b)
                nc.vector.tensor_tensor(lge[:, :, :], lg, bc(lgm[:, :].unsqueeze(2), [P, NT, NE]),
                                        ALU.subtract).then_inc(S["misc_free"], 1)

        for n in range(-LEAD, NB + TAIL):
            for s in range(NSTEP):
                b = n + 1
                if 0 <= b < NB:
                    for k in CHUNKS[s]:
                        g, hs = GROUPS[k]
                        G = NGRP * b + k
                        w = P * (g + 1)
                        dve.wait_ge(S["mx_full"], G + 1)
                        if k == 0 and b >= 2:
                            dve.wait_ge(S["misc_full"], M0.full(("m", b - 2)))
                        c = NH * g + hs[0]
                        nc.vector.tensor_reduce(MX[b % 2][:, c:c + len(hs)],
                                                ps_mx[G % 2][:, 0:len(hs) * w].rearrange("p (x w) -> p x w", w=w),
                                                AX_X, ALU.max).then_inc(S["red_done"], 1)
                b = n + 2
                if 0 <= b < NB and s == 0:
                    dve.wait_ge(s_x[b], 16)
                    norm_stats(X[:, NT * b:NT * b + NT, :], stat, mv[b % 2], S["mv_rdy"])
                if 0 <= b < NB and s == 1:
                    dve.wait_ge(S["rs_rdy"], b + 1)
                    if b >= 1:
                        dve.wait_ge(S["misc_full"], M0.full(("hT", b - 1)))
                    norm_apply(xn, X[:, NT * b:NT * b + NT, :], mv[b % 2], rs[b % 2], S["xn_rdy"])
                b = n - 2
                if 0 <= b < NB and s == 0:
                    dve.wait_ge(S["misc_free"], M0.full(("pj", b)))
                    norm_stats(X[:, NT * b:NT * b + NT, :], stat2, mv2, S["mv2_rdy"])
                if 0 <= b < NB and s == 2:
                    dve.wait_ge(S["rs2_rdy"], b + 1)
                    if b >= 1:
                        dve.wait_ge(S["h2_rdy"], b)
                    norm_apply(xn2, X[:, NT * b:NT * b + NT, :], mv2, rs2, S["xn2_rdy"])
                b = n - 1
                if 0 <= b < NB and s == 3:
                    dve.wait_ge(DS["lc_in"], 16 * (b + 1))
                    if b >= 1:
                        dve.wait_ge(DS["r_st"], 16 * b)
                    nc.vector.reciprocal(rc[:, :], lc[:, :]).then_inc(S["rc_rdy"], 1)
                for kind, o in MISC0.get(s, []):
                    if (kind, n + o) in M0:
                        misc(kind, n + o)
                b = n - 2
                if 0 <= b < NB and s == 9:
                    dve.wait_ge(S["lgx_rdy"], b + 1)
                    lk(nc.vector.tensor_reduce(lgs[:, :], lgx[:, :, :], AX_X, ALU.add))
                    lk(nc.vector.reciprocal(lgr[:, :], lgs[:, :]))
                    if b >= 1:
                        dve.wait_ge(DS["tab_st"], 16 * b)
                    lk(nc.vector.tensor_tensor(tab[:, :, D:ROW], lgx[:, :, :], bc(lgr[:, :].unsqueeze(2), [P, NT, NE]),
                                               ALU.mult))
                    nc.vector.tensor_copy(SC[:, :, NT * b:NT * b + NT].rearrange("p e i -> p i e"),
                                          tab[:, :, D:ROW]).then_inc(S["tab_rdy"], 1)
        barrier(dve, 2)

    @block.gpsimd
    def _(pool):
        def lk(ins):
            link(pool, s_pool, ins)

        lk(nc.gpsimd.memset(ident[:, :], 0.0))
        lk(nc.gpsimd.affine_select(out=ident[:, :], in_=ident[:, :], compare_op=ALU.not_equal, fill=1.0, base=0,
                                   pattern=[[-1, P]], channel_multiplier=1))
        lk(nc.gpsimd.memset(identb[:, :], 0.0))
        lk(nc.gpsimd.affine_select(out=identb[:, :], in_=identb[:, :], compare_op=ALU.not_equal, fill=1.0, base=0,
                                   pattern=[[-1, P]], channel_multiplier=1))
        lk(nc.gpsimd.memset(maskT[:, :], 0.0))
        lk(nc.gpsimd.affine_select(out=maskT[:, :], in_=maskT[:, :], compare_op=ALU.is_ge, fill=-BIG, base=0,
                                   pattern=[[-1, P]], channel_multiplier=1))
        lk(nc.gpsimd.memset(onehot[:, :, :], 0.0))
        lk(nc.gpsimd.affine_select(out=onehot[:, :, :], in_=onehot[:, :, :], compare_op=ALU.not_equal, fill=1.0,
                                   base=0, pattern=[[-1, NB], [0, P]], channel_multiplier=1))
        for q in Q:
            nc.gpsimd.memset(q[:, :, :].rearrange("r h q -> r (h q)").bitcast(F32), 0.0)
        barrier(pool, 1)

        for n in range(-LEAD, NB + TAIL):
            for s in range(NSTEP):
                b = n + 2
                if 0 <= b < NB and s == 0:
                    pool.wait_ge(S["mv_rdy"], b + 1)
                    lk(nc.gpsimd.tensor_scalar(ve[:, :], mv[b % 2][:, :, 1], EPS, None, ALU.add))
                    nc.gpsimd.tensor_tensor(rs[b % 2][:, :], ve[:, :], neghalf[:, :], ALU.pow).then_inc(S["rs_rdy"], 1)
                if 0 <= b < NB and s == 4:
                    pool.wait_ge(S["q2_rdy"], b + 1)
                    nc.gpsimd.tensor_tensor(qs[:, 2, :], qr[:, :], qs[:, 1, :], ALU.subtract).then_inc(S["q3_rdy"], 1)
                if 0 <= b < NB and s == 6:
                    pool.wait_ge(S["k2_rdy"], b + 1)
                    nc.gpsimd.tensor_tensor(ks[:, 2, :], kr[:, :], ks[:, 1, :], ALU.subtract).then_inc(S["k3_rdy"], 1)
                b = n - 2
                if 0 <= b < NB and s == 0:
                    pool.wait_ge(S["mv2_rdy"], b + 1)
                    lk(nc.gpsimd.tensor_scalar(ve2[:, :], mv2[:, :, 1], EPS, None, ALU.add))
                    nc.gpsimd.tensor_tensor(rs2[:, :], ve2[:, :], neghalf[:, :], ALU.pow).then_inc(S["rs2_rdy"], 1)
                if 0 <= b < NB and s == 3:
                    pool.wait_ge(S["xn2_rdy"], b + 1)
                    pool.wait_ge(S["cb_rdy"], b + 1)
                    if b >= 1:
                        pool.wait_ge(DS["tab_st"], 16 * b)
                        pool.wait_ge(S["misc_full"], M0.full(("h2", b - 1)))
                    h = tab[:, :, 0:D]
                    lk(nc.gpsimd.tensor_tensor(h, xn2[:, :, :], bc(cbsb[b % 2][:, 1:2, :], [P, NT, D]), ALU.mult))
                    nc.gpsimd.tensor_tensor(h, h, bc(cbsb[b % 2][:, 0:1, :], [P, NT, D]),
                                            ALU.add).then_inc(S["h2_rdy"], 1)
                b = n - 1
                if 0 <= b < NB and s == 6:
                    pool.wait_ge(DS["yt_in"], 64 * (b + 1))
                    pool.wait_ge(DS["rl_in"], 16 * (b + 1))
                    if b >= 1:
                        pool.wait_ge(S["misc_full"], M0.full(("pj", b - 1)))
                    nc.gpsimd.tensor_tensor(yn[:, :], yt[:, :], rl[:, :], ALU.mult).then_inc(S["yn_rdy"], 1)
        barrier(pool, 2)

    @block.sync
    def _(sp):
        for dst, src in weights:
            sp.dma_start(dst, src, allow_slow_non_contiguous=True).then_inc(s_w, 16)
        xv = ins["L0_attn_x"].rearrange("b (i p) d -> b p i d", p=P)
        for b in range(NB):
            sp.dma_start(X[:, NT * b:NT * b + NT, :], xv[b]).then_inc(s_x[b], 16)
        barrier(sp, 1)
        for dst, src in late_weights:
            sp.dma_start(dst, src, allow_slow_non_contiguous=True).then_inc(s_lw, 16)
        sp.dma_start(d_acc.rearrange("(i p) d -> p i d", p=P), bc(zrow[:, :].unsqueeze(1), [P, NTILE, D])
                     ).then_inc(s_lw, 16)

        def y_store(Y):
            b, g = divmod(Y, NT)
            sp.wait_ge(S["y_ev"], Y + 1)
            if g == 0 and b >= 2:
                sp.wait_ge(DS["yt_in"], 64 * (b - 1))
                sp.wait_ge(DS["lc_in"], 16 * (b - 1))
            for j in range(4):
                sp.dma_start(d_y[b % 2][j][:, :, P * g:P * g + P],
                             ysb[Y % 2][32 * j:32 * j + DH + 1, :].rearrange("p (h q) -> p h q", q=P)
                             ).then_inc(DS[f"y_st{Y % 2}"], 16)

        for n in range(-LEAD, NB + TAIL):
            for s in range(NSTEP):
                t = NSTEP * n + s
                if 0 <= t - 1 < NSTEP * NB:
                    b, ps = divmod(t - 1, NSTEP)
                    g, i = STEPS[ps]
                    if g == i:
                        y_store(NT * b + g)
                b = n - 1
                if 0 <= b < NB and s == 0:
                    for par in range(2):
                        sp.wait_ge(DS[f"y_st{par}"], 64 * 2 * (b + 1))
                    if b >= 1:
                        sp.wait_ge(S["rc_rdy"], b)
                        sp.wait_ge(S["yn_rdy"], b)
                    y = d_y[b % 2]
                    sp.dma_start(lc[:, :], bass.AP(y.tensor, DH * 4 * T, [[(DH + 1) * 4 * T, 4], [64, 32], [1, 64]])
                                 ).then_inc(DS["lc_in"], 16)
                    for j in range(4):
                        sp.dma_start(yt[32 * j:32 * j + 32, :],
                                     bass.AP(y.tensor, j * (DH + 1) * 4 * T, [[T, 4], [4 * T, DH], [1, T]])
                                     ).then_inc(DS["yt_in"], 16)
                if 0 <= b < NB and s == 4:
                    sp.wait_ge(S["rc_rdy"], b + 1)
                    if b >= 2:
                        sp.wait_ge(DS["rl_in"], 16 * (b - 1))
                    r = d_r[b % 2]
                    sp.dma_start(r.rearrange("h (a q) -> (h a) q", q=64), rc[:, :]).then_inc(DS["r_st"], 16)
                    sp.wait_ge(DS["r_st"], 16 * (b + 1))
                    sp.dma_start(rl[:, :], bass.AP(r.tensor, 0, [[T, NH], [0, DH], [1, T]])).then_inc(DS["rl_in"], 16)
                b = n + 2
                if 0 <= b < NB and s == 5:
                    par = b % 2
                    sp.wait_ge(S["q3_rdy"], b + 1)
                    if b >= 2:
                        sp.wait_ge(DS[f"q_in{par}"], 64 * (b // 2))
                    for a in range(PARTS):
                        sp.dma_start(bass.AP(d_q[par].tensor, a * D * T, [[T, NH], [NH * T, DH], [1, T]]),
                                     qs[:, a, :]).then_inc(DS[f"q_st{par}"], 16)
                    sp.wait_ge(DS[f"q_st{par}"], 48 * (b // 2 + 1))
                    sp.dma_start(Q[b % QB][0:NPR].rearrange("r h q -> r (h q)"),
                                 bass.AP(d_q[par].tensor, 0, [[0, PARTS], [NH * T, PARTS * DH], [1, NH * T]])
                                 ).then_inc(DS[f"q_in{par}"], 16)
                if 0 <= b < NB and s == 6:
                    par = b % 2
                    sp.wait_ge(S["k3_rdy"], b + 1)
                    sp.dma_start(bass.AP(d_k[par].tensor, 0, [[T, DH], [DH * T, PARTS], [1, T]]),
                                 ks[:, :, :]).then_inc(DS[f"k_st{par}"], 16)
                    sp.wait_ge(DS[f"k_st{par}"], 16 * (b // 2 + 1))
                    for c in range(PARTS):
                        sp.dma_start(K[b % QB][24 * c:24 * c + 24, :],
                                     bass.AP(d_k[par].tensor, c * DH * T, [[0, PARTS], [T, DH], [1, T]])
                                     ).then_inc(DS[f"q_in{par}"], 16)
                b = n + 1
                if 0 <= b < NB and s == 8:
                    par = b % 2
                    sp.wait_ge(S["m_rdy"], b + 1)
                    if b >= 2:
                        sp.wait_ge(DS[f"m_in{par}"], 48 * (b // 2))
                    sp.dma_start(d_m[par].rearrange("a g f -> g a f"), ms[:, :, :]).then_inc(DS["m_st"], 16)
                    sp.wait_ge(DS["m_st"], 16 * (b + 1))
                    for a in range(PARTS):
                        sp.dma_start(Q[b % QB][KR + a:KR + a + 1, :, :],
                                     bass.AP(d_m[par].tensor, a * 64 * P, [[P, NH], [NH * P, NT], [1, P]])
                                     ).then_inc(DS[f"m_in{par}"], 16)
                b = n - 2
                if 0 <= b < NB and s == 9:
                    sp.wait_ge(S["tab_rdy"], b + 1)
                    sp.dma_start(d_tab[T * b:T * b + T, :].rearrange("(i p) f -> p i f", p=P),
                                 tab[:, :, :]).then_inc(DS["tab_st"], 16)
        sp.wait_ge(DS["tab_st"], 16 * NB)
        sp.wait_ge(s_lw, 16 * (len(late_weights) + 1))
        barrier(sp, 2)
        if stop_after == "attn0":
            ov = out.rearrange("b (i p) d -> p (b i) d", p=P)
            sp.dma_start(ov, X[:, :, :]).then_inc(DS["tab_st"], 16)
            sp.wait_ge(DS["tab_st"], 16 * (NB + 1))

    a0.close()
    if stop_after == "attn0":
        return
    g = Shared()
    g.X = X
    g.ident = ident
    g.identb = identb
    g.neghalf = neghalf
    g.onehot = onehot
    g.modT = modT
    g.modR = modR
    g.SC = SC
    g.w1 = w1
    g.w2 = w2
    g.b1T = b1T
    g.b2r = b2r
    g.w_qkv = w_qkv
    g.w_proj = w_proj
    g.b_proj = b_proj
    g.w_cm = w_cm
    g.mu = mu
    g.gamma = gamma
    g.beta = beta
    g.s_phase = s_phase
    g.d_tab = d_tab
    g.d_acc = d_acc
    g.chains = chains
    g.ins = ins
    moe(nc, ctx, g)
    mid.close()
    if stop_after == "moe":
        block1(nc, ctx, g, out, dump=True)
        return
    block1(nc, ctx, g, out)


def moe(nc, ctx, g):
    ph = ExitStack()

    def sb(name, shape, dt=F32):
        return ph.enter_context(nc.sbuf_tensor(name, shape, dt))

    def sem(name):
        return ctx.enter_context(nc.semaphore(name))

    def bc(ap, shape):
        return ap.to_broadcast(shape)

    NG = P // NE
    ST = sb("ST", [P, 2 * P])
    SCh = sb("SCh", [P, 2, NE, NG])
    upper = sb("upper", [P, P])
    group = sb("group", [P, P])
    ones = sb("ones", [P, P])
    iota = sb("iota", [P, P])
    iota_p = sb("iota_p", [P, 1])
    biti = sb("biti", [P, BITS], I32)
    bitf = sb("bitf", [P, BITS])
    thr = sb("thr", [P, 1], I32)
    cand = sb("cand", [P, 1], I32)
    take = sb("take", [P, 1], I32)
    hit = sb("hit", [P, 2 * P])
    cnt = sb("cnt", [P, 1])
    thb = sb("thb", [P, P])
    TH = sb("TH", [P, NE])
    gt = sb("gt", [P, NE, NTILE])
    eq = sb("eq", [P, NE, NTILE])
    sel = sb("sel", [P, NE, NTILE])
    tot = sb("tot", [P, NE, NTILE])
    run = sb("run", [P, NE, NTILE])
    pos = sb("pos", [P, NE, NTILE])
    onesv = sb("onesv", [P, NE, NTILE])
    need = sb("need", [P, NE])
    posi = sb("posi", [P, NE, NTILE], I32)
    slot = sb("slot", [P, NE, NTILE], I32)
    stile = sb("stile", [P, NE, NTILE], I32)
    slotf = sb("slotf", [P, NE, NTILE])
    stilef = sb("stilef", [P, NE, NTILE])
    A = sb("A", [P, NE, NTILE, 2 * NS], BF16)
    R = [sb(f"R{i}", [P, NTILE, P], BF16) for i in range(2)]
    lst = sb("lst", [P, 2 * NS])
    lstf = sb("lstf", [P, NS])
    idx = sb("idx", [P, NE, NS], I32)
    B2 = sb("B2", [P, NE, D])
    XG = [sb(f"XG{i}", [P, NS, ROW]) for i in range(2)]
    XT = [sb(f"XT{i}", [P, CAP]) for i in range(2)]
    H = [sb(f"H{i}", [P, NC_DI, 512]) for i in range(2)]
    yb = sb("yb", [P, 512])
    Y = [sb(f"Y{i}", [P, NS, D]) for i in range(2)]

    ps_x = [ph.enter_context(nc.psum_tensor(f"ps_x{i}", [P, 512], F32)) for i in range(2)]
    ps_h = [ph.enter_context(nc.psum_tensor(f"ps_h{i}", [P, 512], F32)) for i in range(2)]
    ps_o = [ph.enter_context(nc.psum_tensor(f"ps_o{i}", [P, 512], F32)) for i in range(2)]
    ps_l = ph.enter_context(nc.psum_tensor("ps_l", [P, 512], F32))
    ps_r = ph.enter_context(nc.psum_tensor("ps_r", [P, 512], F32))

    sc_rdy = sem("r_scores_split")
    consts, sT_ps, st_rdy = sem("r_consts"), sem("r_scoresT"), sem("r_scoresT_copied")
    rnd, cnt_rdy, sum_rdy = sem("r_round_chain"), sem("r_counts"), sem("r_sums")
    th_in, th_ps, io_ps, b2_ps, b2_cp = sem("r_thr_in"), sem("r_thr_ps"), sem("r_iota_ps"), sem("r_b2_ps"), sem("r_b2_copied")
    gt_rdy, gt_ps, eq_rdy, eq_ps, sel_rdy, sel_ps = (sem("r_" + n) for n in ("gt", "gt_ps", "eq", "eq_ps", "sel", "sel_ps"))
    R_rdy, l_ps, l_free, idx_rdy = sem("m_onehot"), sem("m_list_ps"), sem("m_list_copied"), sem("m_idx")
    gat = [sem(f"m_gathered{i}") for i in range(2)]
    scat = sem("m_scattered")
    x_ps, x_cp, h_ps, h_cp, o_ps, o_cp, y_rdy = (sem("m_" + n) for n in
                                                 ("xT_ps", "xT_copied", "h_ps", "gelu", "out_ps", "out_copied", "y"))
    s_dve, s_pool = sem("m_dve_chain"), sem("m_pool_chain")

    def link(eng, s, ins):
        g.chains[id(s)] = g.chains.get(id(s), 0) + 1
        ins.then_inc(s, 1)
        eng.wait_ge(s, g.chains[id(s)])

    def barrier(eng, k):
        eng.drain().then_inc(g.s_phase, 1)
        eng.wait_ge(g.s_phase, 5 * k)

    block = ph.enter_context(nc.Block())

    @block.gpsimd
    def _(pool):
        def lk(ins):
            link(pool, s_pool, ins)

        lk(nc.gpsimd.memset(upper[:, :], 1.0))
        lk(nc.gpsimd.affine_select(out=upper[:, :], in_=upper[:, :], compare_op=ALU.is_ge, fill=0.0, base=-1,
                                   pattern=[[1, P]], channel_multiplier=-1))
        lk(nc.gpsimd.memset(group[:, :], 1.0))
        gv = group[:, :].rearrange("p (a b) -> p a b", b=NG)
        lk(nc.gpsimd.affine_select(out=gv, in_=gv, compare_op=ALU.is_ge, fill=0.0, base=0,
                                   pattern=[[-NG, NE], [0, NG]], channel_multiplier=1))
        lk(nc.gpsimd.affine_select(out=gv, in_=gv, compare_op=ALU.is_ge, fill=0.0, base=NG - 1,
                                   pattern=[[NG, NE], [0, NG]], channel_multiplier=-1))
        nc.gpsimd.drain().then_inc(consts, 1)

        def gathers(e):
            pool.wait_ge(idx_rdy, e + 1)
            if e >= 2:
                pool.wait_ge(x_ps, 2 * (e - 1))
                pool.wait_ge(y_rdy, 2 * (e - 1))
            for k in range(NS):
                nc.gpsimd.indirect_dma_start(out=XG[e % 2][:, k, :], out_offset=None, in_=g.d_tab,
                                             in_offset=bass.IndirectOffsetOnAxis(ap=idx[:, e, k:k + 1], axis=0)
                                             ).then_inc(gat[e % 2], 16)

        def scatters(e):
            if e >= 1:
                pool.wait_ge(scat, 16 * NS * e)
            for k in range(NS):
                if k % 4 == 0:
                    pool.wait_ge(y_rdy, 2 * e + k // 4 + 1)
                nc.gpsimd.indirect_dma_start(out=g.d_acc, out_offset=bass.IndirectOffsetOnAxis(ap=idx[:, e, k:k + 1], axis=0),
                                             in_=Y[e % 2][:, k, :], in_offset=None,
                                             compute_op=ALU.add).then_inc(scat, 16)

        gathers(0)
        for e in range(NE):
            if e + 1 < NE:
                gathers(e + 1)
            scatters(e)
        pool.wait_ge(scat, 16 * NS * NE)
        barrier(pool, 3)

    @block.vector
    def _(dve):
        def lk(ins):
            link(dve, s_dve, ins)

        V = nc.vector
        V.memset(ones[:, :], 1.0)
        V.memset(onesv[:, :, :], 1.0)
        for r in range(BITS):
            V.memset(biti[:, r:r + 1], 1 << (BITS - 1 - r))
            V.memset(bitf[:, r:r + 1], float(1 << (BITS - 1 - r)))
        lk(V.memset(thr[:, :], 0))
        nc.vector.drain().then_inc(consts, 1)
        dve.wait_ge(consts, 2)
        dve.wait_ge(sT_ps, 1)
        V.tensor_copy(ST[:, :], ps_x[0][:, 0:2 * P]).then_inc(st_rdy, 1)
        dve.wait_ge(io_ps, 1)
        V.tensor_copy(iota[:, :], ps_x[1][:, 0:P])
        lk(V.tensor_copy(iota_p[:, :], ps_x[1][:, P:P + 1]))
        dve.wait_ge(b2_ps, 1)
        V.tensor_copy(B2[:, 0:4, :], ps_h[0][:, :].rearrange("p (e d) -> p e d", d=D))
        V.tensor_copy(B2[:, 4:8, :], ps_h[1][:, :].rearrange("p (e d) -> p e d", d=D)).then_inc(b2_cp, 1)
        dve.wait_ge(st_rdy, 1)
        dve.wait_ge(b2_cp, 1)
        with dve.Fori(0, BITS) as r:
            V.tensor_tensor(cand[:, :], thr[:, :], biti[:, bass.ds(r, 1)], ALU.bitwise_or).then_inc(rnd, 1)
            dve.wait_ge(rnd, 3 * r + 1)
            V.tensor_scalar(hit[:, :], ST[:, :], cand[:, :].bitcast(F32), None, ALU.is_ge, ALU.add,
                            accum_out=cnt[:, 0:1]).then_inc(cnt_rdy, 1)
            dve.wait_ge(sum_rdy, r + 1)
            V.tensor_scalar(take[:, :], ps_r[:, 0:1], float(CAP), bitf[:, bass.ds(r, 1)], ALU.is_ge,
                            ALU.mult).then_inc(rnd, 1)
            dve.wait_ge(rnd, 3 * r + 2)
            V.tensor_tensor(thr[:, :], thr[:, :], take[:, :], ALU.bitwise_or).then_inc(rnd, 1)
            dve.wait_ge(rnd, 3 * r + 3)
        V.tensor_copy(thb[:, :], bc(thr[:, :].bitcast(F32), [P, P])).then_inc(th_in, 1)
        dve.wait_ge(th_ps, 1)
        lk(V.tensor_copy(TH[:, :], ps_r[:, P:2 * P].rearrange("p (e x) -> p e x", x=NG)[:, :, 0]))
        full3 = [P, NE, NTILE]
        V.tensor_tensor(gt[:, :, :], g.SC[:, :, :], bc(TH[:, :].unsqueeze(2), full3), ALU.is_gt).then_inc(gt_rdy, 1)
        V.tensor_tensor(eq[:, :, :], g.SC[:, :, :], bc(TH[:, :].unsqueeze(2), full3), ALU.is_equal).then_inc(eq_rdy, 1)
        dve.wait_ge(gt_ps, 1)
        lk(V.tensor_reduce(need[:, :], ps_r[:, 256:512].rearrange("p (e t) -> p e t", t=NTILE), AX_X, ALU.add))
        lk(V.tensor_scalar(need[:, :], need[:, :], -1.0, float(CAP), ALU.mult, ALU.add))

        def ranks(dst, ps):
            lk(V.tensor_copy(tot[:, :, :], ps[:, 256:512].rearrange("p (e t) -> p e t", t=NTILE)))
            lk(V.tensor_tensor_scan(run[:, :, :].rearrange("p e t -> p (e t)"),
                                    onesv[:, :, :].rearrange("p e t -> p (e t)"),
                                    tot[:, :, :].rearrange("p e t -> p (e t)"), 0.0, ALU.mult, ALU.add))
            lk(V.tensor_tensor(run[:, :, :], run[:, :, :], tot[:, :, :], ALU.subtract))
            lk(V.tensor_tensor(dst[:, :, :], run[:, :, :], ps[:, 0:256].rearrange("p (e t) -> p e t", t=NTILE), ALU.add))

        dve.wait_ge(eq_ps, 1)
        ranks(pos, ps_x[0])
        lk(V.tensor_tensor(pos[:, :, :], pos[:, :, :], bc(run[:, :, 0:1], full3), ALU.subtract))
        lk(V.tensor_tensor(sel[:, :, :], pos[:, :, :], bc(need[:, :].unsqueeze(2), full3), ALU.is_lt))
        lk(V.tensor_tensor(sel[:, :, :], sel[:, :, :], eq[:, :, :], ALU.mult))
        V.tensor_tensor(sel[:, :, :], sel[:, :, :], gt[:, :, :], ALU.add).then_inc(sel_rdy, 1)
        dve.wait_ge(sel_ps, 1)
        ranks(pos, ps_x[1])
        lk(V.tensor_copy(posi[:, :, :], pos[:, :, :]))
        lk(V.tensor_scalar(slot[:, :, :], posi[:, :, :], P - 1, None, ALU.bitwise_and))
        lk(V.tensor_scalar(stile[:, :, :], posi[:, :, :], CAP - P, None, ALU.bitwise_and))
        lk(V.tensor_copy(slotf[:, :, :], slot[:, :, :]))
        lk(V.tensor_scalar_add(slotf[:, :, :], slotf[:, :, :], 1.0))
        lk(V.tensor_tensor(slotf[:, :, :], slotf[:, :, :], sel[:, :, :], ALU.mult))
        lk(V.tensor_scalar_add(slotf[:, :, :], slotf[:, :, :], -1.0))
        lk(V.tensor_copy(stilef[:, :, :], stile[:, :, :]))
        for k in range(NS):
            lk(V.scalar_tensor_tensor(A[:, :, :, k], stilef[:, :, :], float(P * k),
                                   bc(iota[:, 0:NTILE].unsqueeze(1), full3), ALU.is_equal, ALU.mult))
            lk(V.tensor_scalar(A[:, :, :, NS + k], stilef[:, :, :], float(P * k), iota_p[:, 0:1], ALU.is_equal, ALU.mult))

        def onehot(e):
            if e >= 2:
                dve.wait_ge(l_ps, e - 1)
            V.tensor_tensor(R[e % 2][:, :, :], bc(iota[:, :].unsqueeze(1), [P, NTILE, P]),
                            bc(slotf[:, e, :].unsqueeze(2), [P, NTILE, P]), ALU.is_equal).then_inc(R_rdy, 1)

        def index(e):
            dve.wait_ge(l_ps, e + 1)
            lk(V.tensor_copy(lst[:, :], ps_l[:, 0:2 * NS]))
            nc.vector.scalar_tensor_tensor(lstf[:, :], lst[:, 0:NS], float(P), lst[:, NS:2 * NS], ALU.mult,
                                           ALU.add).then_inc(l_free, 1)
            dve.wait_ge(l_free, e + 1)
            V.tensor_copy(idx[:, e, :], lstf[:, :]).then_inc(idx_rdy, 1)

        onehot(0)
        index(0)
        onehot(1)
        index(1)
        for e in range(NE):
            if e + 2 < NE:
                onehot(e + 2)
                index(e + 2)
            for h in range(2):
                dve.wait_ge(o_ps, 2 * e + h + 1)
                if 2 * e + h >= 1:
                    dve.wait_ge(y_rdy, 2 * e + h)
                V.tensor_tensor(yb[:, :].rearrange("p (k d) -> p k d", d=D),
                                ps_o[h][:, :].rearrange("p (k d) -> p k d", d=D),
                                bc(B2[:, e:e + 1, :], [P, 4, D]), ALU.add).then_inc(o_cp, 1)
                dve.wait_ge(o_cp, 2 * e + h + 1)
                if e >= 2 and h == 0:
                    dve.wait_ge(scat, 16 * NS * (e - 1))
                if h == 0:
                    dve.wait_ge(gat[e % 2], 16 * NS * (e // 2 + 1))
                V.tensor_tensor(Y[e % 2][:, 4 * h:4 * h + 4, :], yb[:, :].rearrange("p (k d) -> p k d", d=D),
                                bc(XG[e % 2][:, 4 * h:4 * h + 4, D + e:D + e + 1], [P, 4, D]),
                                ALU.mult).then_inc(y_rdy, 1)
        barrier(dve, 3)

    @block.tensor
    def _(pe):
        T_ = nc.tensor
        pe.wait_ge(consts, 2)
        pe.wait_ge(sc_rdy, 1)
        for h in range(2):
            last = T_.transpose(ps_x[0][:, P * h:P * h + P], SCh[:, h, :, :].rearrange("p e t -> p (e t)"), g.ident[:, :])
        last.then_inc(sT_ps, 1)
        T_.matmul(ps_x[1][:, 0:P], ones[:, :], upper[:, :], start=True, stop=True)
        T_.matmul(ps_x[1][:, P:P + 1], upper[:, :], ones[:, 0:1], start=True, stop=True).then_inc(io_ps, 1)
        for h in range(2):
            last = T_.matmul(ps_h[h][:, :], ones[0:1, :], g.b2r[:, 4 * h:4 * h + 4, :], start=True, stop=True)
        last.then_inc(b2_ps, 1)
        with pe.Fori(0, BITS) as r:
            pe.wait_ge(cnt_rdy, r + 1)
            T_.matmul(ps_r[:, 0:1], group[:, :], cnt[:, 0:1], start=True, stop=True).then_inc(sum_rdy, 1)
        pe.wait_ge(th_in, 1)
        T_.transpose(ps_r[:, P:2 * P], thb[:, :], g.ident[:, :]).then_inc(th_ps, 1)
        flat = lambda t: t[:, :, :].rearrange("p e t -> p (e t)")
        pe.wait_ge(gt_rdy, 1)
        T_.matmul(ps_r[:, 256:512], ones[:, :], flat(gt), start=True, stop=True).then_inc(gt_ps, 1)
        for rdy, x, ps, done in ((eq_rdy, eq, ps_x[0], eq_ps), (sel_rdy, sel, ps_x[1], sel_ps)):
            pe.wait_ge(rdy, 1)
            T_.matmul(ps[:, 0:256], upper[:, :], flat(x), start=True, stop=True)
            T_.matmul(ps[:, 256:512], ones[:, :], flat(x), start=True, stop=True).then_inc(done, 1)

        def lists(e):
            pe.wait_ge(R_rdy, e + 1)
            if e >= 1:
                pe.wait_ge(l_free, e)
            for t in range(NTILE):
                last = T_.matmul(ps_l[:, 0:2 * NS], R[e % 2][:, t, :], A[:, e, t, :], start=(t == 0), stop=(t == NTILE - 1))
            last.then_inc(l_ps, 1)

        def rows_T(e):
            pe.wait_ge(gat[e % 2], 16 * NS * (e // 2 + 1))
            for h in range(2):
                if e >= 1:
                    pe.wait_ge(x_cp, 2 * e - 1 + h)
                for k in range(4):
                    last = T_.transpose(ps_x[h][:, P * k:P * k + P], XG[e % 2][:, 4 * h + k, 0:D], g.ident[:, :])
                last.then_inc(x_ps, 1)

        def first(e):
            for h in range(2):
                pe.wait_ge(x_cp, 2 * e + h + 1)
                for c in range(NC_DI):
                    u = NC_DI * (2 * e + h) + c
                    if u >= 2:
                        pe.wait_ge(h_cp, u - 1)
                    T_.matmul(ps_h[u % 2][:, :], g.w1[:, e, P * c:P * c + P], XT[e % 2][:, 512 * h:512 * h + 512],
                              start=True, stop=True).then_inc(h_ps, 1)

        def second(e):
            for h in range(2):
                pe.wait_ge(h_cp, NC_DI * (2 * e + h + 1))
                if e >= 1:
                    pe.wait_ge(o_cp, 2 * e - 1 + h)
                for k in range(4):
                    for c in range(NC_DI):
                        last = T_.matmul(ps_o[h][:, P * k:P * k + P], H[h][:, c, P * k:P * k + P], g.w2[:, e, c, :],
                                         start=(c == 0), stop=(c == NC_DI - 1))
                last.then_inc(o_ps, 1)

        lists(0)
        lists(1)
        rows_T(0)
        for e in range(NE):
            first(e)
            if e + 2 < NE:
                lists(e + 2)
            if e + 1 < NE:
                rows_T(e + 1)
            second(e)
        barrier(pe, 3)

    @block.scalar
    def _(act):
        nc.scalar.activation(SCh[:, 0, :, :], g.SC[:, :, 0:NG], ACT.Copy)
        nc.scalar.activation(SCh[:, 1, :, :], g.SC[:, :, NG:2 * NG], ACT.Copy).then_inc(sc_rdy, 1)
        for e in range(NE):
            for h in range(2):
                act.wait_ge(x_ps, 2 * e + h + 1)
                if e >= 2 and h == 0:
                    act.wait_ge(h_ps, 2 * NC_DI * (e - 1))
                nc.scalar.activation(XT[e % 2][:, 512 * h:512 * h + 512], ps_x[h][:, :], ACT.Copy).then_inc(x_cp, 1)
            for h in range(2):
                if e >= 1:
                    act.wait_ge(o_ps, 2 * e - 1 + h)
                for c in range(NC_DI):
                    u = NC_DI * (2 * e + h) + c
                    act.wait_ge(h_ps, u + 1)
                    nc.scalar.activation(H[h][:, c, :], ps_h[u % 2][:, :], ACT.Gelu,
                                         bias=g.b1T[:, e, c:c + 1]).then_inc(h_cp, 1)
        barrier(act, 3)

    @block.sync
    def _(sp):
        barrier(sp, 3)

    ph.close()


MISC1 = {0: [("qk0", 2), ("ck", -2)], 1: [("qk1", 2), ("cr", -2)], 2: [("kT", 1), ("qk2", 2), ("yT", -1)],
         3: [("qT", 1), ("qk3", 2), ("pj", -1), ("kv", -2)], 6: [("gT", -1)], 7: [("hT", 3)]}
LEAD1, TAIL1 = 3, 3
NU = 2 * NT
HU = NH // 2
DV = DH + 1


def block1(nc, ctx, g, out, dump=False):
    if dump:
        sd = ctx.enter_context(nc.semaphore("dumped"))
        with nc.Block() as block:
            @block.sync
            def _(sp):
                sp.dma_start(out.rearrange("b t d -> (b t) d"), g.d_acc).then_inc(sd, 16)
                sp.wait_ge(sd, 16)
        return
    ph = ExitStack()

    def sb(name, shape, dt=F32):
        return ph.enter_context(nc.sbuf_tensor(name, shape, dt))

    def sem(name):
        return ctx.enter_context(nc.semaphore(name))

    def bc(ap, shape):
        return ap.to_broadcast(shape)

    X, modT, ident = g.X, g.modT, g.ident
    wqk = g.w_qkv[:, 0:2 * D]
    WT = sb("WT", [P, 3, D])
    GG = sb("GG", [P, NB, 3, D])
    WPG = sb("WPG", [P, NB, D])
    WVG = sb("WVG", [P, NB, D])
    BPG = sb("BPG", [P, NB, D])
    nh32 = sb("nh32", [P, 2 * NH])
    gmean = sb("gmean", [P, 2 * NH])
    m1 = sb("m1", [P, 2])
    KB = [sb(f"KB{i}", [P, NH, T]) for i in range(2)]
    QT = [sb(f"QT{i}", [P, T]) for i in range(2)]
    KT = sb("KT", [P, T])
    VB = [sb(f"VB{i}", [P, NT, 2, HU, 2 * DV]) for i in range(3)]
    AC = sb("AC", [P, NT, D])
    stat = sb("bstat", [P, NT, 6])
    mv = sb("bmv", [P, NT, 2])
    ve = sb("bve", [P, NT])
    rs = sb("brs", [P, NT])
    xn = sb("bxn", [P, NT, D])
    hT = sb("bhT", [P, T])
    sq = [sb(f"sq{i}", [P, 2 * D]) for i in range(2)]
    QK = [sb(f"QK{i}", [P, NT, 2 * D]) for i in range(2)]
    var = [sb(f"var{i}", [P, NT, 2 * NH]) for i in range(2)]
    rq = [sb(f"rq{i}", [P, NT, 2 * NH]) for i in range(2)]
    QKN = sb("QKN", [P, NT, 2 * D])
    mxs = [sb(f"mxs{i}", [P, HU]) for i in range(2)]
    SU = [sb(f"SU{i}", [P, 512]) for i in range(2)]
    PB = [sb(f"PB{i}", [P, 512]) for i in range(2)]
    PT = [sb(f"PT{i}", [P, 512]) for i in range(2)]
    rcp = sb("rcp", [P, 2, NH])
    YN = sb("YN", [P, NT, D])
    yT = sb("yT", [P, T])
    stat2 = sb("bstat2", [P, NT, 6])
    mv2 = sb("bmv2", [P, NT, 2])
    ve2 = sb("bve2", [P, NT])
    rs2 = sb("brs2", [P, NT])
    xn2 = sb("bxn2", [P, NT, D])
    GT = sb("GT", [P, T + 1])
    t1 = sb("t1", [P, 2, T])
    xm = sb("xm", [P, 2, T])
    KA = sb("KA", [P, T])
    KA2 = sb("KA2", [P, T])
    RT = sb("RT", [P, T])
    OU = sb("OU", [P, NT, D])

    ps = [ph.enter_context(nc.psum_tensor(f"b1ps{i}", [P, 512], F32)) for i in range(8)]
    ps_s, ps_t, ps_v, ps_m = ps[0:2], ps[2:4], ps[4:6], ps[6:8]

    names = ["wT_ps", "wT", "gg_ps", "gg", "s_ps", "max", "sub", "exp", "t_ps", "pt", "v_ps", "yn",
             "accg", "xadd", "mv", "rs", "xn", "qk_cp", "sq", "var", "rq", "qkn", "bp",
             "mv2", "rs2", "xn2", "t1", "xm", "ka2", "xo", "misc_free0", "misc_free1",
             "misc_full0", "misc_full1"]
    S = {n: sem("b1_" + n) for n in names}
    k_in = [sem(f"b1_keys_in{i}") for i in range(2)]
    acc_in, o_st = sem("b1_acc_in"), sem("b1_out_stored")
    s_dve, s_pool = sem("b1_dve_chain"), sem("b1_pool_chain")
    order = [(kind, n + o) for n in range(-LEAD1, NB + TAIL1) for u in range(NU)
             for kind, o in MISC1.get(u, []) if 0 <= n + o < NB]
    M = Misc(order, 2)

    def link(eng, s, ins):
        g.chains[id(s)] = g.chains.get(id(s), 0) + 1
        ins.then_inc(s, 1)
        eng.wait_ge(s, g.chains[id(s)])

    def barrier(eng, k):
        eng.drain().then_inc(g.s_phase, 1)
        eng.wait_ge(g.s_phase, 5 * k)

    def m_of(u):
        return ps_m[M.bank(u)]

    def full(eng, u):
        eng.wait_ge(S[f"misc_full{M.bank(u)}"], M.full(u))

    def free(u):
        return S[f"misc_free{M.bank(u)}"]

    def evacuated(eng, u):
        eng.wait_ge(free(u), M.full(u))

    block = ph.enter_context(nc.Block())

    @block.tensor
    def _(pe):
        T_ = nc.tensor
        for k in range(3):
            last = T_.transpose(ps_m[0][:, P * k:P * k + P], g.w_cm[:, k, :], ident[:, :])
        last.then_inc(S["wT_ps"], 1)
        for b in range(NB):
            if b >= 2:
                pe.wait_ge(S["gg"], b - 1)
            for k, (l, c) in enumerate(((0, 5), (1, 2), (1, 5))):
                last = T_.matmul(ps_s[b % 2][:, D * k:D * k + D], g.onehot[:, b, :], g.modR[:, l, D * c:D * c + D],
                                 start=True, stop=True)
            last.then_inc(S["gg_ps"], 1)
        barrier(pe, 4)

        def misc(kind, b):
            u = (kind, b)
            m = m_of(u)
            if M.full(u) >= 2:
                pe.wait_ge(free(u), M.full(u) - 1)
            if kind == "hT":
                pe.wait_ge(S["xn"], b + 1)
                for i in range(NT):
                    last = T_.transpose(m[:, P * i:P * i + P], xn[:, i, :], ident[:, :])
            elif kind[:2] == "qk":
                i = int(kind[2])
                evacuated(pe, ("hT", b))
                T_.matmul(m[:, 0:2 * D], hT[:, P * i:P * i + P], wqk, start=True, stop=True)
                for w in range(2):
                    for h2 in range(2):
                        last = T_.matmul(m[64 * h2:64 * h2 + 64, 2 * D + 64 * w:2 * D + 64 * w + 64],
                                         hT[:, P * i + 64 * w:P * i + 64 * w + 64],
                                         g.w_qkv[:, 2 * D:3 * D].rearrange("c (a b d) -> c b a d", b=2, d=DH)[:, h2],
                                         start=True, stop=True, tile_position=(0, 64 * h2), skip_group_check=True)
            elif kind == "kT" or kind == "qT":
                pe.wait_ge(S["qkn"], b + 1)
                o = D if kind == "kT" else 0
                for i in range(NT):
                    last = T_.transpose(m[:, P * i:P * i + P], QKN[:, i, o:o + D], ident[:, :])
            elif kind == "yT":
                pe.wait_ge(S["yn"], NT * (b + 1))
                for i in range(NT):
                    last = T_.transpose(m[:, P * i:P * i + P], YN[:, i, :], ident[:, :])
            elif kind == "pj":
                evacuated(pe, ("yT", b))
                for i in range(NT):
                    last = T_.matmul(m[:, P * i:P * i + P], yT[:, P * i:P * i + P], WPG[:, b, :], start=True, stop=True)
            elif kind == "gT":
                pe.wait_ge(S["xn2"], b + 1)
                for i in range(NT):
                    last = T_.transpose(m[:, P * i:P * i + P], xn2[:, i, :], ident[:, :])
            elif kind == "ck":
                pe.wait_ge(S["xm"], b + 1)
                last = T_.matmul(m[:, :], WT[:, 1, :], xm[:, 1, :], start=True, stop=True)
            elif kind == "cr":
                for i in range(NT):
                    last = T_.matmul(m[:, P * i:P * i + P], xm[:, 0, P * i:P * i + P], WT[:, 0, :], start=True, stop=True)
            elif kind == "kv":
                pe.wait_ge(S["ka2"], b + 1)
                for i in range(NT):
                    last = T_.matmul(m[:, P * i:P * i + P], KA2[:, P * i:P * i + P], WVG[:, b, :], start=True, stop=True)
            last.then_inc(S[f"misc_full{M.bank(u)}"], 1)

        def scores(U):
            b, u = divmod(U, NU)
            i, hh = divmod(u, 2)
            if u == 0:
                evacuated(pe, ("qT", b))
                pe.wait_ge(k_in[b % 2], 16 * NH * (b // 2 + 1))
            if U >= 2:
                pe.wait_ge(S["sub"], U - 1)
            for j in range(4):
                o = P * i + 64 * (j // 2)
                last = T_.matmul(ps_s[U % 2][32 * j:32 * j + 32, :], QT[b % 2][:, P * i + 32 * j:P * i + 32 * j + 32],
                                 KB[b % 2][:, HU * hh:HU * hh + HU, o:o + 64], start=True, stop=True,
                                 tile_position=(0, 32 * j))
            last.then_inc(S["s_ps"], 1)

        def transposes(U):
            pe.wait_ge(S["exp"], U + 1)
            if U >= 2:
                pe.wait_ge(S["pt"], U - 1)
            for k in range(HU // 2):
                last = T_.transpose(ps_t[U % 2][:, P * k:P * k + P], PB[U % 2][:, P * k:P * k + P], ident[:, :])
            last.then_inc(S["t_ps"], 1)

        def values(U):
            b, u = divmod(U, NU)
            i, hh = divmod(u, 2)
            tile = U // 2
            pe.wait_ge(S["pt"], U + 1)
            if hh == 0 and tile >= 2:
                pe.wait_ge(S["yn"], tile - 1)
            for k in range(HU // 2):
                c = 2 * DV * (k + HU // 2 * hh)
                for j in range(4):
                    last = T_.matmul(ps_v[tile % 2][32 * j:32 * j + 32, c:c + 2 * DV],
                                     PT[U % 2][:, P * k + 32 * j:P * k + 32 * j + 32],
                                     VB[b % 3][:, i, j // 2, k + HU // 2 * hh, :], start=True, stop=True,
                                     tile_position=(0, 32 * j), skip_group_check=True)
            last.then_inc(S["v_ps"], 1)

        for n in range(-LEAD1, NB + TAIL1):
            for u in range(NU):
                U = NU * n + u
                if 0 <= U < NU * NB:
                    scores(U)
                for kind, o in MISC1.get(u, []):
                    if (kind, n + o) in M:
                        misc(kind, n + o)
                if 0 <= U - 1 < NU * NB:
                    transposes(U - 1)
                if 0 <= U - 2 < NU * NB:
                    values(U - 2)

    @block.scalar
    def _(act):
        A_ = nc.scalar
        for b in range(NB):
            act.wait_ge(S["gg_ps"], b + 1)
            A_.activation(GG[:, b, :, :], ps_s[b % 2][:, 0:3 * D].rearrange("p (k d) -> p k d", d=D),
                          ACT.Copy).then_inc(S["gg"], 1)
        barrier(act, 4)

        def misc(kind, b):
            u = (kind, b)
            m = m_of(u)
            if kind == "hT":
                full(act, u)
                A_.activation(hT[:, :], m[:, :], ACT.Identity, bias=modT[:, 1, 0, b:b + 1],
                              scale=modT[:, 1, 1, b:b + 1]).then_inc(free(u), 1)
            elif kind[:2] == "qk":
                i = int(kind[2])
                t = NT * b + i
                full(act, u)
                if t >= 2:
                    act.wait_ge(S["var"], t - 1)
                A_.activation(sq[t % 2][:, :], m[:, 0:2 * D], ACT.Square).then_inc(S["sq"], 1)
                if i == 0 and b >= 2:
                    act.wait_ge(S["qkn"], b - 1)
                A_.activation(QK[b % 2][:, i, :], m[:, 0:2 * D], ACT.Copy).then_inc(S["qk_cp"], 1)
            elif kind == "kT":
                full(act, u)
                if b >= 1:
                    act.wait_ge(k_in[(b - 1) % 2], 16 * NH * ((b - 1) // 2 + 1))
                A_.activation(KT[:, :], m[:, :], ACT.Identity, bias=g.beta[:, 0:1], scale=g.gamma[:, 0:1]
                              ).then_inc(free(u), 1)
            elif kind == "qT":
                full(act, u)
                if b >= 2:
                    act.wait_ge(S["s_ps"], NU * (b - 1))
                A_.activation(QT[b % 2][:, :], m[:, :], ACT.Identity, bias=g.beta[:, 0:1], scale=g.gamma[:, 0:1]
                              ).then_inc(free(u), 1)
            elif kind == "yT":
                full(act, u)
                A_.activation(yT[:, :], m[:, :], ACT.Copy).then_inc(free(u), 1)
            elif kind == "gT":
                full(act, u)
                if b >= 1:
                    act.wait_ge(S["xm"], b)
                A_.activation(GT[:, 1:T + 1], m[:, :], ACT.Identity, bias=modT[:, 1, 3, b:b + 1],
                              scale=modT[:, 1, 4, b:b + 1]).then_inc(free(u), 1)
            elif kind == "ck":
                full(act, u)
                if b >= 1:
                    act.wait_ge(S["ka2"], b)
                A_.activation(KA[:, :], m[:, :], ACT.Relu).then_inc(free(u), 1)
            elif kind == "cr":
                full(act, u)
                if b >= 1:
                    evacuated(act, ("kv", b - 1))
                A_.activation(RT[:, :], m[:, :], ACT.Tanh, scale=0.5).then_inc(free(u), 1)

        for n in range(-LEAD1, NB + TAIL1):
            for u in range(NU):
                U = NU * n + u
                if 0 <= U < NU * NB:
                    act.wait_ge(S["sub"], U + 1)
                    if U >= 2:
                        act.wait_ge(S["t_ps"], U - 1)
                    A_.activation(PB[U % 2][:, :], SU[U % 2][:, :], ACT.Exp).then_inc(S["exp"], 1)
                for kind, o in MISC1.get(u, []):
                    if (kind, n + o) in M:
                        misc(kind, n + o)
                if 0 <= U - 1 < NU * NB:
                    act.wait_ge(S["t_ps"], U)
                    if U - 1 >= 2:
                        act.wait_ge(S["v_ps"], U - 2)
                    A_.activation(PT[(U - 1) % 2][:, :], ps_t[(U - 1) % 2][:, :], ACT.Copy).then_inc(S["pt"], 1)

    @block.vector
    def _(dve):
        V = nc.vector

        def lk(ins):
            link(dve, s_dve, ins)

        V.memset(KB[0][:, :, :], 0.0)
        for v in VB:
            lk(V.memset(v[:, :, :, :, :], 0.0))
            V.memset(v[0:64, :, :, :, DH:DV], 1.0)
            V.memset(v[64:P, :, :, :, DV + DH:2 * DV], 1.0)
        V.memset(GT[:, 0:1], 0.0)
        V.memset(nh32[:, :], -0.5)
        qk4 = wqk.rearrange("c (h d) -> c h d", d=DH)
        lk(V.tensor_reduce(gmean[:, :], qk4, AX_X, ALU.add))
        lk(V.scalar_tensor_tensor(qk4, bc(gmean[:, :].unsqueeze(2), [P, 2 * NH, DH]), -1.0 / DH, qk4, ALU.mult, ALU.add))
        V.tensor_scalar(m1[:, :], g.mu[:, :], -1.0, 1.0, ALU.mult, ALU.add)
        dve.wait_ge(S["wT_ps"], 1)
        V.tensor_copy(WT[:, :, :], ps_m[0][:, 0:3 * D].rearrange("p (k d) -> p k d", d=D)).then_inc(S["wT"], 1)
        dve.wait_ge(S["wT"], 1)
        dve.wait_ge(S["gg"], NB)
        V.scalar_tensor_tensor(WVG[:, :, :], bc(WT[:, 2:3, :], [P, NB, D]), 0.5, GG[:, :, 2, :], ALU.mult, ALU.mult)
        barrier(dve, 4)

        def norm_stats(src, st, m_, rdy):
            for i in range(NT):
                last = V.bn_stats(st[:, i, :], src[:, i, :])
            lk(last)
            for i in range(NT):
                last = V.bn_aggr(m_[:, i, :], st[:, i, :])
            last.then_inc(rdy, 1)

        def norm_apply(dst, src, m_, r_, rdy):
            for i in range(NT):
                last = V.tensor_scalar(dst[:, i, :], src[:, i, :], m_[:, i, 0:1], r_[:, i:i + 1],
                                       ALU.subtract, ALU.mult)
            last.then_inc(rdy, 1)

        def misc(kind, b):
            u = (kind, b)
            m = m_of(u)
            if kind[:2] == "qk":
                i = int(kind[2])
                t = NT * b + i
                full(dve, u)
                if b >= 3:
                    dve.wait_ge(S["v_ps"], NU * (b - 3) + 2 * i + 2)
                mv4 = m[:, 2 * D:3 * D].rearrange("p (w a d) -> p w a d", w=2, d=DH)
                dve.wait_ge(S["qk_cp"], t + 1)
                V.tensor_copy(VB[b % 3][0:64, i, :, :, 0:DH], mv4[0:64])
                V.tensor_copy(VB[b % 3][64:P, i, :, :, DV:DV + DH], mv4[64:P]).then_inc(free(u), 1)
                dve.wait_ge(S["sq"], t + 1)
                if i == 0 and b >= 2:
                    dve.wait_ge(S["rq"], NT * (b - 1))
                V.tensor_reduce(var[b % 2][:, i, :], sq[t % 2][:, :].rearrange("p (h d) -> p h d", d=DH), AX_X,
                                ALU.add).then_inc(S["var"], 1)
            elif kind == "pj":
                full(dve, u)
                dve.wait_ge(S["bp"], b + 1)
                Xb = X[:, NT * b:NT * b + NT, :]
                V.tensor_tensor(Xb, Xb, m[:, :].rearrange("p (i d) -> p i d", i=NT), ALU.add).then_inc(free(u), 1)
                evacuated(dve, u)
                norm_stats(Xb, stat2, mv2, S["mv2"])
            elif kind == "kv":
                full(dve, u)
                evacuated(dve, ("cr", b))
                if b >= 1:
                    dve.wait_ge(S["xo"], b)
                V.scalar_tensor_tensor(OU[:, :, :].rearrange("p i d -> p (i d)"), RT[:, :], 1.0, m[:, :], ALU.add,
                                       ALU.mult).then_inc(free(u), 1)

        for n in range(-LEAD1, NB + TAIL1):
            for u in range(NU):
                U = NU * n + u
                b = n + 1
                if 0 <= b < NB and u == 0:
                    dve.wait_ge(S["rq"], NT * (b + 1))
                    dve.wait_ge(S["qk_cp"], NT * (b + 1))
                    if b >= 1:
                        full(dve, ("kT", b - 1))
                        full(dve, ("qT", b - 1))
                    V.tensor_tensor(QKN[:, :, :].rearrange("p i (h d) -> p (i h) d", d=DH),
                                    QK[b % 2][:, :, :].rearrange("p i (h d) -> p (i h) d", d=DH),
                                    bc(rq[b % 2][:, :, :].rearrange("p i h -> p (i h)").unsqueeze(2),
                                       [P, NT * 2 * NH, DH]), ALU.mult).then_inc(S["qkn"], 1)
                if 0 <= U < NU * NB:
                    dve.wait_ge(S["s_ps"], U + 1)
                    s3 = ps_s[U % 2][:, :].rearrange("p (h s) -> p h s", h=HU)
                    V.tensor_reduce(mxs[U % 2][:, :], s3, AX_X, ALU.max).then_inc(S["max"], 1)
                    dve.wait_ge(S["max"], U + 1)
                    if U >= 2:
                        dve.wait_ge(S["exp"], U - 1)
                    V.tensor_tensor(SU[U % 2][:, :].rearrange("p (h s) -> p h s", h=HU), s3,
                                    bc(mxs[U % 2][:, :].unsqueeze(2), [P, HU, 512 // HU]),
                                    ALU.subtract).then_inc(S["sub"], 1)
                for kind, o in MISC1.get(u, []):
                    if (kind, n + o) in M:
                        misc(kind, n + o)
                W = U - 3
                if 0 <= W < NU * NB and W % 2 == 1:
                    tile = W // 2
                    i = tile % NT
                    dve.wait_ge(S["v_ps"], W + 1)
                    v3 = ps_v[tile % 2][:, 0:NH * DV].rearrange("p (h x) -> p h x", x=DV)
                    lk(V.reciprocal(rcp[:, tile % 2, :], v3[:, :, DH]))
                    if i == 0 and tile >= NT:
                        full(dve, ("yT", tile // NT - 1))
                    V.tensor_tensor(YN[:, i, :].rearrange("p (h d) -> p h d", d=DH), v3[:, :, 0:DH],
                                    bc(rcp[:, tile % 2, :].unsqueeze(2), [P, NH, DH]), ALU.mult).then_inc(S["yn"], 1)
                b = n - 1
                if 0 <= b < NB and u == 5:
                    dve.wait_ge(S["rs2"], b + 1)
                    if b >= 1:
                        full(dve, ("gT", b - 1))
                    norm_apply(xn2, X[:, NT * b:NT * b + NT, :], mv2, rs2, S["xn2"])
                if 0 <= b < NB and u == 7:
                    dve.wait_ge(S["t1"], b + 1)
                    if b >= 1:
                        full(dve, ("ck", b - 1))
                        full(dve, ("cr", b - 1))
                    V.scalar_tensor_tensor(xm[:, 0, :], GT[:, 0:T], m1[:, 0:1], t1[:, 0, :], ALU.mult, ALU.add)
                    V.scalar_tensor_tensor(xm[:, 1, :], GT[:, 0:T], m1[:, 1:2], t1[:, 1, :], ALU.mult,
                                           ALU.add).then_inc(S["xm"], 1)
                b = n + 3
                if 0 <= b < NB and u == 2:
                    Xb = X[:, NT * b:NT * b + NT, :]
                    dve.wait_ge(S["accg"], b + 1)
                    V.tensor_tensor(Xb, Xb, AC[:, :, :], ALU.add).then_inc(S["xadd"], 1)
                    dve.wait_ge(S["xadd"], b + 1)
                    norm_stats(Xb, stat, mv, S["mv"])
                if 0 <= b < NB and u == 5:
                    dve.wait_ge(S["rs"], b + 1)
                    if b >= 1:
                        full(dve, ("hT", b - 1))
                    norm_apply(xn, X[:, NT * b:NT * b + NT, :], mv, rs, S["xn"])

    @block.gpsimd
    def _(pool):
        G = nc.gpsimd

        def lk(ins):
            link(pool, s_pool, ins)

        G.memset(KB[1][:, :, :], 0.0)
        pool.wait_ge(S["gg"], NB)
        G.tensor_tensor(WPG[:, :, :], GG[:, :, 1, :], bc(g.w_proj[:, :].unsqueeze(1), [P, NB, D]), ALU.mult)
        G.tensor_tensor(BPG[:, :, :], GG[:, :, 1, :], bc(g.b_proj[:, :].unsqueeze(1), [P, NB, D]), ALU.mult)
        barrier(pool, 4)

        def rstd(ve_, m_, dst, rdy):
            lk(G.tensor_scalar(ve_[:, :], m_[:, :, 1], EPS, None, ALU.add))
            G.tensor_tensor(dst[:, :], ve_[:, :], g.neghalf[:, :], ALU.pow).then_inc(rdy, 1)

        for n in range(-LEAD1, NB + TAIL1):
            for u in range(NU):
                b = n + 3
                if 0 <= b < NB and u == 0:
                    pool.wait_ge(acc_in, 16 * (b + 1))
                    G.tensor_tensor(AC[:, :, :], AC[:, :, :], bc(GG[:, b, 0:1, :], [P, NT, D]), ALU.mult
                                    ).then_inc(S["accg"], 1)
                if 0 <= b < NB and u == 3:
                    pool.wait_ge(S["mv"], b + 1)
                    rstd(ve, mv, rs, S["rs"])
                if 0 <= b < NB and u == 7:
                    Xb = X[:, NT * b:NT * b + NT, :]
                    pool.wait_ge(S["xn"], b + 1)
                    G.tensor_tensor(Xb, Xb, bc(BPG[:, b:b + 1, :], [P, NT, D]), ALU.add).then_inc(S["bp"], 1)
                b = n + 2
                if 0 <= b < NB and 1 <= u <= 4:
                    i = u - 1
                    pool.wait_ge(S["var"], NT * b + i + 1)
                    if i == 0 and b >= 2:
                        pool.wait_ge(S["qkn"], b - 1)
                    lk(G.tensor_scalar(var[b % 2][:, i, :], var[b % 2][:, i, :], 1.0 / DH, EPS, ALU.mult, ALU.add))
                    G.tensor_tensor(rq[b % 2][:, i, :], var[b % 2][:, i, :], nh32[:, :], ALU.pow).then_inc(S["rq"], 1)
                b = n - 1
                if 0 <= b < NB and u == 4:
                    pool.wait_ge(S["mv2"], b + 1)
                    rstd(ve2, mv2, rs2, S["rs2"])
                if 0 <= b < NB and u == 6:
                    uu = ("gT", b)
                    evacuated(pool, uu)
                    if b >= 1:
                        pool.wait_ge(S["xm"], b)
                    G.tensor_scalar(t1[:, 0, :], GT[:, 1:T + 1], g.mu[:, 0:1], None, ALU.mult)
                    G.tensor_scalar(t1[:, 1, :], GT[:, 1:T + 1], g.mu[:, 1:2], None, ALU.mult).then_inc(S["t1"], 1)
                b = n - 2
                if 0 <= b < NB and u == 1:
                    uu = ("ck", b)
                    evacuated(pool, uu)
                    if b >= 1:
                        full(pool, ("kv", b - 1))
                    G.tensor_tensor(KA2[:, :], KA[:, :], KA[:, :], ALU.mult).then_inc(S["ka2"], 1)
                if 0 <= b < NB and u == 4:
                    uu = ("kv", b)
                    evacuated(pool, uu)
                    Xb = X[:, NT * b:NT * b + NT, :]
                    G.tensor_tensor(Xb, Xb, OU[:, :, :], ALU.add).then_inc(S["xo"], 1)

    @block.sync
    def _(sp):
        barrier(sp, 4)
        ov = out.rearrange("b (i p) d -> b p i d", p=P)
        for n in range(-LEAD1, NB + TAIL1):
            for u in range(NU):
                b = n + 3
                if 0 <= b < NB and u == 0:
                    if b >= 1:
                        sp.wait_ge(S["xadd"], b)
                    sp.dma_start(AC[:, :, :], g.d_acc[T * b:T * b + T, :].rearrange("(i p) d -> p i d", p=P)
                                 ).then_inc(acc_in, 16)
                b = n + 1
                if 0 <= b < NB and u == 3:
                    uu = ("kT", b)
                    evacuated(sp, uu)
                    if b >= 2:
                        sp.wait_ge(S["s_ps"], NU * (b - 1))
                    for h in range(NH):
                        sp.dma_start(KB[b % 2][DH * h:DH * h + DH, h, :], KT[DH * h:DH * h + DH, :]
                                     ).then_inc(k_in[b % 2], 16)
                b = n - 2
                if 0 <= b < NB and u == 5:
                    sp.wait_ge(S["xo"], b + 1)
                    sp.dma_start(ov[b], X[:, NT * b:NT * b + NT, :]).then_inc(o_st, 16)
        sp.wait_ge(o_st, 16 * NB)

    ph.close()


_INS = ["L0_attn_x", "L0_attn_Wc_down", "L0_attn_Wq_up", "L0_attn_Wkv_up", "L0_attn_Wc_proj", "L0_ffn_Wr", "L0_ffn_W1",
        "L0_ffn_b1", "L0_ffn_W2", "L0_ffn_b2", "L0_c", "L0_wmod", "L1_attn_W_qkv", "L1_attn_ln_gamma",
        "L1_attn_ln_beta", "L1_attn_W_proj", "L1_attn_b_proj", "L1_ffn_W_r", "L1_ffn_W_k", "L1_ffn_W_v",
        "L1_ffn_mu_r", "L1_ffn_mu_k", "L1_c", "L1_wmod"]


def kernel(**inputs):
    import numpy as np
    import concourse.bacc as bacc
    from concourse.bass_utils import run_bass_kernel_spmd

    nc = bacc.Bacc("TRN2", target_bir_lowering=False, num_devices=1)
    arrays, aps = {}, {}
    for name in _INS:
        a = np.ascontiguousarray(inputs[name])
        arrays[name] = a
        aps[name] = nc.dram_tensor(name, a.shape, mybir.dt.from_np(a.dtype), kind="ExternalInput").ap()
    out = nc.dram_tensor("y", (NB, T, D), F32, kind="ExternalOutput").ap()
    build(nc, aps, out)
    r = run_bass_kernel_spmd(nc, [arrays], core_ids=[0])
    return r.results[0]["y"]
```

```python
from contextlib import ExitStack

import concourse.bass as bass
from concourse import mybir

F32 = mybir.dt.float32
BF16 = mybir.dt.bfloat16
I32 = mybir.dt.int32
ALU = mybir.AluOpType
ACT = mybir.ActivationFunctionType
AX_X = mybir.AxisListType.X

P = 128
NB, T, D = 8, 512, 128
NT = T // P
NTILE = NB * NT
NH, DH = 16, 8
LAT = 64
NE, DI = 8, 512
CAP = 1024
NC_DI = DI // P
NS = CAP // P
ROW = D + NE
EPS = 1e-5
BIG = 1.0e30
PARTS = 3
NPR = PARTS * PARTS * DH
KR = 96
KM = KR + PARTS
QB = 3
NSTEP = 10
STEPS = [(g, i) for g in range(NT) for i in range(g + 1)]
DIGITS = 15
UNROLL = 5
NCH = 6


def max_groups():
    out = []
    for g in range(NT):
        per = 512 // (P * (g + 1))
        out += [(g, list(range(h, h + per))) for h in range(0, NH, per)]
    return out


GROUPS = max_groups()
NGRP = len(GROUPS)
HEAD_STEPS, BODY_STEPS = 1, 8
SLOTS = 4


def spread_groups():
    cost = [P * (g + 1) * len(hs) + 500 for g, hs in GROUPS]
    out = {(s, x): [] for s in range(NSTEP) for x in range(SLOTS)}
    n = (HEAD_STEPS + BODY_STEPS) * SLOTS
    acc = 0
    for k, c in enumerate(cost):
        s, x = divmod(min(int(acc / sum(cost) * n), n - 1), SLOTS)
        if s < HEAD_STEPS:
            out[NSTEP - HEAD_STEPS + s, x].append((2, k))
        else:
            out[s - HEAD_STEPS, x].append((1, k))
        acc += c
    return out


PLACES = spread_groups()
CHUNKS = [[k for x in range(SLOTS) for k in PLACES[s, x]] for s in range(NSTEP)]


class Shared:
    pass


class Misc:

    def __init__(self, order, banks):
        self.banks = banks
        self.index = {u: k for k, u in enumerate(order)}

    def __contains__(self, u):
        return u in self.index

    def bank(self, u):
        return self.index[u] % self.banks

    def full(self, u):
        return self.index[u] // self.banks + 1


MISC0 = {1: [("bc", -1)], 2: [("hT", 2)], 3: [("lat", 2)], 4: [("q", 2)], 5: [("k", 2)], 6: [("v", 2), ("h2", -2)],
         7: [("m", 1), ("lg", -2)], 8: [("pj", -1)]}
LEAD, TAIL = 2, 2
MIDDLE = 2


def misc_order(sched):
    return [(kind, n + o) for n in range(-LEAD, NB + TAIL) for s in range(NSTEP)
            for kind, o in sched.get(s, []) if 0 <= n + o < NB]


def build(nc, ins, out):
    ctx = ExitStack()
    with ctx:
        program(nc, ctx, ins, out)


def program(nc, ctx, ins, out):
    def sb(name, shape, dt=F32):
        return ctx.enter_context(nc.sbuf_tensor(name, shape, dt))

    def sem(name):
        return ctx.enter_context(nc.semaphore(name))

    mid = ExitStack()
    a0 = ExitStack()

    def sbm(name, shape, dt=F32):
        return mid.enter_context(nc.sbuf_tensor(name, shape, dt))

    def sb0(name, shape, dt=F32):
        return a0.enter_context(nc.sbuf_tensor(name, shape, dt))

    def dram(name, shape, dt):
        return nc.dram_tensor(name, shape, dt, kind="Internal").ap()

    d_q = [dram(f"d_q{i}", [PARTS, DH, NH, T], BF16) for i in range(2)]
    d_k = [dram(f"d_k{i}", [PARTS, DH, T], BF16) for i in range(2)]
    d_m = [dram(f"d_m{i}", [PARTS, 64, P], BF16) for i in range(2)]
    d_y = [dram(f"d_y{i}", [4, DH + 1, 4, T], F32) for i in range(2)]
    d_r = [dram(f"d_r{i}", [NH, T], F32) for i in range(2)]
    d_tab = dram("d_tab", [NB * T, ROW], F32)

    d_acc = dram("d_acc", [NB * T, D], F32)

    bank = [a0.enter_context(nc.psum_tensor(f"bank{i}", [P, 512], F32)) for i in range(4)]
    ps_s = [a0.enter_context(nc.psum_tensor(f"ps_s{i}", [P, 1024], F32)) for i in range(2)]
    ps_mx, ps_y, ps_misc = bank[0:2], bank[2], bank[3]

    X = sb("X", [P, NTILE, D])
    ident = sb("ident", [P, P])
    identb = sb("identb", [P, P], BF16)
    maskT = sb("maskT", [P, P], BF16)
    neghalf = sb("neghalf", [P, NT])
    onehot = sb("onehot", [NB, NB, P])
    modT = sb("modT", [P, 2, NCH, NB])
    modR = sb("modR", [NB, 2, NCH * D])
    zrow = sb("zrow", [P, D])
    biti = sb("biti", [P, DIGITS + 1, 3], I32)
    bitf = sb("bitf", [P, DIGITS])
    WT = sb("WT", [P, 3, D])
    GG = sb("GG", [P, NB, 3, D])
    WPG = sb("WPG", [P, NB, D])
    WVG = sb("WVG", [P, NB, D])
    BPG = sb("BPG", [P, NB, D])
    m1 = sb("m1", [P, 2])
    gmean = sb("gmean", [P, 2 * NH])
    w_qkv = sb("w_qkv", [P, 3 * D])
    w_proj = sb("w_proj", [P, D])
    b_proj = sb("b_proj", [P, D])
    w_cm = sb("w_cm", [P, 3, D])
    mu = sb("mu", [P, 2])
    gamma = sb("gamma", [P, 1])
    beta = sb("beta", [P, 1])
    SC = sbm("SC", [P, NE, NTILE])
    w1 = sbm("w1", [P, NE, DI])
    w2 = sbm("w2", [P, NE, NC_DI, D])
    b1T = sbm("b1T", [P, NE, NC_DI])
    cT = sb0("cT", [P, 2, NB])
    sT_e = sb0("sT_e", [P, 2, NB])
    siluT = sb0("siluT", [P, 2, NB])
    wmod = sb0("wmod", [P, 2, NCH * D])
    gtmp = sb0("gtmp", [NB, 2, 2, D])
    w_down = sb0("w_down", [P, LAT])
    w_q = sb0("w_q", [LAT, D])
    w_kv = sb0("w_kv", [LAT, 2 * DH])
    w_cp = sb0("w_cp", [P, D])
    w_r = sb0("w_r", [P, NE])
    Q = [sb0(f"Q{i}", [P, NH, T], BF16) for i in range(QB)]
    K = [sb0(f"K{i}", [P, T], BF16) for i in range(QB)]
    VE = [sb0(f"VE{i}", [P, NT, 32]) for i in range(QB)]
    PR = [sb0(f"PR{i}", [P, 4, 512]) for i in range(2)]
    MX = [sb0(f"MX{i}", [P, 64]) for i in range(2)]

    stat = sb0("stat", [P, NT, 6])
    mv = [sb0(f"mv{i}", [P, NT, 2]) for i in range(2)]
    ve = sb0("ve", [P, NT])
    rs = [sb0(f"rs{i}", [P, NT]) for i in range(2)]
    xn = sb0("xn", [P, NT, D])
    hT = sb0("hT", [P, T])
    latT = sb0("latT", [LAT, T])
    qs = sb0("qs", [P, PARTS, T], BF16)
    qr = sb0("qr", [P, T])
    ks = sb0("ks", [DH, PARTS, T], BF16)
    kr = sb0("kr", [DH, T])
    ms = sb0("ms", [64, PARTS, P], BF16)
    mr = sb0("mr", [64, P])
    ysb = [sb0(f"ysb{i}", [P, 512]) for i in range(2)]
    yt = sb0("yt", [P, T])
    lc = sb0("lc", [P, NH * T // P])
    rc = sb0("rc", [P, NH * T // P])
    rl = sb0("rl", [P, T])
    yn = sb0("yn", [P, T])
    wg = sb0("wg", [P, D])
    cbsb = [sb0(f"cbsb{i}", [P, 2, D]) for i in range(2)]
    stat2 = sb0("stat2", [P, NT, 6])
    mv2 = sb0("mv2", [P, NT, 2])
    ve2 = sb0("ve2", [P, NT])
    rs2 = sb0("rs2", [P, NT])
    xn2 = sb0("xn2", [P, NT, D])
    tab = sb0("tab", [P, NT, ROW])
    h2T = sb0("h2T", [P, T])
    lgm = sb0("lgm", [P, NT])
    lge = sb0("lge", [P, NT, NE])
    lgx = sb0("lgx", [P, NT, NE])
    lgs = sb0("lgs", [P, NT])
    lgr = sb0("lgr", [P, NT])

    s_x = [sem(f"x_loaded{b}") for b in range(NB)]
    s_w = sem("weights_loaded")
    s_qz = sem("queries_cleared")
    s_lw = sem("late_weights_loaded")
    s_phase = sem("phase_done")
    s_cst, s_cst2 = sem("consts_cleared"), sem("consts_ready")
    s_mod_e, s_silu, s_modps, s_modR = sem("mod_exp"), sem("silu_ready"), sem("mod_ps_full"), sem("mod_rows_done")
    names = ["sT_full", "exp_done", "pv_done", "mx_full", "red_done", "misc_full", "misc_free",
             "mv_rdy", "rs_rdy", "xn_rdy", "q1_rdy", "q2_rdy", "q3_rdy", "k1_rdy", "k2_rdy", "k3_rdy",
             "m_rdy", "y_ev", "rc_rdy", "yn_rdy", "cb_rdy", "mv2_rdy", "rs2_rdy", "xn2_rdy", "h2_rdy", "lgx_rdy", "tab_rdy"]
    S = {n: sem("a0_" + n) for n in names}
    dnames = ["q_st0", "q_st1", "k_st0", "k_st1", "q_in0", "q_in1", "m_st", "m_in0", "m_in1", "y_st0", "y_st1",
              "yt_in", "lc_in", "r_st", "rl_in", "tab_st"]
    DS = {n: sem("a0_" + n) for n in dnames}
    s_act, s_dve, s_pool = sem("act_chain"), sem("dve_chain"), sem("pool_chain")

    weights = [
        (cT[:, 0, :], ins["L0_c"].rearrange("b d -> d b")), (cT[:, 1, :], ins["L1_c"].rearrange("b d -> d b")),
        (wmod[:, 0, :], ins["L0_wmod"]), (wmod[:, 1, :], ins["L1_wmod"]),
        (w_down[:, :], ins["L0_attn_Wc_down"]), (w_q[:, :], ins["L0_attn_Wq_up"]), (w_kv[:, :], ins["L0_attn_Wkv_up"]),
        (w_cp[:, :], ins["L0_attn_Wc_proj"]), (w_r[:, :], ins["L0_ffn_Wr"]),
    ]
    N_W = len(weights)
    def per_head(name):
        return bass.AP(ins[name].tensor, 0, [[0, NH], [1, DH], [1, 1]])

    late_weights = [
        (w_qkv[:, :], ins["L1_attn_W_qkv"]), (w_proj[:, :], ins["L1_attn_W_proj"]),
        (b_proj[:, :], bass.AP(ins["L1_attn_b_proj"].tensor, 0, [[0, P], [1, D]])),
        (w_cm[:, 0, :], ins["L1_ffn_W_r"]), (w_cm[:, 1, :], ins["L1_ffn_W_k"]), (w_cm[:, 2, :], ins["L1_ffn_W_v"]),
        (mu[:, 0:1], ins["L1_ffn_mu_r"].rearrange("(p o) -> p o", o=1)),
        (mu[:, 1:2], ins["L1_ffn_mu_k"].rearrange("(p o) -> p o", o=1)),
        (gamma[:, :], per_head("L1_attn_ln_gamma")), (beta[:, :], per_head("L1_attn_ln_beta")),
        (w1[:, :, :], ins["L0_ffn_W1"].rearrange("e d f -> d e f")),
        (b1T[:, :, :], ins["L0_ffn_b1"].rearrange("e (c p) -> p e c", p=P)),
    ] + [(w2[:, e, :, :], ins["L0_ffn_W2"][e].rearrange("(c p) d -> p c d", p=P)) for e in range(NE)]

    block = a0.enter_context(nc.Block())
    M0 = Misc(misc_order(MISC0), 1)
    chains = {}

    def link(eng, s, ins):
        chains[id(s)] = chains.get(id(s), 0) + 1
        ins.then_inc(s, 1)
        eng.wait_ge(s, chains[id(s)])

    def barrier(eng, k):
        eng.drain().then_inc(s_phase, 1)
        eng.wait_ge(s_phase, 5 * k)

    def bc(ap, shape):
        return ap.to_broadcast(shape)

    @block.tensor
    def _(pe):
        pe.wait_ge(s_w, 16 * N_W)
        pe.wait_ge(s_silu, 1)
        for l in range(2):
            for c in range(NCH):
                last = nc.tensor.matmul(ps_misc[:, (l * NCH + c) * NB:(l * NCH + c + 1) * NB],
                                        wmod[:, l, c * D:(c + 1) * D], siluT[:, l, :], start=True, stop=True)
        last.then_inc(s_modps, 1)
        barrier(pe, 1)
        for l in range(2):
            for h in range(2):
                last = nc.tensor.matmul(ps_s[l][0:NB, h * 512:h * 512 + 384], siluT[:, l, :],
                                        wmod[:, l, h * 384:(h + 1) * 384], start=True, stop=True)
        last.then_inc(s_modps, 1)

        def acquire(u):
            if M0.index[u] >= 1:
                pe.wait_ge(S["misc_free"], M0.index[u])

        def scores_T(b, s, half):
            g, i = STEPS[s]
            if b == 0 and s == 0 and half == 0:
                pe.wait_ge(s_modR, 2)
            if s == 0 and half == 0:
                pe.wait_ge(DS[f"m_in{b % 2}"], 48 * (b // 2 + 1))
            t2 = 2 * (NSTEP * b + s) + half
            if t2 >= 2:
                pe.wait_ge(S["exp_done"], t2 - 1)
            for hh in range(2):
                hg = 2 * half + hh
                last = nc.tensor.matmul(ps_s[half][:, 512 * hh:512 * hh + 512], K[b % QB][0:KM, P * i:P * i + P],
                                        Q[b % QB][0:KM, 4 * hg:4 * hg + 4, P * g:P * g + P],
                                        start=True, stop=(i < g))
            if i == g:
                for hh in range(2):
                    last = nc.tensor.matmul(ps_s[half][:, 512 * hh:512 * hh + 512], maskT[:, :],
                                            bc(identb[:, :].unsqueeze(1), [P, 4, P]), start=False, stop=True)
            last.then_inc(S["sT_full"], 1)

        def values(t):
            b, s = divmod(t, NSTEP)
            g, i = STEPS[s]
            pe.wait_ge(S["exp_done"], 2 * t + 2)
            if s == 0:
                pe.wait_ge(S["misc_free"], M0.full(("v", b)))
            if i == 0 and NT * b + g >= 1:
                pe.wait_ge(S["y_ev"], NT * b + g)
            for j in range(4):
                last = nc.tensor.matmul(ps_y[32 * j:32 * j + 32, :], VE[b % QB][:, i, :], PR[t % 2][:, j, :],
                                        start=(i == 0), stop=(i == g), tile_position=(0, 32 * j))
            last.then_inc(S["pv_done"], 1)

        def maxima(n, groups):
            for o, k in groups:
                b = n + o
                if not 0 <= b < NB:
                    continue
                g, hs = GROUPS[k]
                G = NGRP * b + k
                w = P * (g + 1)
                if k == 0:
                    pe.wait_ge(DS[f"q_in{b % 2}"], 64 * (b // 2 + 1))
                if G >= 2:
                    pe.wait_ge(S["red_done"], G - 1)
                for x, h in enumerate(hs):
                    nc.tensor.matmul(ps_mx[G % 2][:, x * w:(x + 1) * w], Q[b % QB][0:KR, h, P * g:P * g + P],
                                     K[b % QB][0:KR, 0:w], start=(x == 0), stop=False, skip_group_check=True)
                diag = ps_mx[G % 2][:, 0:len(hs) * w].rearrange("p (x w) -> p x w", w=w)[:, :, w - P:w]
                nc.tensor.matmul(diag, identb[:, :], bc(maskT[:, :].unsqueeze(1), [P, len(hs), P]),
                                 start=False, stop=True, skip_group_check=True).then_inc(S["mx_full"], 1)

        def misc(kind, b):
            acquire((kind, b))
            m = ps_misc
            if kind == "hT":
                pe.wait_ge(S["xn_rdy"], b + 1)
                for i in range(NT):
                    last = nc.tensor.transpose(m[:, P * i:P * i + P], xn[:, i, :], ident[:, :])
            elif kind == "lat":
                last = nc.tensor.matmul(m[0:LAT, :], w_down[:, :], hT[:, :], start=True, stop=True)
            elif kind == "q":
                last = nc.tensor.matmul(m[:, :], w_q[:, :], latT[:, :], start=True, stop=True)
            elif kind == "k":
                last = nc.tensor.matmul(m[0:DH, :], w_kv[:, 0:DH], latT[:, :], start=True, stop=True)
            elif kind == "v":
                for i in range(NT):
                    last = nc.tensor.matmul(m[:, DH * i:DH * i + DH], latT[:, P * i:P * i + P], w_kv[:, DH:2 * DH],
                                            start=True, stop=True)
            elif kind == "m":
                pe.wait_ge(S["red_done"], NGRP * (b + 1))
                last = nc.tensor.transpose(m[0:64, 0:P], MX[b % 2][:, :], ident[:, :])
            elif kind == "bc":
                pe.wait_ge(s_modR, 2)
                last = nc.tensor.matmul(m[:, 0:384], onehot[:, b, :], modR[:, 0, 2 * D:5 * D], start=True, stop=True)
            elif kind == "pj":
                pe.wait_ge(S["yn_rdy"], b + 1)
                for i in range(NT):
                    last = nc.tensor.matmul(m[:, P * i:P * i + P], yn[:, P * i:P * i + P], wg[:, :],
                                            start=True, stop=True)
            elif kind == "h2":
                pe.wait_ge(S["h2_rdy"], b + 1)
                for i in range(NT):
                    last = nc.tensor.transpose(m[:, P * i:P * i + P], tab[:, i, 0:D], ident[:, :])
            elif kind == "lg":
                for i in range(NT):
                    last = nc.tensor.matmul(m[:, NE * i:NE * i + NE], h2T[:, P * i:P * i + P], w_r[:, :],
                                            start=True, stop=True)
            last.then_inc(S["misc_full"], 1)

        for n in range(-LEAD, NB + TAIL):
            for s in range(NSTEP):
                t = NSTEP * n + s - 1
                for x in range(SLOTS):
                    if x < 2 and 0 <= n < NB:
                        scores_T(n, s, x)
                    if x == 2 and 0 <= t < NSTEP * NB:
                        values(t)
                    maxima(n, PLACES[s, x])
                    if x == MIDDLE:
                        uses = [u for u in MISC0.get(s, []) if (u[0], n + u[1]) in M0]
                        early = 1 if uses and uses[0][0] != "m" else 0
                        for kind, o in uses[:early]:
                            misc(kind, n + o)
                for kind, o in uses[early:]:
                    misc(kind, n + o)
        barrier(pe, 2)

    @block.scalar
    def _(act):
        act.wait_ge(s_w, 16 * N_W)
        nc.scalar.activation(sT_e[:, :, :], cT[:, :, :], ACT.Exp, scale=-1.0).then_inc(s_mod_e, 1)
        barrier(act, 1)

        def full(u):
            act.wait_ge(S["misc_full"], M0.full(u))

        def misc(kind, b):
            m = ps_misc
            if kind == "hT":
                full((kind, b))
                nc.scalar.activation(hT[:, :], m[:, :], ACT.Identity, bias=modT[:, 0, 0, b:b + 1],
                                     scale=modT[:, 0, 1, b:b + 1]).then_inc(S["misc_free"], 1)
            elif kind == "lat":
                full((kind, b))
                nc.scalar.activation(latT[:, :], m[0:LAT, :], ACT.Copy).then_inc(S["misc_free"], 1)
            elif kind == "q":
                full((kind, b))
                if b >= 1:
                    act.wait_ge(DS[f"q_st{(b - 1) % 2}"], 16 * PARTS * ((b - 1) // 2 + 1))
                nc.scalar.activation(qs[:, 0, :], m[:, :], ACT.Copy).then_inc(S["q1_rdy"], 1)
            elif kind == "k":
                full((kind, b))
                if b >= 1:
                    act.wait_ge(DS[f"k_st{(b - 1) % 2}"], 16 * ((b - 1) // 2 + 1))
                nc.scalar.activation(ks[:, 0, :], m[0:DH, :], ACT.Copy).then_inc(S["k1_rdy"], 1)
            elif kind == "bc":
                full((kind, b))
                if b >= 2:
                    act.wait_ge(S["h2_rdy"], b - 1)
                nc.scalar.activation(cbsb[b % 2][:, :, :], m[:, D:3 * D].rearrange("p (a d) -> p a d", a=2),
                                     ACT.Copy).then_inc(S["cb_rdy"], 1)
            elif kind == "h2":
                full((kind, b))
                nc.scalar.activation(h2T[:, :], m[:, :], ACT.Copy).then_inc(S["misc_free"], 1)

        def y_out(Y):
            b, g = divmod(Y, NT)
            act.wait_ge(S["pv_done"], NSTEP * b + STEPS.index((g, g)) + 1)
            if Y >= 2:
                act.wait_ge(DS[f"y_st{Y % 2}"], 64 * (Y // 2))
            nc.scalar.activation(ysb[Y % 2][:, :], ps_y[:, :], ACT.Copy).then_inc(S["y_ev"], 1)

        for n in range(-LEAD, NB + TAIL):
            for s in range(NSTEP):
                t = NSTEP * n + s
                if 0 <= n < NB:
                    for half in range(2):
                        act.wait_ge(S["sT_full"], 2 * t + half + 1)
                        if t >= 2:
                            act.wait_ge(S["pv_done"], t - 1)
                        nc.scalar.activation(PR[t % 2][:, 2 * half:2 * half + 2, :],
                                             ps_s[half][:, :].rearrange("p (a f) -> p a f", a=2), ACT.Exp,
                                             scale=DH ** -0.5).then_inc(S["exp_done"], 1)
                if 0 <= t - 1 < NSTEP * NB:
                    b, ps = divmod(t - 1, NSTEP)
                    g, i = STEPS[ps]
                    if g == i:
                        y_out(NT * b + g)
                for kind, o in MISC0.get(s, []):
                    if (kind, n + o) in M0:
                        misc(kind, n + o)
                if s == 8 and 0 <= n - 2 < NB:
                    b = n - 2
                    act.wait_ge(S["misc_free"], M0.full(("lg", b)))
                    nc.scalar.activation(lgx[:, :, :], lge[:, :, :], ACT.Exp).then_inc(S["lgx_rdy"], 1)
        barrier(act, 2)

    @block.vector
    def _(dve):
        def lk(ins):
            link(dve, s_dve, ins)

        nc.vector.memset(neghalf[:, :], -0.5)
        nc.vector.memset(zrow[:, :], 0.0)
        for v in VE:
            nc.vector.memset(v[:, :, :], 0.0)
        lk(nc.vector.memset(K[0][:, :].bitcast(F32), 0.0))
        for k in K[1:]:
            lk(nc.vector.memset(k[:, :].bitcast(F32), 0.0))
        for v in VE:
            nc.vector.memset(v[:, :, DH:DH + 1], 1.0)
        for k in K:
            lk(nc.vector.memset(k[KR:KM, :], -1.0))
        dve.wait_ge(s_mod_e, 1)
        lk(nc.vector.tensor_scalar_add(sT_e[:, :, :], sT_e[:, :, :], 1.0))
        lk(nc.vector.reciprocal(siluT[:, :, :], sT_e[:, :, :]))
        nc.vector.tensor_tensor(siluT[:, :, :], siluT[:, :, :], cT[:, :, :], ALU.mult).then_inc(s_silu, 1)
        dve.wait_ge(s_modps, 1)
        lk(nc.vector.tensor_copy(modT[:, :, :, :].rearrange("p l c b -> p (l c b)"), ps_misc[:, 0:2 * NCH * NB]))
        for c in (1, 4):
            lk(nc.vector.tensor_scalar_add(modT[:, :, c, :], modT[:, :, c, :], 1.0))
        barrier(dve, 1)

        def modulation_rows():
            dve.wait_ge(s_modps, 2)
            for l in range(2):
                lk(nc.vector.tensor_copy(modR[:, l, :].rearrange("b (h f) -> b h f", h=2),
                                         ps_s[l][0:NB, :].rearrange("b (h f) -> b h f", h=2)[:, :, 0:384]))
            gates = modR[:, :, :].rearrange("b l (h r) -> b l h r", h=2)[:, :, :, 2 * D:3 * D]
            for l in range(2):
                lk(nc.vector.tensor_scalar(gtmp[:, l, :, :], gates[:, l, :, :], 0.0, 2.0, ALU.is_ge, ALU.mult))
                lk(nc.vector.scalar_tensor_tensor(gates[:, l, :, :], gtmp[:, l, :, :], -1.0, gates[:, l, :, :],
                                                  ALU.add, ALU.mult))
                lk(nc.vector.tensor_scalar(gates[:, l, :, :], gates[:, l, :, :], 0.25, None, ALU.max))
                lk(nc.vector.scalar_tensor_tensor(gates[:, l, :, :], gtmp[:, l, :, :], -1.0, gates[:, l, :, :],
                                                  ALU.add, ALU.mult))
                nc.vector.tensor_scalar_add(modR[:, l, 4 * D:5 * D], modR[:, l, 4 * D:5 * D], 1.0).then_inc(s_modR, 1)

        def full(u):
            dve.wait_ge(S["misc_full"], M0.full(u))

        def free(u):
            dve.wait_ge(S["misc_free"], M0.full(u))

        def norm_stats(src, st, m_, rdy):
            for i in range(NT):
                last = nc.vector.bn_stats(st[:, i, :], src[:, i, :])
            lk(last)
            for i in range(NT):
                last = nc.vector.bn_aggr(m_[:, i, :], st[:, i, :])
            last.then_inc(rdy, 1)

        def misc(kind, b):
            m = ps_misc
            if kind == "q":
                dve.wait_ge(S["q1_rdy"], b + 1)
                if b >= 1:
                    dve.wait_ge(S["q3_rdy"], b)
                nc.vector.tensor_tensor(qr[:, :], m[:, :], qs[:, 0, :], ALU.subtract).then_inc(S["misc_free"], 1)
                free((kind, b))
                nc.vector.tensor_copy(qs[:, 1, :], qr[:, :]).then_inc(S["q2_rdy"], 1)
            elif kind == "k":
                dve.wait_ge(S["k1_rdy"], b + 1)
                if b >= 1:
                    dve.wait_ge(S["k3_rdy"], b)
                nc.vector.tensor_tensor(kr[:, :], m[0:DH, :], ks[:, 0, :], ALU.subtract).then_inc(S["misc_free"], 1)
                free((kind, b))
                nc.vector.tensor_copy(ks[:, 1, :], kr[:, :]).then_inc(S["k2_rdy"], 1)
            elif kind == "v":
                full((kind, b))
                nc.vector.tensor_copy(VE[b % QB][:, :, 0:DH],
                                      m[:, 0:NT * DH].rearrange("p (i d) -> p i d", d=DH)).then_inc(S["misc_free"], 1)
            elif kind == "m":
                full((kind, b))
                if b >= 1:
                    dve.wait_ge(DS["m_st"], 16 * b)
                lk(nc.vector.tensor_copy(ms[:, 0, :], m[0:64, 0:P]))
                nc.vector.tensor_tensor(mr[:, :], m[0:64, 0:P], ms[:, 0, :], ALU.subtract).then_inc(S["misc_free"], 1)
                free((kind, b))
                lk(nc.vector.tensor_copy(ms[:, 1, :], mr[:, :]))
                nc.vector.tensor_tensor(ms[:, 2, :], mr[:, :], ms[:, 1, :], ALU.subtract).then_inc(S["m_rdy"], 1)
            elif kind == "bc":
                dve.wait_ge(S["cb_rdy"], b + 1)
                nc.vector.tensor_tensor(wg[:, :], m[:, 0:D], w_cp[:, :], ALU.mult).then_inc(S["misc_free"], 1)
            elif kind == "pj":
                full((kind, b))
                nc.vector.tensor_tensor(X[:, NT * b:NT * b + NT, :], X[:, NT * b:NT * b + NT, :],
                                        m[:, :].rearrange("p (i d) -> p i d", i=NT), ALU.add).then_inc(S["misc_free"], 1)
            elif kind == "lg":
                full((kind, b))
                lg = m[:, 0:NT * NE].rearrange("p (i e) -> p i e", i=NT)
                lk(nc.vector.tensor_reduce(lgm[:, :], lg, AX_X, ALU.max))
                if b >= 1:
                    dve.wait_ge(S["lgx_rdy"], b)
                nc.vector.tensor_tensor(lge[:, :, :], lg, bc(lgm[:, :].unsqueeze(2), [P, NT, NE]),
                                        ALU.subtract).then_inc(S["misc_free"], 1)

        for n in range(-LEAD, NB + TAIL):
            for s in range(NSTEP):
                for o, k in CHUNKS[s]:
                    b = n + o
                    if 0 <= b < NB:
                        g, hs = GROUPS[k]
                        G = NGRP * b + k
                        w = P * (g + 1)
                        dve.wait_ge(S["mx_full"], G + 1)
                        if k == 0 and b >= 2:
                            dve.wait_ge(S["misc_full"], M0.full(("m", b - 2)))
                        c = NH * g + hs[0]
                        nc.vector.tensor_reduce(MX[b % 2][:, c:c + len(hs)],
                                                ps_mx[G % 2][:, 0:len(hs) * w].rearrange("p (x w) -> p x w", w=w),
                                                AX_X, ALU.max).then_inc(S["red_done"], 1)
                b = n + 2
                if 0 <= b < NB and s == 0:
                    dve.wait_ge(s_x[b], 16)
                    norm_stats(X[:, NT * b:NT * b + NT, :], stat, mv[b % 2], S["mv_rdy"])
                    if b == 0:
                        modulation_rows()
                b = n - 2
                if 0 <= b < NB and s == 0:
                    dve.wait_ge(S["misc_free"], M0.full(("pj", b)))
                    if b >= 1:
                        dve.wait_ge(S["xn2_rdy"], b)
                    norm_stats(X[:, NT * b:NT * b + NT, :], stat2, mv2, S["mv2_rdy"])
                b = n - 1
                if 0 <= b < NB and s == 3:
                    dve.wait_ge(DS["lc_in"], 16 * (b + 1))
                    if b >= 1:
                        dve.wait_ge(DS["r_st"], 16 * b)
                    nc.vector.reciprocal(rc[:, :], lc[:, :]).then_inc(S["rc_rdy"], 1)
                for kind, o in MISC0.get(s, []):
                    if (kind, n + o) in M0:
                        misc(kind, n + o)
                b = n - 2
                if 0 <= b < NB and s == 9:
                    dve.wait_ge(S["lgx_rdy"], b + 1)
                    lk(nc.vector.tensor_reduce(lgs[:, :], lgx[:, :, :], AX_X, ALU.add))
                    lk(nc.vector.reciprocal(lgr[:, :], lgs[:, :]))
                    if b >= 1:
                        dve.wait_ge(DS["tab_st"], 16 * b)
                    lk(nc.vector.tensor_tensor(tab[:, :, D:ROW], lgx[:, :, :], bc(lgr[:, :].unsqueeze(2), [P, NT, NE]),
                                               ALU.mult))
                    nc.vector.tensor_copy(SC[:, :, NT * b:NT * b + NT].rearrange("p e i -> p i e"),
                                          tab[:, :, D:ROW]).then_inc(S["tab_rdy"], 1)
        barrier(dve, 2)

    @block.gpsimd
    def _(pool):
        def lk(ins):
            link(pool, s_pool, ins)

        lk(nc.gpsimd.memset(ident[:, :], 0.0))
        lk(nc.gpsimd.affine_select(out=ident[:, :], in_=ident[:, :], compare_op=ALU.not_equal, fill=1.0, base=0,
                                   pattern=[[-1, P]], channel_multiplier=1))
        lk(nc.gpsimd.memset(identb[:, :], 0.0))
        lk(nc.gpsimd.affine_select(out=identb[:, :], in_=identb[:, :], compare_op=ALU.not_equal, fill=1.0, base=0,
                                   pattern=[[-1, P]], channel_multiplier=1))
        lk(nc.gpsimd.memset(maskT[:, :], 0.0))
        lk(nc.gpsimd.affine_select(out=maskT[:, :], in_=maskT[:, :], compare_op=ALU.is_ge, fill=-BIG, base=0,
                                   pattern=[[-1, P]], channel_multiplier=1))
        lk(nc.gpsimd.memset(onehot[:, :, :], 0.0))
        lk(nc.gpsimd.affine_select(out=onehot[:, :, :], in_=onehot[:, :, :], compare_op=ALU.not_equal, fill=1.0,
                                   base=0, pattern=[[-1, NB], [0, P]], channel_multiplier=1))
        def clear(q):
            return nc.gpsimd.memset(q[:, :, :].rearrange("r h q -> r (h q)").bitcast(F32), 0.0)

        clear(Q[0])
        barrier(pool, 1)
        def norm_apply(dst, src, m_, r_, rdy):
            for i in range(NT):
                last = nc.gpsimd.tensor_scalar(dst[:, i, :], src[:, i, :], m_[:, i, 0:1], r_[:, i:i + 1],
                                               ALU.subtract, ALU.mult)
            last.then_inc(rdy, 1)

        for n in range(-LEAD, NB + TAIL):
            for s in range(NSTEP):
                b = n + 2
                if 0 <= b < NB and s == 0:
                    pool.wait_ge(S["mv_rdy"], b + 1)
                    lk(nc.gpsimd.tensor_scalar(ve[:, :], mv[b % 2][:, :, 1], EPS, None, ALU.add))
                    nc.gpsimd.tensor_tensor(rs[b % 2][:, :], ve[:, :], neghalf[:, :], ALU.pow).then_inc(S["rs_rdy"], 1)
                    pool.wait_ge(S["rs_rdy"], b + 1)
                    if b >= 1:
                        pool.wait_ge(S["misc_full"], M0.full(("hT", b - 1)))
                    norm_apply(xn, X[:, NT * b:NT * b + NT, :], mv[b % 2], rs[b % 2], S["xn_rdy"])
                    if b == 0:
                        for q in Q[1:]:
                            clear(q).then_inc(s_qz, 1)
                if 0 <= b < NB and s == 4:
                    pool.wait_ge(S["q2_rdy"], b + 1)
                    nc.gpsimd.tensor_tensor(qs[:, 2, :], qr[:, :], qs[:, 1, :], ALU.subtract).then_inc(S["q3_rdy"], 1)
                if 0 <= b < NB and s == 6:
                    pool.wait_ge(S["k2_rdy"], b + 1)
                    nc.gpsimd.tensor_tensor(ks[:, 2, :], kr[:, :], ks[:, 1, :], ALU.subtract).then_inc(S["k3_rdy"], 1)
                b = n - 2
                if 0 <= b < NB and s == 0:
                    pool.wait_ge(S["mv2_rdy"], b + 1)
                    lk(nc.gpsimd.tensor_scalar(ve2[:, :], mv2[:, :, 1], EPS, None, ALU.add))
                    nc.gpsimd.tensor_tensor(rs2[:, :], ve2[:, :], neghalf[:, :], ALU.pow).then_inc(S["rs2_rdy"], 1)
                    pool.wait_ge(S["rs2_rdy"], b + 1)
                    if b >= 1:
                        pool.wait_ge(S["h2_rdy"], b)
                    norm_apply(xn2, X[:, NT * b:NT * b + NT, :], mv2, rs2, S["xn2_rdy"])
                if 0 <= b < NB and s == 3:
                    pool.wait_ge(S["xn2_rdy"], b + 1)
                    pool.wait_ge(S["cb_rdy"], b + 1)
                    if b >= 1:
                        pool.wait_ge(DS["tab_st"], 16 * b)
                        pool.wait_ge(S["misc_full"], M0.full(("h2", b - 1)))
                    h = tab[:, :, 0:D]
                    lk(nc.gpsimd.tensor_tensor(h, xn2[:, :, :], bc(cbsb[b % 2][:, 1:2, :], [P, NT, D]), ALU.mult))
                    nc.gpsimd.tensor_tensor(h, h, bc(cbsb[b % 2][:, 0:1, :], [P, NT, D]),
                                            ALU.add).then_inc(S["h2_rdy"], 1)
                b = n - 1
                if 0 <= b < NB and s == 6:
                    pool.wait_ge(DS["yt_in"], 64 * (b + 1))
                    pool.wait_ge(DS["rl_in"], 16 * (b + 1))
                    if b >= 1:
                        pool.wait_ge(S["misc_full"], M0.full(("pj", b - 1)))
                    nc.gpsimd.tensor_tensor(yn[:, :], yt[:, :], rl[:, :], ALU.mult).then_inc(S["yn_rdy"], 1)
        nc.gpsimd.memset(biti[:, DIGITS, :], 0)
        for r in range(DIGITS):
            place = 1 << (2 * (DIGITS - 1 - r))
            for k in range(3):
                nc.gpsimd.memset(biti[:, r, k:k + 1], (k + 1) * place)
            nc.gpsimd.memset(bitf[:, r:r + 1], float(place))
        barrier(pool, 2)

    @block.sync
    def _(sp):
        for dst, src in weights:
            sp.dma_start(dst, src, allow_slow_non_contiguous=True).then_inc(s_w, 16)
        xv = ins["L0_attn_x"].rearrange("b (i p) d -> b p i d", p=P)
        for b in range(NB):
            sp.dma_start(X[:, NT * b:NT * b + NT, :], xv[b]).then_inc(s_x[b], 16)
        barrier(sp, 1)

        def y_store(Y):
            b, g = divmod(Y, NT)
            sp.wait_ge(S["y_ev"], Y + 1)
            if g == 0 and b >= 2:
                sp.wait_ge(DS["yt_in"], 64 * (b - 1))
                sp.wait_ge(DS["lc_in"], 16 * (b - 1))
            for j in range(4):
                sp.dma_start(d_y[b % 2][j][:, :, P * g:P * g + P],
                             ysb[Y % 2][32 * j:32 * j + DH + 1, :].rearrange("p (h q) -> p h q", q=P)
                             ).then_inc(DS[f"y_st{Y % 2}"], 16)

        for n in range(-LEAD, NB + TAIL):
            for s in range(NSTEP):
                t = NSTEP * n + s
                if 0 <= t - 1 < NSTEP * NB:
                    b, ps = divmod(t - 1, NSTEP)
                    g, i = STEPS[ps]
                    if g == i:
                        y_store(NT * b + g)
                b = n - 1
                if 0 <= b < NB and s == 0:
                    for par in range(2):
                        sp.wait_ge(DS[f"y_st{par}"], 64 * 2 * (b + 1))
                    if b >= 1:
                        sp.wait_ge(S["rc_rdy"], b)
                        sp.wait_ge(S["yn_rdy"], b)
                    y = d_y[b % 2]
                    sp.dma_start(lc[:, :], bass.AP(y.tensor, DH * 4 * T, [[(DH + 1) * 4 * T, 4], [64, 32], [1, 64]])
                                 ).then_inc(DS["lc_in"], 16)
                    for j in range(4):
                        sp.dma_start(yt[32 * j:32 * j + 32, :],
                                     bass.AP(y.tensor, j * (DH + 1) * 4 * T, [[T, 4], [4 * T, DH], [1, T]])
                                     ).then_inc(DS["yt_in"], 16)
                if 0 <= b < NB and s == 4:
                    sp.wait_ge(S["rc_rdy"], b + 1)
                    if b >= 2:
                        sp.wait_ge(DS["rl_in"], 16 * (b - 1))
                    r = d_r[b % 2]
                    sp.dma_start(r.rearrange("h (a q) -> (h a) q", q=64), rc[:, :]).then_inc(DS["r_st"], 16)
                    sp.wait_ge(DS["r_st"], 16 * (b + 1))
                    sp.dma_start(rl[:, :], bass.AP(r.tensor, 0, [[T, NH], [0, DH], [1, T]])).then_inc(DS["rl_in"], 16)
                b = n + 2
                if 0 <= b < NB and s == 5:
                    par = b % 2
                    if b == 1:
                        sp.wait_ge(s_qz, QB - 1)
                    sp.wait_ge(S["q3_rdy"], b + 1)
                    if b >= 2:
                        sp.wait_ge(DS[f"q_in{par}"], 64 * (b // 2))
                    for a in range(PARTS):
                        sp.dma_start(bass.AP(d_q[par].tensor, a * D * T, [[T, NH], [NH * T, DH], [1, T]]),
                                     qs[:, a, :]).then_inc(DS[f"q_st{par}"], 16)
                    sp.wait_ge(DS[f"q_st{par}"], 48 * (b // 2 + 1))
                    sp.dma_start(Q[b % QB][0:NPR].rearrange("r h q -> r (h q)"),
                                 bass.AP(d_q[par].tensor, 0, [[0, PARTS], [NH * T, PARTS * DH], [1, NH * T]])
                                 ).then_inc(DS[f"q_in{par}"], 16)
                if 0 <= b < NB and s == 6:
                    par = b % 2
                    sp.wait_ge(S["k3_rdy"], b + 1)
                    sp.dma_start(bass.AP(d_k[par].tensor, 0, [[T, DH], [DH * T, PARTS], [1, T]]),
                                 ks[:, :, :]).then_inc(DS[f"k_st{par}"], 16)
                    sp.wait_ge(DS[f"k_st{par}"], 16 * (b // 2 + 1))
                    for c in range(PARTS):
                        sp.dma_start(K[b % QB][24 * c:24 * c + 24, :],
                                     bass.AP(d_k[par].tensor, c * DH * T, [[0, PARTS], [T, DH], [1, T]])
                                     ).then_inc(DS[f"q_in{par}"], 16)
                b = n + 1
                if 0 <= b < NB and s == 7:
                    par = b % 2
                    sp.wait_ge(S["m_rdy"], b + 1)
                    if b >= 2:
                        sp.wait_ge(DS[f"m_in{par}"], 48 * (b // 2))
                    sp.dma_start(d_m[par].rearrange("a g f -> g a f"), ms[:, :, :]).then_inc(DS["m_st"], 16)
                    sp.wait_ge(DS["m_st"], 16 * (b + 1))
                    for a in range(PARTS):
                        sp.dma_start(Q[b % QB][KR + a:KR + a + 1, :, :],
                                     bass.AP(d_m[par].tensor, a * 64 * P, [[P, NH], [NH * P, NT], [1, P]])
                                     ).then_inc(DS[f"m_in{par}"], 16)
                if 0 <= n < NB and s == 9:
                    for dst, src in late_weights[n::NB]:
                        sp.dma_start(dst, src, allow_slow_non_contiguous=True).then_inc(s_lw, 16)
                    if n == 0:
                        sp.dma_start(d_acc.rearrange("(i p) d -> p i d", p=P),
                                     bc(zrow[:, :].unsqueeze(1), [P, NTILE, D])).then_inc(s_lw, 16)
                b = n - 2
                if 0 <= b < NB and s == 9:
                    sp.wait_ge(S["tab_rdy"], b + 1)
                    sp.dma_start(d_tab[T * b:T * b + T, :].rearrange("(i p) f -> p i f", p=P),
                                 tab[:, :, :]).then_inc(DS["tab_st"], 16)
        sp.wait_ge(DS["tab_st"], 16 * NB)
        sp.wait_ge(s_lw, 16 * (len(late_weights) + 1))
        barrier(sp, 2)

    a0.close()
    g = Shared()
    g.X = X
    g.ident = ident
    g.identb = identb
    g.neghalf = neghalf
    g.onehot = onehot
    g.modT = modT
    g.modR = modR
    g.SC = SC
    g.w1 = w1
    g.w2 = w2
    g.b1T = b1T
    g.w_qkv = w_qkv
    g.w_proj = w_proj
    g.b_proj = b_proj
    g.w_cm = w_cm
    g.mu = mu
    g.gamma = gamma
    g.beta = beta
    g.s_phase = s_phase
    g.d_tab = d_tab
    g.d_acc = d_acc
    g.chains = chains
    g.ins = ins
    g.zrow, g.biti, g.bitf = zrow, biti, bitf
    g.WT, g.GG, g.WPG, g.WVG, g.BPG, g.m1, g.gmean = WT, GG, WPG, WVG, BPG, m1, gmean
    moe(nc, ctx, g)
    mid.close()
    block1(nc, ctx, g, out)



def moe(nc, ctx, g):
    ph = ExitStack()

    def sb(name, shape, dt=F32):
        return ph.enter_context(nc.sbuf_tensor(name, shape, dt))

    def sem(name):
        return ctx.enter_context(nc.semaphore(name))

    def bc(ap, shape):
        return ap.to_broadcast(shape)

    NG = P // NE
    ST = sb("ST", [P, 2 * P])
    SCh = sb("SCh", [P, 2, NE, NG])
    upper = sb("upper", [P, P])
    group = sb("group", [P, P])
    ones = sb("ones", [P, P])
    iota = sb("iota", [P, P])
    iota_p = sb("iota_p", [P, 1])
    biti, bitf = g.biti, g.bitf
    thr = sb("thr", [P, 1], I32)
    cand = sb("cand", [P, 3], I32)
    nxt = sb("nxt", [P, 3], I32)
    took = sb("took", [P, 3])
    takef = sb("takef", [P, 1])
    take = sb("take", [P, 1], I32)
    hit = [sb(f"hit{i}", [P, 2 * P]) for i in range(3)]
    cnt = sb("cnt", [P, 3])
    thb = sb("thb", [P, P])
    TH = sb("TH", [P, NE])
    gt = sb("gt", [P, NE, NTILE])
    eq = sb("eq", [P, NE, NTILE])
    sel = sb("sel", [P, NE, NTILE])
    tot = sb("tot", [P, NE, NTILE])
    run = sb("run", [P, NE, NTILE])
    pos = sb("pos", [P, NE, NTILE])
    onesv = sb("onesv", [P, NE, NTILE])
    need = sb("need", [P, NE])
    posi = sb("posi", [P, NE, NTILE], I32)
    slot = sb("slot", [P, NE, NTILE], I32)
    stile = sb("stile", [P, NE, NTILE], I32)
    kval = sb("kval", [P, NS])
    ohA = sb("ohA", [P, NTILE, NS])
    slotf = sb("slotf", [P, NE, NTILE])
    stilef = sb("stilef", [P, NE, NTILE])
    A = sb("A", [P, NE, NTILE, 2 * NS], BF16)
    R = [sb(f"R{i}", [P, NTILE, P], BF16) for i in range(2)]
    lst = sb("lst", [P, 2 * NS])
    lstf = sb("lstf", [P, NS])
    idx = sb("idx", [P, NE, NS], I32)
    B2 = sb("B2", [P, NE, D])
    XG = [sb(f"XG{i}", [P, NS, ROW]) for i in range(3)]
    XT = [sb(f"XT{i}", [P, CAP]) for i in range(2)]
    H = [sb(f"H{i}", [P, NC_DI, 512]) for i in range(2)]
    yb = sb("yb", [P, 512])
    Y = [sb(f"Y{i}", [P, NS, D]) for i in range(2)]

    ps_x = [ph.enter_context(nc.psum_tensor(f"ps_x{i}", [P, 512], F32)) for i in range(2)]
    ps_h = [ph.enter_context(nc.psum_tensor(f"ps_h{i}", [P, 512], F32)) for i in range(2)]
    ps_o = [ph.enter_context(nc.psum_tensor(f"ps_o{i}", [P, 512], F32)) for i in range(2)]
    ps_l = ph.enter_context(nc.psum_tensor("ps_l", [P, 512], F32))
    ps_r = ph.enter_context(nc.psum_tensor("ps_r", [P, 512], F32))

    sc_rdy = sem("r_scores_split")
    consts, sT_ps, st_rdy = sem("r_consts"), sem("r_scoresT"), sem("r_scoresT_copied")
    rnd, cnt_rdy, sum_rdy = sem("r_round_chain"), sem("r_counts"), sem("r_sums")
    th_in, th_ps, io_ps, b2_in = sem("r_thr_in"), sem("r_thr_ps"), sem("r_iota_ps"), sem("m_b2_loaded")
    gt_rdy, gt_ps, eq_rdy, eq_ps, sel_rdy, sel_ps = (sem("r_" + n) for n in ("gt", "gt_ps", "eq", "eq_ps", "sel", "sel_ps"))
    R_rdy, l_ps, l_free, idx_rdy = sem("m_onehot"), sem("m_list_ps"), sem("m_list_copied"), sem("m_idx")
    gat = [[sem(f"m_gathered{i}_{h}") for h in range(2)] for i in range(3)]
    scat = sem("m_scattered")
    x_ps, x_cp, h_ps, h_cp, o_ps, o_cp, y_rdy = (sem("m_" + n) for n in
                                                 ("xT_ps", "xT_copied", "h_ps", "gelu", "out_ps", "out_copied", "y"))
    s_dve, s_pool = sem("m_dve_chain"), sem("m_pool_chain")
    wT_ps, wT_cp, gg_ps, gg_cp = sem("p_wT_ps"), sem("p_wT"), sem("p_gates_ps"), sem("p_gates")

    def link(eng, s, ins):
        g.chains[id(s)] = g.chains.get(id(s), 0) + 1
        ins.then_inc(s, 1)
        eng.wait_ge(s, g.chains[id(s)])

    def barrier(eng, k):
        eng.drain().then_inc(g.s_phase, 1)
        eng.wait_ge(g.s_phase, 5 * k)

    block = ph.enter_context(nc.Block())

    @block.gpsimd
    def _(pool):
        def lk(ins):
            link(pool, s_pool, ins)

        lk(nc.gpsimd.memset(upper[:, :], 1.0))
        lk(nc.gpsimd.affine_select(out=upper[:, :], in_=upper[:, :], compare_op=ALU.is_ge, fill=0.0, base=-1,
                                   pattern=[[1, P]], channel_multiplier=-1))
        lk(nc.gpsimd.memset(group[:, :], 1.0))
        gv = group[:, :].rearrange("p (a b) -> p a b", b=NG)
        lk(nc.gpsimd.affine_select(out=gv, in_=gv, compare_op=ALU.is_ge, fill=0.0, base=0,
                                   pattern=[[-NG, NE], [0, NG]], channel_multiplier=1))
        lk(nc.gpsimd.affine_select(out=gv, in_=gv, compare_op=ALU.is_ge, fill=0.0, base=NG - 1,
                                   pattern=[[NG, NE], [0, NG]], channel_multiplier=-1))
        nc.gpsimd.drain().then_inc(consts, 1)

        pool.wait_ge(wT_cp, 1)
        pool.wait_ge(gg_cp, NB)
        full = [P, NB, D]
        nc.gpsimd.tensor_tensor(g.WPG[:, :, :], g.GG[:, :, 1, :], bc(g.w_proj[:, :].unsqueeze(1), full), ALU.mult)
        nc.gpsimd.tensor_tensor(g.BPG[:, :, :], g.GG[:, :, 1, :], bc(g.b_proj[:, :].unsqueeze(1), full), ALU.mult)
        lk(nc.gpsimd.tensor_tensor(g.WVG[:, :, :], g.GG[:, :, 2, :], bc(g.WT[:, 2:3, :], full), ALU.mult))
        nc.gpsimd.tensor_scalar(g.WVG[:, :, :], g.WVG[:, :, :], 0.5, None, ALU.mult)

        def gathers(e):
            pool.wait_ge(idx_rdy, e + 1)
            if e >= 3:
                pool.wait_ge(x_ps, 2 * (e - 2))
                pool.wait_ge(y_rdy, 2 * (e - 2))
            for k in range(NS):
                nc.gpsimd.indirect_dma_start(out=XG[e % 3][:, k, :], out_offset=None, in_=g.d_tab,
                                             in_offset=bass.IndirectOffsetOnAxis(ap=idx[:, e, k:k + 1], axis=0)
                                             ).then_inc(gat[e % 3][k // 4], 16)

        def scatters(e):
            if e >= 1:
                pool.wait_ge(scat, 16 * NS * e)
            for k in range(NS):
                if k % 4 == 0:
                    pool.wait_ge(y_rdy, 2 * e + k // 4 + 1)
                nc.gpsimd.indirect_dma_start(out=g.d_acc, out_offset=bass.IndirectOffsetOnAxis(ap=idx[:, e, k:k + 1], axis=0),
                                             in_=Y[e % 2][:, k, :], in_offset=None,
                                             compute_op=ALU.add).then_inc(scat, 16)

        gathers(0)
        gathers(1)
        for e in range(NE):
            if e + 2 < NE:
                gathers(e + 2)
            scatters(e)
        pool.wait_ge(scat, 16 * NS * NE)
        barrier(pool, 3)

    @block.vector
    def _(dve):
        def lk(ins):
            link(dve, s_dve, ins)

        V = nc.vector
        V.memset(ones[:, :], 1.0)
        V.memset(onesv[:, :, :], 1.0)
        V.memset(thr[:, :], 0)
        lk(V.tensor_copy(cand[:, :], biti[:, 0, :]))
        nc.vector.drain().then_inc(consts, 1)
        dve.wait_ge(consts, 2)
        dve.wait_ge(sT_ps, 1)
        V.tensor_copy(ST[:, :], ps_x[0][:, 0:2 * P]).then_inc(st_rdy, 1)
        dve.wait_ge(io_ps, 1)
        V.tensor_copy(iota[:, :], ps_x[1][:, 0:P])
        lk(V.tensor_copy(iota_p[:, :], ps_x[1][:, P:P + 1]))
        lk(V.tensor_scalar(kval[:, :], iota[:, 0:NS], float(P), None, ALU.mult))
        dve.wait_ge(st_rdy, 1)
        with dve.Fori(0, DIGITS // UNROLL) as q:
            for x in range(UNROLL):
                r = UNROLL * q + x
                for k in range(3):
                    last = V.tensor_scalar(hit[k][:, :], ST[:, :], cand[:, k:k + 1].bitcast(F32), None, ALU.is_ge,
                                           ALU.add, accum_out=cnt[:, k:k + 1])
                last.then_inc(cnt_rdy, 1)
                V.tensor_tensor(nxt[:, :], bc(thr[:, 0:1], [P, 3]),
                                biti[:, bass.ds(r + 1, 1), :].rearrange("p o k -> p (o k)"), ALU.bitwise_or)
                dve.wait_ge(sum_rdy, r + 1)
                V.tensor_scalar(took[:, :], ps_r[:, 0:3], float(CAP), None, ALU.is_ge, ALU.add,
                                accum_out=takef[:, 0:1]).then_inc(rnd, 1)
                dve.wait_ge(rnd, 3 * r + 1)
                V.tensor_tensor(take[:, :], takef[:, :], bitf[:, bass.ds(r, 1)], ALU.mult).then_inc(rnd, 1)
                dve.wait_ge(rnd, 3 * r + 2)
                V.tensor_tensor(thr[:, :], thr[:, :], take[:, :], ALU.bitwise_or)
                V.tensor_tensor(cand[:, :], nxt[:, :], bc(take[:, 0:1], [P, 3]), ALU.bitwise_or).then_inc(rnd, 1)
                dve.wait_ge(rnd, 3 * r + 3)
        V.tensor_copy(thb[:, :], bc(thr[:, :].bitcast(F32), [P, P])).then_inc(th_in, 1)
        dve.wait_ge(th_ps, 1)
        lk(V.tensor_copy(TH[:, :], ps_r[:, P:2 * P].rearrange("p (e x) -> p e x", x=NG)[:, :, 0]))
        full3 = [P, NE, NTILE]
        V.tensor_tensor(gt[:, :, :], g.SC[:, :, :], bc(TH[:, :].unsqueeze(2), full3), ALU.is_gt).then_inc(gt_rdy, 1)
        V.tensor_tensor(eq[:, :, :], g.SC[:, :, :], bc(TH[:, :].unsqueeze(2), full3), ALU.is_equal).then_inc(eq_rdy, 1)
        dve.wait_ge(gt_ps, 1)
        lk(V.tensor_reduce(need[:, :], ps_r[:, 256:512].rearrange("p (e t) -> p e t", t=NTILE), AX_X, ALU.add))
        lk(V.tensor_scalar(need[:, :], need[:, :], -1.0, float(CAP), ALU.mult, ALU.add))

        def ranks(dst, ps):
            lk(V.tensor_copy(tot[:, :, :], ps[:, 256:512].rearrange("p (e t) -> p e t", t=NTILE)))
            lk(V.tensor_tensor_scan(run[:, :, :].rearrange("p e t -> p (e t)"),
                                    onesv[:, :, :].rearrange("p e t -> p (e t)"),
                                    tot[:, :, :].rearrange("p e t -> p (e t)"), 0.0, ALU.mult, ALU.add))
            lk(V.tensor_tensor(run[:, :, :], run[:, :, :], tot[:, :, :], ALU.subtract))
            lk(V.tensor_tensor(dst[:, :, :], run[:, :, :], ps[:, 0:256].rearrange("p (e t) -> p e t", t=NTILE), ALU.add))

        dve.wait_ge(eq_ps, 1)
        ranks(pos, ps_x[0])
        lk(V.tensor_tensor(pos[:, :, :], pos[:, :, :], bc(run[:, :, 0:1], full3), ALU.subtract))
        lk(V.tensor_tensor(sel[:, :, :], pos[:, :, :], bc(need[:, :].unsqueeze(2), full3), ALU.is_lt))
        lk(V.tensor_tensor(sel[:, :, :], sel[:, :, :], eq[:, :, :], ALU.mult))
        V.tensor_tensor(sel[:, :, :], sel[:, :, :], gt[:, :, :], ALU.add).then_inc(sel_rdy, 1)
        dve.wait_ge(sel_ps, 1)
        ranks(pos, ps_x[1])
        lk(V.tensor_copy(posi[:, :, :], pos[:, :, :]))
        lk(V.tensor_scalar(slot[:, :, :], posi[:, :, :], P - 1, None, ALU.bitwise_and))
        lk(V.tensor_scalar(stile[:, :, :], posi[:, :, :], CAP - P, None, ALU.bitwise_and))
        lk(V.tensor_copy(slotf[:, :, :], slot[:, :, :]))
        lk(V.tensor_scalar_add(slotf[:, :, :], slotf[:, :, :], 1.0))
        lk(V.tensor_tensor(slotf[:, :, :], slotf[:, :, :], sel[:, :, :], ALU.mult))
        lk(V.tensor_scalar_add(slotf[:, :, :], slotf[:, :, :], -1.0))
        lk(V.tensor_copy(stilef[:, :, :], stile[:, :, :]))
        def tile_onehot(e):
            wide = [P, NTILE, NS]
            lk(V.tensor_tensor(ohA[:, :, :], bc(stilef[:, e, :].unsqueeze(2), wide), bc(kval[:, :].unsqueeze(1), wide),
                               ALU.is_equal))
            V.tensor_tensor(A[:, e, :, 0:NS], ohA[:, :, :], bc(iota[:, 0:NTILE].unsqueeze(2), wide), ALU.mult)
            lk(V.tensor_scalar(A[:, e, :, NS:2 * NS], ohA[:, :, :], iota_p[:, 0:1], None, ALU.mult))

        def onehot(e):
            tile_onehot(e)
            if e >= 2:
                dve.wait_ge(l_ps, e - 1)
            V.tensor_tensor(R[e % 2][:, :, :], bc(iota[:, :].unsqueeze(1), [P, NTILE, P]),
                            bc(slotf[:, e, :].unsqueeze(2), [P, NTILE, P]), ALU.is_equal).then_inc(R_rdy, 1)

        def index(e):
            dve.wait_ge(l_ps, e + 1)
            lk(V.tensor_copy(lst[:, :], ps_l[:, 0:2 * NS]))
            nc.vector.scalar_tensor_tensor(lstf[:, :], lst[:, 0:NS], float(P), lst[:, NS:2 * NS], ALU.mult,
                                           ALU.add).then_inc(l_free, 1)
            dve.wait_ge(l_free, e + 1)
            V.tensor_copy(idx[:, e, :], lstf[:, :]).then_inc(idx_rdy, 1)

        onehot(0)
        index(0)
        onehot(1)
        index(1)
        qk4 = g.w_qkv[:, 0:2 * D].rearrange("c (h d) -> c h d", d=DH)
        lk(V.tensor_reduce(g.gmean[:, :], qk4, AX_X, ALU.add))
        V.scalar_tensor_tensor(qk4, bc(g.gmean[:, :].unsqueeze(2), [P, 2 * NH, DH]), -1.0 / DH, qk4, ALU.mult, ALU.add)
        V.tensor_scalar(g.m1[:, :], g.mu[:, :], -1.0, 1.0, ALU.mult, ALU.add)
        dve.wait_ge(b2_in, 16)
        for e in range(NE):
            if e + 2 < NE:
                onehot(e + 2)
                index(e + 2)
            for h in range(2):
                dve.wait_ge(o_ps, 2 * e + h + 1)
                if 2 * e + h >= 1:
                    dve.wait_ge(y_rdy, 2 * e + h)
                V.tensor_tensor(yb[:, :].rearrange("p (k d) -> p k d", d=D),
                                ps_o[h][:, :].rearrange("p (k d) -> p k d", d=D),
                                bc(B2[:, e:e + 1, :], [P, 4, D]), ALU.add).then_inc(o_cp, 1)
                dve.wait_ge(o_cp, 2 * e + h + 1)
                if e >= 2 and h == 0:
                    dve.wait_ge(scat, 16 * NS * (e - 1))
                dve.wait_ge(gat[e % 3][h], 16 * 4 * (e // 3 + 1))
                V.tensor_tensor(Y[e % 2][:, 4 * h:4 * h + 4, :], yb[:, :].rearrange("p (k d) -> p k d", d=D),
                                bc(XG[e % 3][:, 4 * h:4 * h + 4, D + e:D + e + 1], [P, 4, D]),
                                ALU.mult).then_inc(y_rdy, 1)
        barrier(dve, 3)

    @block.tensor
    def _(pe):
        T_ = nc.tensor
        pe.wait_ge(consts, 2)
        pe.wait_ge(sc_rdy, 1)
        for h in range(2):
            last = T_.transpose(ps_x[0][:, P * h:P * h + P], SCh[:, h, :, :].rearrange("p e t -> p (e t)"), g.ident[:, :])
        last.then_inc(sT_ps, 1)
        T_.matmul(ps_x[1][:, 0:P], ones[:, :], upper[:, :], start=True, stop=True)
        T_.matmul(ps_x[1][:, P:P + 1], upper[:, :], ones[:, 0:1], start=True, stop=True).then_inc(io_ps, 1)
        for k in range(3):
            last = T_.transpose(ps_l[:, P * k:P * k + P], g.w_cm[:, k, :], g.ident[:, :])
        last.then_inc(wT_ps, 1)
        for b in range(NB):
            if b >= 2:
                pe.wait_ge(gg_cp, b - 1)
            for k, (l, c) in enumerate(((0, 5), (1, 2), (1, 5))):
                last = T_.matmul(ps_o[b % 2][:, D * k:D * k + D], g.onehot[:, b, :], g.modR[:, l, D * c:D * c + D],
                                 start=True, stop=True)
            last.then_inc(gg_ps, 1)
        with pe.Fori(0, DIGITS // UNROLL) as q:
            for x in range(UNROLL):
                pe.wait_ge(cnt_rdy, UNROLL * q + x + 1)
                T_.matmul(ps_r[:, 0:3], group[:, :], cnt[:, :], start=True, stop=True).then_inc(sum_rdy, 1)
        pe.wait_ge(th_in, 1)
        T_.transpose(ps_r[:, P:2 * P], thb[:, :], g.ident[:, :]).then_inc(th_ps, 1)
        flat = lambda t: t[:, :, :].rearrange("p e t -> p (e t)")
        pe.wait_ge(gt_rdy, 1)
        T_.matmul(ps_r[:, 256:512], ones[:, :], flat(gt), start=True, stop=True).then_inc(gt_ps, 1)
        for rdy, x, ps, done in ((eq_rdy, eq, ps_x[0], eq_ps), (sel_rdy, sel, ps_x[1], sel_ps)):
            pe.wait_ge(rdy, 1)
            T_.matmul(ps[:, 0:256], upper[:, :], flat(x), start=True, stop=True)
            T_.matmul(ps[:, 256:512], ones[:, :], flat(x), start=True, stop=True).then_inc(done, 1)

        def lists(e):
            pe.wait_ge(R_rdy, e + 1)
            if e == 0:
                pe.wait_ge(wT_cp, 1)
            if e >= 1:
                pe.wait_ge(l_free, e)
            for t in range(NTILE):
                last = T_.matmul(ps_l[:, 0:2 * NS], R[e % 2][:, t, :], A[:, e, t, :], start=(t == 0), stop=(t == NTILE - 1))
            last.then_inc(l_ps, 1)

        def rows_T(e):
            for h in range(2):
                pe.wait_ge(gat[e % 3][h], 16 * 4 * (e // 3 + 1))
                if e >= 1:
                    pe.wait_ge(x_cp, 2 * e - 1 + h)
                for k in range(4):
                    last = T_.transpose(ps_x[h][:, P * k:P * k + P], XG[e % 3][:, 4 * h + k, 0:D], g.ident[:, :])
                last.then_inc(x_ps, 1)

        def first(e):
            for h in range(2):
                pe.wait_ge(x_cp, 2 * e + h + 1)
                for c in range(NC_DI):
                    u = NC_DI * (2 * e + h) + c
                    if u >= 2:
                        pe.wait_ge(h_cp, u - 1)
                    T_.matmul(ps_h[u % 2][:, :], g.w1[:, e, P * c:P * c + P], XT[e % 2][:, 512 * h:512 * h + 512],
                              start=True, stop=True).then_inc(h_ps, 1)

        def second(e):
            for h in range(2):
                pe.wait_ge(h_cp, NC_DI * (2 * e + h + 1))
                if e >= 1:
                    pe.wait_ge(o_cp, 2 * e - 1 + h)
                else:
                    pe.wait_ge(gg_cp, NB)
                for k in range(4):
                    for c in range(NC_DI):
                        last = T_.matmul(ps_o[h][:, P * k:P * k + P], H[h][:, c, P * k:P * k + P], g.w2[:, e, c, :],
                                         start=(c == 0), stop=(c == NC_DI - 1))
                last.then_inc(o_ps, 1)

        lists(0)
        lists(1)
        rows_T(0)
        for e in range(NE):
            first(e)
            if e + 2 < NE:
                lists(e + 2)
            if e + 1 < NE:
                rows_T(e + 1)
            second(e)
        barrier(pe, 3)

    @block.scalar
    def _(act):
        nc.scalar.activation(SCh[:, 0, :, :], g.SC[:, :, 0:NG], ACT.Copy)
        nc.scalar.activation(SCh[:, 1, :, :], g.SC[:, :, NG:2 * NG], ACT.Copy).then_inc(sc_rdy, 1)
        act.wait_ge(wT_ps, 1)
        nc.scalar.activation(g.WT[:, :, :], ps_l[:, 0:3 * D].rearrange("p (k d) -> p k d", d=D), ACT.Copy).then_inc(wT_cp, 1)
        for b in range(NB):
            act.wait_ge(gg_ps, b + 1)
            nc.scalar.activation(g.GG[:, b, :, :], ps_o[b % 2][:, 0:3 * D].rearrange("p (k d) -> p k d", d=D),
                                 ACT.Copy).then_inc(gg_cp, 1)
        for e in range(NE):
            for h in range(2):
                act.wait_ge(x_ps, 2 * e + h + 1)
                if e >= 2 and h == 0:
                    act.wait_ge(h_ps, 2 * NC_DI * (e - 1))
                nc.scalar.activation(XT[e % 2][:, 512 * h:512 * h + 512], ps_x[h][:, :], ACT.Copy).then_inc(x_cp, 1)
            for h in range(2):
                if e >= 1:
                    act.wait_ge(o_ps, 2 * e - 1 + h)
                for c in range(NC_DI):
                    u = NC_DI * (2 * e + h) + c
                    act.wait_ge(h_ps, u + 1)
                    nc.scalar.activation(H[h][:, c, :], ps_h[u % 2][:, :], ACT.Gelu,
                                         bias=g.b1T[:, e, c:c + 1]).then_inc(h_cp, 1)
        barrier(act, 3)

    @block.sync
    def _(sp):
        sp.dma_start(B2[:, :, :].rearrange("p e d -> p (e d)"), bass.AP(g.ins["L0_ffn_b2"].tensor, 0, [[0, P], [1, NE * D]])
                     ).then_inc(b2_in, 16)
        barrier(sp, 3)

    ph.close()


MISC1 = {0: [("qk0", 2)], 1: [("qk1", 2), ("ck", -2)], 2: [("kT", 1), ("qk2", 2)], 3: [("qT", 1), ("yT", -1)],
         4: [("pj", -1), ("qk3", 2)], 5: [("cr", -2)], 6: [("hT", 3), ("kv", -2)], 7: [("gT", -1)]}
LEAD1, TAIL1 = 3, 3
NU = 2 * NT
HU = NH // 2
DV = DH + 1
EARLY = 1
RSQRT_MAGIC = float(0x5F3759DF)


def block1(nc, ctx, g, out):
    ph = ExitStack()

    def sb(name, shape, dt=F32):
        return ph.enter_context(nc.sbuf_tensor(name, shape, dt))

    def sem(name):
        return ctx.enter_context(nc.semaphore(name))

    def bc(ap, shape):
        return ap.to_broadcast(shape)

    X, modT, ident = g.X, g.modT, g.ident
    wqk = g.w_qkv[:, 0:2 * D]
    GG, WPG, WVG, BPG, WT, m1 = g.GG, g.WPG, g.WVG, g.BPG, g.WT, g.m1
    KB = [sb(f"KB{i}", [P, NH, T]) for i in range(2)]
    QT = [sb(f"QT{i}", [P, T]) for i in range(2)]
    KT = sb("KT", [P, T])
    VF = [sb(f"VF{i}", [P, NT * HU * 2 * 2 * DV + 32]) for i in range(3)]
    VB = [v[:, 0:NT * HU * 2 * 2 * DV].rearrange("p (i a w x) -> p i a w x", i=NT, a=HU, w=2) for v in VF]
    yrow = [sb(f"yrow{i}", [P, 2 * P]) for i in range(2)]
    AC = sb("AC", [P, NT, D])
    stat = sb("bstat", [P, NT, 6])
    mv = sb("bmv", [P, NT, 2])
    ve = sb("bve", [P, NT])
    rs = sb("brs", [P, NT])
    xn = sb("bxn", [P, NT, D])
    hT = sb("bhT", [P, T])
    sq = [sb(f"sq{i}", [P, 2 * D]) for i in range(2)]
    QK = [sb(f"QK{i}", [P, NT, 2 * D]) for i in range(2)]
    var = sb("var", [P, NT, 2 * NH])
    nwt = sb("nwt", [P, NT, 2 * NH])
    half = sb("half", [P, NT, 2 * NH], I32)
    rq = sb("rq", [P, NT, 2 * NH])
    QKN = sb("QKN", [P, NT, 2 * D])
    mxs = [sb(f"mxs{i}", [P, HU]) for i in range(2)]
    SU = [sb(f"SU{i}", [P, 512]) for i in range(2)]
    PB = [sb(f"PB{i}", [P, 512]) for i in range(2)]
    PT = [sb(f"PT{i}", [P, 512]) for i in range(2)]
    rcp = sb("rcp", [P, 2, NH])
    YN = sb("YN", [P, NT, D])
    yT = sb("yT", [P, T])
    stat2 = sb("bstat2", [P, NT, 6])
    mv2 = sb("bmv2", [P, NT, 2])
    ve2 = sb("bve2", [P, NT])
    rs2 = sb("brs2", [P, NT])
    xn2 = sb("bxn2", [P, NT, D])
    GT = sb("GT", [P, T + 1])
    t1 = sb("t1", [P, 2, T])
    xm = sb("xm", [P, 2, T])
    KA = sb("KA", [P, T])
    KA2 = sb("KA2", [P, T])
    RT = sb("RT", [P, T])
    OU = sb("OU", [P, NT, D])

    ps = [ph.enter_context(nc.psum_tensor(f"b1ps{i}", [P, 512], F32)) for i in range(8)]
    ps_s, ps_t, ps_v, ps_n, ps_m = ps[0:2], ps[2], ps[3], ps[4], ps[5:8]

    names = ["yrow", "n_ps", "kz", "vz", "s_ps", "max", "sub", "exp", "t_ps", "pt", "v_ps", "yn",
             "accg", "xadd", "mv", "rs", "xn", "qk_cp", "sq", "var", "rq0", "rq", "qkn", "bp",
             "mv2", "rs2", "xn2", "t1", "xm", "ka2", "xo", "misc_free0", "misc_free1", "misc_free2",
             "misc_full0", "misc_full1", "misc_full2"]
    S = {n: sem("b1_" + n) for n in names}
    k_in = [sem(f"b1_keys_in{i}") for i in range(2)]
    acc_in, o_st = sem("b1_acc_in"), sem("b1_out_stored")
    s_dve, s_pool = sem("b1_dve_chain"), sem("b1_pool_chain")
    order = [(kind, n + o) for n in range(-LEAD1, NB + TAIL1) for u in range(NU)
             for kind, o in MISC1.get(u, []) if 0 <= n + o < NB]
    M = Misc(order, 3)

    def link(eng, s, ins):
        g.chains[id(s)] = g.chains.get(id(s), 0) + 1
        ins.then_inc(s, 1)
        eng.wait_ge(s, g.chains[id(s)])

    def barrier(eng, k):
        eng.drain().then_inc(g.s_phase, 1)
        eng.wait_ge(g.s_phase, 5 * k)

    def m_of(u):
        return ps_m[M.bank(u)]

    def full(eng, u):
        eng.wait_ge(S[f"misc_full{M.bank(u)}"], M.full(u))

    def free(u):
        return S[f"misc_free{M.bank(u)}"]

    def evacuated(eng, u):
        eng.wait_ge(free(u), M.full(u))

    def newton(eng, lk):
        v_, y_, w_ = var[:, :, :], rq[:, :, :], nwt[:, :, :]
        for step in range(3):
            lk(eng.tensor_tensor(w_, v_, y_, ALU.mult))
            lk(eng.tensor_tensor(w_, w_, y_, ALU.mult))
            lk(eng.tensor_scalar(w_, w_, -0.5, 1.5, ALU.mult, ALU.add))
            last = eng.tensor_tensor(y_, y_, w_, ALU.mult)
            if step < 2:
                lk(last)
        last.then_inc(S["rq"], 1)

    block = ph.enter_context(nc.Block())

    @block.tensor
    def _(pe):
        T_ = nc.tensor

        def misc(kind, b):
            u = (kind, b)
            m = m_of(u)
            if M.full(u) >= 2:
                pe.wait_ge(free(u), M.full(u) - 1)
            if kind == "hT":
                pe.wait_ge(S["xn"], b + 1)
                for i in range(NT):
                    last = T_.transpose(m[:, P * i:P * i + P], xn[:, i, :], ident[:, :])
            elif kind[:2] == "qk":
                i = int(kind[2])
                evacuated(pe, ("hT", b))
                T_.matmul(m[:, 0:2 * D], hT[:, P * i:P * i + P], wqk, start=True, stop=True)
                for w in range(2):
                    for h2 in range(2):
                        last = T_.matmul(m[64 * h2:64 * h2 + 64, 2 * D + 64 * w:2 * D + 64 * w + 64],
                                         hT[:, P * i + 64 * w:P * i + 64 * w + 64],
                                         g.w_qkv[:, 2 * D:3 * D].rearrange("c (a b d) -> c b a d", b=2, d=DH)[:, h2],
                                         start=True, stop=True, tile_position=(0, 64 * h2), skip_group_check=True)
            elif kind == "kT" or kind == "qT":
                pe.wait_ge(S["qkn"], b + 1)
                o = D if kind == "kT" else 0
                for i in range(NT):
                    last = T_.transpose(m[:, P * i:P * i + P], QKN[:, i, o:o + D], ident[:, :])
            elif kind == "yT":
                pe.wait_ge(S["yn"], NT * (b + 1))
                for i in range(NT):
                    last = T_.transpose(m[:, P * i:P * i + P], YN[:, i, :], ident[:, :])
            elif kind == "pj":
                evacuated(pe, ("yT", b))
                for i in range(NT):
                    last = T_.matmul(m[:, P * i:P * i + P], yT[:, P * i:P * i + P], WPG[:, b, :], start=True, stop=True)
            elif kind == "gT":
                pe.wait_ge(S["xn2"], b + 1)
                for i in range(NT):
                    last = T_.transpose(m[:, P * i:P * i + P], xn2[:, i, :], ident[:, :])
            elif kind == "ck":
                pe.wait_ge(S["xm"], b + 1)
                last = T_.matmul(m[:, :], WT[:, 1, :], xm[:, 1, :], start=True, stop=True)
            elif kind == "cr":
                for i in range(NT):
                    last = T_.matmul(m[:, P * i:P * i + P], xm[:, 0, P * i:P * i + P], WT[:, 0, :], start=True, stop=True)
            elif kind == "kv":
                pe.wait_ge(S["ka2"], b + 1)
                for i in range(NT):
                    last = T_.matmul(m[:, P * i:P * i + P], KA2[:, P * i:P * i + P], WVG[:, b, :], start=True, stop=True)
            last.then_inc(S[f"misc_full{M.bank(u)}"], 1)

        def scores(U):
            b, u = divmod(U, NU)
            i, hh = divmod(u, 2)
            if u == 0:
                evacuated(pe, ("qT", b))
                pe.wait_ge(k_in[b % 2], 16 * NH * (b // 2 + 1))
            if U >= 2:
                pe.wait_ge(S["sub"], U - 1)
            for j in range(4):
                o = P * i + 64 * (j // 2)
                last = T_.matmul(ps_s[U % 2][32 * j:32 * j + 32, :], QT[b % 2][:, P * i + 32 * j:P * i + 32 * j + 32],
                                 KB[b % 2][:, HU * hh:HU * hh + HU, o:o + 64], start=True, stop=True,
                                 tile_position=(0, 32 * j))
            last.then_inc(S["s_ps"], 1)

        def transposes(U):
            pe.wait_ge(S["exp"], U + 1)
            if U >= 1:
                pe.wait_ge(S["pt"], U)
            for k in range(HU // 2):
                last = T_.transpose(ps_t[:, P * k:P * k + P], PB[U % 2][:, P * k:P * k + P], ident[:, :])
            last.then_inc(S["t_ps"], 1)

        def values(U):
            b, u = divmod(U, NU)
            i, hh = divmod(u, 2)
            tile = U // 2
            pe.wait_ge(S["pt"], U + 1)
            if hh == 0 and tile >= 1:
                pe.wait_ge(S["yrow"], tile)
            for w in range(2):
                for k in range(HU // 2):
                    c = ((i * HU + k + HU // 2 * hh) * 2 + w) * 2 * DV
                    last = T_.matmul(ps_v[32 * k:32 * k + 32, P * hh + 64 * w:P * hh + 64 * w + 64], VF[b % 3][:, c:c + 32],
                                     PT[U % 2][:, P * k + 64 * w:P * k + 64 * w + 64], start=True, stop=True,
                                     tile_position=(0, 32 * k), skip_group_check=True)
            last.then_inc(S["v_ps"], 1)

        def rows_T(tile):
            pe.wait_ge(S["yrow"], tile + 1)
            if tile >= 1:
                pe.wait_ge(S["yn"], tile)
            for hh in range(2):
                last = T_.transpose(ps_n[:, P * hh:P * hh + P], yrow[tile % 2][:, P * hh:P * hh + P], ident[:, :])
            last.then_inc(S["n_ps"], 1)

        for n in range(-LEAD1, NB + TAIL1):
            for u in range(NU):
                U = NU * n + u
                if 0 <= U < NU * NB:
                    scores(U)
                if 0 <= U - 1 < NU * NB:
                    transposes(U - 1)
                for kind, o in MISC1.get(u, []):
                    if (kind, n + o) in M:
                        misc(kind, n + o)
                if 0 <= U - 2 < NU * NB and U % 2 == 1:
                    rows_T((U - 2) // 2)
                if 0 <= U - 1 < NU * NB:
                    values(U - 1)

    @block.scalar
    def _(act):
        A_ = nc.scalar
        for k in KB:
            A_.activation(k[:, :, :].rearrange("p h (a d) -> p (h a) d", d=D), bc(g.zrow[:, :].unsqueeze(1), [P, NH * T // D, D]),
                          ACT.Copy).then_inc(S["kz"], 1)

        def misc(kind, b):
            u = (kind, b)
            m = m_of(u)
            if kind == "hT":
                full(act, u)
                A_.activation(hT[:, :], m[:, :], ACT.Identity, bias=modT[:, 1, 0, b:b + 1],
                              scale=modT[:, 1, 1, b:b + 1]).then_inc(free(u), 1)
            elif kind[:2] == "qk":
                i = int(kind[2])
                t = NT * b + i
                full(act, u)
                if t >= 2:
                    act.wait_ge(S["var"], t - 1)
                A_.activation(sq[t % 2][:, :], m[:, 0:2 * D], ACT.Square).then_inc(S["sq"], 1)
                if i == 0 and b >= 2:
                    act.wait_ge(S["qkn"], b - 1)
                A_.activation(QK[b % 2][:, i, :], m[:, 0:2 * D], ACT.Copy).then_inc(S["qk_cp"], 1)
                if b >= 3:
                    act.wait_ge(S["v_ps"], NU * (b - 3) + 2 * i + 2)
                if b < 3 and i == 0:
                    act.wait_ge(S["vz"], b + 1)
                mv4 = m[:, 2 * D:3 * D].rearrange("p (w a d) -> p a w d", w=2, d=DH)
                A_.activation(VB[b % 3][0:64, i, :, :, 0:DH], mv4[0:64], ACT.Copy)
                A_.activation(VB[b % 3][64:P, i, :, :, DV:DV + DH], mv4[64:P], ACT.Copy).then_inc(free(u), 1)
            elif kind == "kT":
                full(act, u)
                if b >= 1:
                    act.wait_ge(k_in[(b - 1) % 2], 16 * NH * ((b - 1) // 2 + 1))
                A_.activation(KT[:, :], m[:, :], ACT.Identity, bias=g.beta[:, 0:1], scale=g.gamma[:, 0:1]
                              ).then_inc(free(u), 1)
            elif kind == "qT":
                full(act, u)
                if b >= 2:
                    act.wait_ge(S["s_ps"], NU * (b - 1))
                A_.activation(QT[b % 2][:, :], m[:, :], ACT.Identity, bias=g.beta[:, 0:1], scale=g.gamma[:, 0:1]
                              ).then_inc(free(u), 1)
            elif kind == "yT":
                full(act, u)
                A_.activation(yT[:, :], m[:, :], ACT.Copy).then_inc(free(u), 1)
            elif kind == "gT":
                full(act, u)
                if b >= 1:
                    act.wait_ge(S["xm"], b)
                A_.activation(GT[:, 1:T + 1], m[:, :], ACT.Identity, bias=modT[:, 1, 3, b:b + 1],
                              scale=modT[:, 1, 4, b:b + 1]).then_inc(free(u), 1)
                evacuated(act, u)
                A_.activation(t1[:, 0, :], GT[:, 1:T + 1], ACT.Copy, scale=g.mu[:, 0:1])
                A_.activation(t1[:, 1, :], GT[:, 1:T + 1], ACT.Copy, scale=g.mu[:, 1:2]).then_inc(S["t1"], 1)
            elif kind == "ck":
                full(act, u)
                if b >= 1:
                    act.wait_ge(S["ka2"], b)
                A_.activation(KA[:, :], m[:, :], ACT.Relu).then_inc(free(u), 1)
            elif kind == "cr":
                full(act, u)
                if b >= 1:
                    evacuated(act, ("kv", b - 1))
                A_.activation(RT[:, :], m[:, :], ACT.Tanh, scale=0.5).then_inc(free(u), 1)

        for n in range(-LEAD1, NB + TAIL1):
            for u in range(NU):
                U = NU * n + u
                if 0 <= U - 2 < NU * NB and U % 2 == 1:
                    tile = (U - 2) // 2
                    act.wait_ge(S["v_ps"], U - 1)
                    if tile >= 2:
                        act.wait_ge(S["n_ps"], tile - 1)
                    A_.activation(yrow[tile % 2][:, :], ps_v[:, 0:2 * P], ACT.Copy).then_inc(S["yrow"], 1)
                if 0 <= U - 1 < NU * NB:
                    act.wait_ge(S["t_ps"], U)
                    if U - 1 >= 2:
                        act.wait_ge(S["v_ps"], U - 2)
                    A_.activation(PT[(U - 1) % 2][:, :], ps_t[:, :], ACT.Copy).then_inc(S["pt"], 1)
                if 0 <= U < NU * NB:
                    act.wait_ge(S["sub"], U + 1)
                    if U >= 2:
                        act.wait_ge(S["t_ps"], U - 1)
                    A_.activation(PB[U % 2][:, :], SU[U % 2][:, :], ACT.Exp).then_inc(S["exp"], 1)
                for kind, o in MISC1.get(u, []):
                    if (kind, n + o) in M:
                        misc(kind, n + o)

    @block.vector
    def _(dve):
        V = nc.vector

        def lk(ins):
            link(dve, s_dve, ins)

        for f, v in zip(VF, VB):
            lk(V.memset(f[:, :], 0.0))
            V.memset(v[0:64, :, :, :, DH:DV], 1.0)
            V.memset(v[64:P, :, :, :, DV + DH:2 * DV], 1.0).then_inc(S["vz"], 1)
        V.memset(GT[:, 0:1], 0.0)

        def norm_stats(src, st, m_, rdy):
            for i in range(NT):
                last = V.bn_stats(st[:, i, :], src[:, i, :])
            lk(last)
            for i in range(NT):
                last = V.bn_aggr(m_[:, i, :], st[:, i, :])
            last.then_inc(rdy, 1)

        def misc(kind, b):
            u = (kind, b)
            m = m_of(u)
            if kind[:2] == "qk":
                i = int(kind[2])
                t = NT * b + i
                dve.wait_ge(S["sq"], t + 1)
                if i == 0 and b >= 1:
                    dve.wait_ge(S["rq"], b)
                V.tensor_reduce(var[:, i, :], sq[t % 2][:, :].rearrange("p (h d) -> p h d", d=DH), AX_X,
                                ALU.add).then_inc(S["var"], 1)
            elif kind == "pj":
                full(dve, u)
                dve.wait_ge(S["bp"], b + 1)
                Xb = X[:, NT * b:NT * b + NT, :]
                V.tensor_tensor(Xb, Xb, m[:, :].rearrange("p (i d) -> p i d", i=NT), ALU.add).then_inc(free(u), 1)
                evacuated(dve, u)
                norm_stats(Xb, stat2, mv2, S["mv2"])
            elif kind == "kv":
                full(dve, u)
                evacuated(dve, ("cr", b))
                if b >= 1:
                    dve.wait_ge(S["xo"], b)
                V.scalar_tensor_tensor(OU[:, :, :].rearrange("p i d -> p (i d)"), RT[:, :], 1.0, m[:, :], ALU.add,
                                       ALU.mult).then_inc(free(u), 1)

        for n in range(-LEAD1, NB + TAIL1):
            for u in range(NU):
                U = NU * n + u
                b = n + 1
                if 0 <= b < NB and u == 1:
                    dve.wait_ge(S["rq"], b + 1)
                    dve.wait_ge(S["qk_cp"], NT * (b + 1))
                    if b >= 1:
                        full(dve, ("kT", b - 1))
                        full(dve, ("qT", b - 1))
                    V.tensor_tensor(QKN[:, :, :].rearrange("p i (h d) -> p (i h) d", d=DH),
                                    QK[b % 2][:, :, :].rearrange("p i (h d) -> p (i h) d", d=DH),
                                    bc(rq[:, :, :].rearrange("p i h -> p (i h)").unsqueeze(2),
                                       [P, NT * 2 * NH, DH]), ALU.mult).then_inc(S["qkn"], 1)
                if 0 <= U < NU * NB:
                    dve.wait_ge(S["s_ps"], U + 1)
                    s3 = ps_s[U % 2][:, :].rearrange("p (h s) -> p h s", h=HU)
                    V.tensor_reduce(mxs[U % 2][:, :], s3, AX_X, ALU.max).then_inc(S["max"], 1)
                    dve.wait_ge(S["max"], U + 1)
                    if U >= 2:
                        dve.wait_ge(S["exp"], U - 1)
                    V.tensor_tensor(SU[U % 2][:, :].rearrange("p (h s) -> p h s", h=HU), s3,
                                    bc(mxs[U % 2][:, :].unsqueeze(2), [P, HU, 512 // HU]),
                                    ALU.subtract).then_inc(S["sub"], 1)
                for kind, o in MISC1.get(u, []):
                    if (kind, n + o) in M and kind[:2] != "qk":
                        misc(kind, n + o)
                for kind, o in MISC1.get(u - 1, []):
                    if (kind, n + o) in M and kind[:2] == "qk":
                        misc(kind, n + o)
                W = U - 2
                if 0 <= W < NU * NB and W % 2 == 1:
                    tile = W // 2
                    i = tile % NT
                    dve.wait_ge(S["n_ps"], tile + 1)
                    v4 = ps_n[:, 0:2 * P].rearrange("p (a c) -> p a c", c=32)[:, :, 0:2 * DV].rearrange(
                        "p a (b x) -> p a b x", x=DV)
                    lk(V.reciprocal(rcp[:, tile % 2, :].rearrange("p (a b) -> p a b", b=2), v4[:, :, :, DH]))
                    if i == 0 and tile >= NT:
                        full(dve, ("yT", tile // NT - 1))
                    last = V.tensor_tensor(YN[:, i, :].rearrange("p (a b d) -> p a b d", b=2, d=DH), v4[:, :, :, 0:DH],
                                           bc(rcp[:, tile % 2, :].rearrange("p (a b) -> p a b", b=2).unsqueeze(3),
                                              [P, HU, 2, DH]), ALU.mult)
                    last.then_inc(S["yn"], 1)
                b = n + 2
                if 0 <= b < NB and u == 5:
                    dve.wait_ge(S["var"], NT * (b + 1))
                    lk(V.tensor_scalar(var[:, :, :], var[:, :, :], 1.0 / DH, EPS, ALU.mult, ALU.add))
                    lk(V.tensor_scalar(half[:, :, :], var[:, :, :].bitcast(I32), 1, None, ALU.logical_shift_right))
                    if b >= 1:
                        dve.wait_ge(S["qkn"], b)
                    V.tensor_scalar(rq[:, :, :].bitcast(I32), half[:, :, :], -1.0, RSQRT_MAGIC, ALU.mult,
                                    ALU.add).then_inc(S["rq0"], 1)
                    if b < EARLY:
                        dve.wait_ge(S["rq0"], b + 1)
                        newton(V, lk)
                b = n - 2
                if 0 <= b < NB and u == 0:
                    dve.wait_ge(S["t1"], b + 1)
                    if b >= 1:
                        full(dve, ("ck", b - 1))
                        full(dve, ("cr", b - 1))
                    V.scalar_tensor_tensor(xm[:, 0, :], GT[:, 0:T], m1[:, 0:1], t1[:, 0, :], ALU.mult, ALU.add)
                    V.scalar_tensor_tensor(xm[:, 1, :], GT[:, 0:T], m1[:, 1:2], t1[:, 1, :], ALU.mult,
                                           ALU.add).then_inc(S["xm"], 1)
                b = n + 3
                if 0 <= b < NB and u == 2:
                    Xb = X[:, NT * b:NT * b + NT, :]
                    dve.wait_ge(S["xadd"], b + 1)
                    if b >= 1:
                        dve.wait_ge(S["xn"], b)
                    norm_stats(Xb, stat, mv, S["mv"])

    @block.gpsimd
    def _(pool):
        G = nc.gpsimd

        def lk(ins):
            link(pool, s_pool, ins)


        def norm_apply(dst, src, m_, r_, rdy):
            for i in range(NT):
                last = G.tensor_scalar(dst[:, i, :], src[:, i, :], m_[:, i, 0:1], r_[:, i:i + 1],
                                       ALU.subtract, ALU.mult)
            last.then_inc(rdy, 1)

        def rstd(ve_, m_, dst, rdy):
            lk(G.tensor_scalar(ve_[:, :], m_[:, :, 1], EPS, None, ALU.add))
            G.tensor_tensor(dst[:, :], ve_[:, :], g.neghalf[:, :], ALU.pow).then_inc(rdy, 1)

        for n in range(-LEAD1, NB + TAIL1):
            for u in range(NU):
                b = n + 3
                if 0 <= b < NB and u == 0:
                    pool.wait_ge(acc_in, 16 * (b + 1))
                    G.tensor_tensor(AC[:, :, :], AC[:, :, :], bc(GG[:, b, 0:1, :], [P, NT, D]), ALU.mult
                                    ).then_inc(S["accg"], 1)
                    pool.wait_ge(S["accg"], b + 1)
                    Xb = X[:, NT * b:NT * b + NT, :]
                    G.tensor_tensor(Xb, Xb, AC[:, :, :], ALU.add).then_inc(S["xadd"], 1)
                if 0 <= b < NB and u == 3:
                    pool.wait_ge(S["mv"], b + 1)
                    rstd(ve, mv, rs, S["rs"])
                    pool.wait_ge(S["rs"], b + 1)
                    if b >= 1:
                        full(pool, ("hT", b - 1))
                    norm_apply(xn, X[:, NT * b:NT * b + NT, :], mv, rs, S["xn"])
                if 0 <= b < NB and u == 7:
                    Xb = X[:, NT * b:NT * b + NT, :]
                    pool.wait_ge(S["xn"], b + 1)
                    G.tensor_tensor(Xb, Xb, bc(BPG[:, b:b + 1, :], [P, NT, D]), ALU.add).then_inc(S["bp"], 1)
                b = n + 2
                if EARLY <= b < NB and u == 6:
                    pool.wait_ge(S["rq0"], b + 1)
                    newton(G, lk)
                b = n - 1
                if 0 <= b < NB and u == 5:
                    pool.wait_ge(S["mv2"], b + 1)
                    rstd(ve2, mv2, rs2, S["rs2"])
                    pool.wait_ge(S["rs2"], b + 1)
                    if b >= 1:
                        full(pool, ("gT", b - 1))
                    norm_apply(xn2, X[:, NT * b:NT * b + NT, :], mv2, rs2, S["xn2"])
                b = n - 2
                if 0 <= b < NB and u == 3:
                    uu = ("ck", b)
                    evacuated(pool, uu)
                    if b >= 1:
                        full(pool, ("kv", b - 1))
                    G.tensor_tensor(KA2[:, :], KA[:, :], KA[:, :], ALU.mult).then_inc(S["ka2"], 1)
                if 0 <= b < NB and u == 7:
                    uu = ("kv", b)
                    evacuated(pool, uu)
                    Xb = X[:, NT * b:NT * b + NT, :]
                    G.tensor_tensor(Xb, Xb, OU[:, :, :], ALU.add).then_inc(S["xo"], 1)

    @block.sync
    def _(sp):
        ov = out.rearrange("b (i p) d -> b p i d", p=P)
        for n in range(-LEAD1, NB + TAIL1):
            for u in range(NU):
                b = n + 3
                if 0 <= b < NB and u == 0:
                    if b >= 1:
                        sp.wait_ge(S["xadd"], b)
                    sp.dma_start(AC[:, :, :], g.d_acc[T * b:T * b + T, :].rearrange("(i p) d -> p i d", p=P)
                                 ).then_inc(acc_in, 16)
                b = n + 1
                if 0 <= b < NB and u == 2:
                    uu = ("kT", b)
                    evacuated(sp, uu)
                    if b == 0:
                        sp.wait_ge(S["kz"], 2)
                    if b >= 2:
                        sp.wait_ge(S["s_ps"], NU * (b - 1))
                    for h in range(NH):
                        sp.dma_start(KB[b % 2][DH * h:DH * h + DH, h, :], KT[DH * h:DH * h + DH, :]
                                     ).then_inc(k_in[b % 2], 16)
                b = n - 2
                if 0 <= b < NB and u == 7:
                    sp.wait_ge(S["xo"], b + 1)
                    sp.dma_start(ov[b], X[:, NT * b:NT * b + NT, :]).then_inc(o_st, 16)
        sp.wait_ge(o_st, 16 * NB)

    ph.close()


_INS = ["L0_attn_x", "L0_attn_Wc_down", "L0_attn_Wq_up", "L0_attn_Wkv_up", "L0_attn_Wc_proj", "L0_ffn_Wr", "L0_ffn_W1",
        "L0_ffn_b1", "L0_ffn_W2", "L0_ffn_b2", "L0_c", "L0_wmod", "L1_attn_W_qkv", "L1_attn_ln_gamma",
        "L1_attn_ln_beta", "L1_attn_W_proj", "L1_attn_b_proj", "L1_ffn_W_r", "L1_ffn_W_k", "L1_ffn_W_v",
        "L1_ffn_mu_r", "L1_ffn_mu_k", "L1_c", "L1_wmod"]


def kernel(**inputs):
    import numpy as np
    import concourse.bacc as bacc
    from concourse.bass_utils import run_bass_kernel_spmd

    nc = bacc.Bacc("TRN2", target_bir_lowering=False, num_devices=1)
    arrays, aps = {}, {}
    for name in _INS:
        a = np.ascontiguousarray(inputs[name])
        arrays[name] = a
        aps[name] = nc.dram_tensor(name, a.shape, mybir.dt.from_np(a.dtype), kind="ExternalInput").ap()
    out = nc.dram_tensor("y", (NB, T, D), F32, kind="ExternalOutput").ap()
    build(nc, aps, out)
    r = run_bass_kernel_spmd(nc, [arrays], core_ids=[0])
    return r.results[0]["y"]
```
